# Optimizing a Trainium2 kernel written in Bass

```python
import numpy as np
import jax
import jax.numpy as jnp

def _softmax(x, axis=-1):
    return jax.nn.softmax(x, axis=axis)

def _gelu(x):
    return jax.nn.gelu(x, approximate=True)

def _silu(x):
    return jax.nn.silu(x)

def _sigmoid(x):
    return jax.nn.sigmoid(x)

def _layernorm(x, axis=-1, eps=1e-05):
    m = jnp.mean(x, axis=axis, keepdims=True)
    v = jnp.var(x, axis=axis, keepdims=True)
    return (x - m) / jnp.sqrt(v + eps)

def _scatter_add(tgt, idx, src, axis=0):
    return tgt.at[idx].add(src)

def _segment_sum(src, seg, n):
    return jax.ops.segment_sum(src, seg, n)
kernel_name = 'mk_adaln_d1_jaxref_r8_47ba79'

def setup_inputs(seed: int=0):
    np.random.seed(seed)
    _w = jnp.asarray

    def _L0_attn_setup():
        import jax, jax.numpy as jnp
        import numpy as np
        import math
        B, L, D = (2, 256, 128)
        H, KV, HD = (16, 4, 64)
        GROUPS = H // KV
        ROPE_BASE = 10000.0

        def _alibi_slopes(n_heads):

            def pow2(n):
                start = 2.0 ** (-2.0 ** (-(math.log2(n) - 3)))
                return [start * start ** i for i in range(n)]
            if math.log2(n_heads).is_integer():
                return pow2(n_heads)
            c = 2 ** math.floor(math.log2(n_heads))
            return pow2(c) + _alibi_slopes(2 * c)[0::2][:n_heads - c]

        def _rope_cos_sin(seq_len, dim, dtype):
            inv_freq = 1.0 / ROPE_BASE ** (jnp.arange(0, dim, 2, dtype=jnp.float32) / dim)
            t = jnp.arange(seq_len, dtype=jnp.float32)
            freqs = t[:, None] * inv_freq[None, :]
            emb = jnp.concatenate([freqs, freqs], axis=-1)
            return (jnp.cos(emb).astype(dtype), jnp.sin(emb).astype(dtype))

        def _rotate_half(x):
            x1, x2 = (x[..., :x.shape[-1] // 2], x[..., x.shape[-1] // 2:])
            return jnp.concatenate([-x2, x1], axis=-1)
        key = jax.random.key(seed)
        ks = jax.random.split(key, 5)
        s = 0.02
        return {'x': jax.random.normal(ks[0], (B, L, D), jnp.float32), 'Wq': jax.random.normal(ks[1], (D, H * HD), jnp.float32) * s, 'Wk': jax.random.normal(ks[2], (D, KV * HD), jnp.float32) * s, 'Wv': jax.random.normal(ks[3], (D, KV * HD), jnp.float32) * s, 'Wo': jax.random.normal(ks[4], (H * HD, D), jnp.float32) * s}
    _L0_attn_in = _L0_attn_setup()

    def _L0_ffn_setup():
        import jax, jax.numpy as jnp
        import numpy as np
        DIM = 128
        DEPTH = 2
        HEADS = 8
        DIM_HEAD = 64
        WINDOW = 64
        INNER = HEADS * DIM_HEAD
        HID = int(DIM * 4 * 2 / 3)
        B, N = (2, 1024)
        QK_SCALE = 8.0

        def shift_token(t):
            t1, t2 = jnp.split(t, 2, axis=-1)
            t2 = jnp.pad(t2, ((0, 0), (1, 0), (0, 0)))[:, :-1]
            return jnp.concatenate([t1, t2], axis=-1)

        def l2norm(t):
            return t / jnp.clip(jnp.linalg.norm(t, axis=-1, keepdims=True), 1e-12)

        def rotate_half(x):
            x1, x2 = jnp.split(x, 2, axis=-1)
            return jnp.concatenate([-x2, x1], axis=-1)

        def rotary_xpos(q, k):
            n = q.shape[-2]
            half_idx = jnp.arange(0, DIM_HEAD, 2, dtype=jnp.float32)
            inv_freq = 1.0 / 10000.0 ** (half_idx / DIM_HEAD)
            t = jnp.arange(n, dtype=jnp.float32)
            freqs = t[:, None] * inv_freq[None, :]
            freqs = jnp.concatenate([freqs, freqs], axis=-1)
            base = (half_idx + 0.4 * DIM_HEAD) / (1.4 * DIM_HEAD)
            power = (t - n // 2) / float(WINDOW // 2)
            scale = base[None, :] ** power[:, None]
            scale = jnp.concatenate([scale, scale], axis=-1)
            cos, sin = (jnp.cos(freqs), jnp.sin(freqs))
            q = q * cos * scale + rotate_half(q) * sin * scale
            k = k * cos / scale + rotate_half(k) * sin / scale
            return (q, k)

        def local_attention(q, k, v):
            b, h, n, d = q.shape
            w = n // WINDOW
            bq = q.reshape(b, h, w, WINDOW, d) * QK_SCALE
            bk = k.reshape(b, h, w, WINDOW, d)
            bv = v.reshape(b, h, w, WINDOW, d)

            def look_around(t):
                p = jnp.pad(t, ((0, 0), (0, 0), (1, 0), (0, 0), (0, 0)))
                return jnp.concatenate([p[:, :, :w], p[:, :, 1:]], axis=3)
            bk, bv = (look_around(bk), look_around(bv))
            bt = jnp.arange(n).reshape(w, WINDOW)
            btp = jnp.pad(bt, ((1, 0), (0, 0)), constant_values=-1)
            btk = jnp.concatenate([btp[:w], btp[1:]], axis=1)
            sim = jnp.einsum('bhwid,bhwjd->bhwij', bq, bk)
            i = bt[:, :, None]
            j = btk[:, None, :]
            mask = (i < j) | (i > j + WINDOW) | (j == -1)
            sim = jnp.where(mask, -jnp.finfo(sim.dtype).max, sim)
            attn = jax.nn.softmax(sim, axis=-1)
            out = jnp.einsum('bhwij,bhwjd->bhwid', attn, bv)
            return out.reshape(b, h, n, d)

        def _layer(x, wqkv, qs, ksc, wo, lg, lb, w1, b1, w2, b2):
            b, n, _ = x.shape
            h = shift_token(x)
            qkv = h @ wqkv
            q, k, v = jnp.split(qkv, 3, axis=-1)
            to_heads = lambda t: t.reshape(b, n, HEADS, DIM_HEAD).transpose(0, 2, 1, 3)
            q, k, v = (to_heads(q), to_heads(k), to_heads(v))
            q = l2norm(q) * qs
            k = l2norm(k) * ksc
            q, k = rotary_xpos(q, k)
            o = local_attention(q, k, v)
            o = o.transpose(0, 2, 1, 3).reshape(b, n, INNER)
            x = x + o @ wo
            h = shift_token(x)
            mu = h.mean(-1, keepdims=True)
            var = h.var(-1, keepdims=True)
            h = (h - mu) / jnp.sqrt(var + 1e-05) * lg + lb
            h = h @ w1 + b1
            a, g = jnp.split(h, 2, axis=-1)
            h = a * jax.nn.gelu(g, approximate=False)
            x = x + h @ w2 + b2
            return x
        key = jax.random.key(seed)
        ks = jax.random.split(key, 6)
        return {'x': jax.random.normal(ks[0], (B, N, DIM), jnp.float32), 'wqkv': jax.random.normal(ks[1], (DEPTH, DIM, 3 * INNER), jnp.float32) * 0.02, 'q_scale': jnp.ones((DEPTH, DIM_HEAD), jnp.float32), 'k_scale': jnp.ones((DEPTH, DIM_HEAD), jnp.float32), 'wo': jax.random.normal(ks[2], (DEPTH, INNER, DIM), jnp.float32) * 0.02, 'ln_g': jnp.ones((DEPTH, DIM), jnp.float32), 'ln_b': jnp.zeros((DEPTH, DIM), jnp.float32), 'w1': jax.random.normal(ks[3], (DEPTH, DIM, 2 * HID), jnp.float32) * 0.02, 'b1': jnp.zeros((DEPTH, 2 * HID), jnp.float32), 'w2': jax.random.normal(ks[4], (DEPTH, HID, DIM), jnp.float32) * 0.02, 'b2': jnp.zeros((DEPTH, DIM), jnp.float32)}
    _L0_ffn_in = _L0_ffn_setup()
    _L0_c = _w((lambda *s: np.random.randn(*s).astype(np.float32) * 0.05)(2, 128))
    _L0_wmod = _w((lambda *s: np.random.randn(*s).astype(np.float32) * 0.05)(128, 6 * 128) * 128 ** (-0.5))
    _d = {'L0_attn_x': _L0_attn_in['x'], 'L0_attn_Wq': _L0_attn_in['Wq'], 'L0_attn_Wk': _L0_attn_in['Wk'], 'L0_attn_Wv': _L0_attn_in['Wv'], 'L0_attn_Wo': _L0_attn_in['Wo'], 'L0_ffn_wqkv': _L0_ffn_in['wqkv'], 'L0_ffn_q_scale': _L0_ffn_in['q_scale'], 'L0_ffn_k_scale': _L0_ffn_in['k_scale'], 'L0_ffn_wo': _L0_ffn_in['wo'], 'L0_ffn_ln_g': _L0_ffn_in['ln_g'], 'L0_ffn_ln_b': _L0_ffn_in['ln_b'], 'L0_ffn_w1': _L0_ffn_in['w1'], 'L0_ffn_b1': _L0_ffn_in['b1'], 'L0_ffn_w2': _L0_ffn_in['w2'], 'L0_ffn_b2': _L0_ffn_in['b2'], 'L0_c': _L0_c, 'L0_wmod': _L0_wmod}
    _x0 = _d['L0_attn_x']
    _d['L0_attn_x'] = jax.random.normal(jax.random.fold_in(jax.random.key(seed), 1), (2, 1024, 128), dtype=_x0.dtype)
    del _x0
    return _d

def reference(L0_attn_x, L0_attn_Wq, L0_attn_Wk, L0_attn_Wv, L0_attn_Wo, L0_ffn_wqkv, L0_ffn_q_scale, L0_ffn_k_scale, L0_ffn_wo, L0_ffn_ln_g, L0_ffn_ln_b, L0_ffn_w1, L0_ffn_b1, L0_ffn_w2, L0_ffn_b2, L0_c, L0_wmod):

    def _L0_attn_ref(x, Wq, Wk, Wv, Wo):
        import jax, jax.numpy as jnp
        import numpy as np
        import math
        B, L, D = (2, 256, 128)
        H, KV, HD = (16, 4, 64)
        GROUPS = H // KV
        ROPE_BASE = 10000.0

        def _alibi_slopes(n_heads):

            def pow2(n):
                start = 2.0 ** (-2.0 ** (-(math.log2(n) - 3)))
                return [start * start ** i for i in range(n)]
            if math.log2(n_heads).is_integer():
                return pow2(n_heads)
            c = 2 ** math.floor(math.log2(n_heads))
            return pow2(c) + _alibi_slopes(2 * c)[0::2][:n_heads - c]

        def _rope_cos_sin(seq_len, dim, dtype):
            inv_freq = 1.0 / ROPE_BASE ** (jnp.arange(0, dim, 2, dtype=jnp.float32) / dim)
            t = jnp.arange(seq_len, dtype=jnp.float32)
            freqs = t[:, None] * inv_freq[None, :]
            emb = jnp.concatenate([freqs, freqs], axis=-1)
            return (jnp.cos(emb).astype(dtype), jnp.sin(emb).astype(dtype))

        def _rotate_half(x):
            x1, x2 = (x[..., :x.shape[-1] // 2], x[..., x.shape[-1] // 2:])
            return jnp.concatenate([-x2, x1], axis=-1)
        b, l, _ = x.shape
        q = (x @ Wq).reshape(b, l, H, HD).transpose(0, 2, 1, 3)
        k = (x @ Wk).reshape(b, l, KV, HD).transpose(0, 2, 1, 3)
        v = (x @ Wv).reshape(b, l, KV, HD).transpose(0, 2, 1, 3)
        k = jnp.repeat(k, GROUPS, axis=1)
        v = jnp.repeat(v, GROUPS, axis=1)
        cos, sin = _rope_cos_sin(l, HD, x.dtype)
        q = q * cos + _rotate_half(q) * sin
        k = k * cos + _rotate_half(k) * sin
        attn = jnp.einsum('bhqd,bhkd->bhqk', q, k) / math.sqrt(HD)
        pos = jnp.arange(l)
        rel = (pos[None, :] - pos[:, None]).astype(x.dtype)
        slopes = jnp.asarray(_alibi_slopes(H), dtype=x.dtype)
        attn = attn + slopes[None, :, None, None] * rel[None, None, :, :]
        attn = jax.nn.softmax(attn, axis=-1)
        out = jnp.einsum('bhqk,bhkd->bhqd', attn, v)
        out = out.transpose(0, 2, 1, 3).reshape(b, l, H * HD)
        return out @ Wo

    def _L0_ffn_ref(x, wqkv, q_scale, k_scale, wo, ln_g, ln_b, w1, b1, w2, b2):
        import jax, jax.numpy as jnp
        import numpy as np
        DIM = 128
        DEPTH = 2
        HEADS = 8
        DIM_HEAD = 64
        WINDOW = 64
        INNER = HEADS * DIM_HEAD
        HID = int(DIM * 4 * 2 / 3)
        B, N = (2, 1024)
        QK_SCALE = 8.0

        def shift_token(t):
            t1, t2 = jnp.split(t, 2, axis=-1)
            t2 = jnp.pad(t2, ((0, 0), (1, 0), (0, 0)))[:, :-1]
            return jnp.concatenate([t1, t2], axis=-1)

        def l2norm(t):
            return t / jnp.clip(jnp.linalg.norm(t, axis=-1, keepdims=True), 1e-12)

        def rotate_half(x):
            x1, x2 = jnp.split(x, 2, axis=-1)
            return jnp.concatenate([-x2, x1], axis=-1)

        def rotary_xpos(q, k):
            n = q.shape[-2]
            half_idx = jnp.arange(0, DIM_HEAD, 2, dtype=jnp.float32)
            inv_freq = 1.0 / 10000.0 ** (half_idx / DIM_HEAD)
            t = jnp.arange(n, dtype=jnp.float32)
            freqs = t[:, None] * inv_freq[None, :]
            freqs = jnp.concatenate([freqs, freqs], axis=-1)
            base = (half_idx + 0.4 * DIM_HEAD) / (1.4 * DIM_HEAD)
            power = (t - n // 2) / float(WINDOW // 2)
            scale = base[None, :] ** power[:, None]
            scale = jnp.concatenate([scale, scale], axis=-1)
            cos, sin = (jnp.cos(freqs), jnp.sin(freqs))
            q = q * cos * scale + rotate_half(q) * sin * scale
            k = k * cos / scale + rotate_half(k) * sin / scale
            return (q, k)

        def local_attention(q, k, v):
            b, h, n, d = q.shape
            w = n // WINDOW
            bq = q.reshape(b, h, w, WINDOW, d) * QK_SCALE
            bk = k.reshape(b, h, w, WINDOW, d)
            bv = v.reshape(b, h, w, WINDOW, d)

            def look_around(t):
                p = jnp.pad(t, ((0, 0), (0, 0), (1, 0), (0, 0), (0, 0)))
                return jnp.concatenate([p[:, :, :w], p[:, :, 1:]], axis=3)
            bk, bv = (look_around(bk), look_around(bv))
            bt = jnp.arange(n).reshape(w, WINDOW)
            btp = jnp.pad(bt, ((1, 0), (0, 0)), constant_values=-1)
            btk = jnp.concatenate([btp[:w], btp[1:]], axis=1)
            sim = jnp.einsum('bhwid,bhwjd->bhwij', bq, bk)
            i = bt[:, :, None]
            j = btk[:, None, :]
            mask = (i < j) | (i > j + WINDOW) | (j == -1)
            sim = jnp.where(mask, -jnp.finfo(sim.dtype).max, sim)
            attn = jax.nn.softmax(sim, axis=-1)
            out = jnp.einsum('bhwij,bhwjd->bhwid', attn, bv)
            return out.reshape(b, h, n, d)

        def _layer(x, wqkv, qs, ksc, wo, lg, lb, w1, b1, w2, b2):
            b, n, _ = x.shape
            h = shift_token(x)
            qkv = h @ wqkv
            q, k, v = jnp.split(qkv, 3, axis=-1)
            to_heads = lambda t: t.reshape(b, n, HEADS, DIM_HEAD).transpose(0, 2, 1, 3)
            q, k, v = (to_heads(q), to_heads(k), to_heads(v))
            q = l2norm(q) * qs
            k = l2norm(k) * ksc
            q, k = rotary_xpos(q, k)
            o = local_attention(q, k, v)
            o = o.transpose(0, 2, 1, 3).reshape(b, n, INNER)
            x = x + o @ wo
            h = shift_token(x)
            mu = h.mean(-1, keepdims=True)
            var = h.var(-1, keepdims=True)
            h = (h - mu) / jnp.sqrt(var + 1e-05) * lg + lb
            h = h @ w1 + b1
            a, g = jnp.split(h, 2, axis=-1)
            h = a * jax.nn.gelu(g, approximate=False)
            x = x + h @ w2 + b2
            return x
        for l in range(DEPTH):
            x = _layer(x, wqkv[l], q_scale[l], k_scale[l], wo[l], ln_g[l], ln_b[l], w1[l], b1[l], w2[l], b2[l])
        return x
    x = L0_attn_x
    mod = (_silu(L0_c) @ L0_wmod).reshape(L0_c.shape[0], 6, 1, -1)
    sa, ca, ga, sb, cb, gb = (mod[:, 0], mod[:, 1], mod[:, 2], mod[:, 3], mod[:, 4], mod[:, 5])
    ga = (2 * (ga >= 0) - 1) * jnp.maximum(jnp.abs(ga), 0.25)
    gb = (2 * (gb >= 0) - 1) * jnp.maximum(jnp.abs(gb), 0.25)
    h = _layernorm(x, axis=-1) * (1 + ca) + sa
    x = x + ga * _L0_attn_ref(h, L0_attn_Wq, L0_attn_Wk, L0_attn_Wv, L0_attn_Wo)
    h = _layernorm(x, axis=-1) * (1 + cb) + sb
    x = x + gb * _L0_ffn_ref(h, L0_ffn_wqkv, L0_ffn_q_scale, L0_ffn_k_scale, L0_ffn_wo, L0_ffn_ln_g, L0_ffn_ln_b, L0_ffn_w1, L0_ffn_b1, L0_ffn_w2, L0_ffn_b2)
    return x

_drawn_inputs = setup_inputs


def setup_inputs(seed=0):
    import zlib

    import numpy as np

    out = dict(_drawn_inputs(seed))
    spreads = {'L0_ffn_q_scale': (1.0, 0.6),
     'L0_ffn_k_scale': (1.0, 0.6),
     'L0_ffn_ln_g': (1.0, 0.6),
     'L0_ffn_ln_b': (0.0, 0.8),
     'L0_ffn_b1': (0.0, 0.8),
     'L0_ffn_b2': (0.0, 0.8)}
    factors = {'L0_attn_Wq': 8.0,
     'L0_attn_Wk': 8.0,
     'L0_attn_Wv': 5.036,
     'L0_attn_Wo': 6.061,
     'L0_ffn_wqkv': 8.0,
     'L0_ffn_wo': 8.0,
     'L0_ffn_w1': 8.0,
     'L0_ffn_w2': 8.0}
    for name, (base, spread) in spreads.items():
        noise = np.random.default_rng([zlib.crc32(name.encode()), seed]).standard_normal(out[name].shape)
        drawn = base * np.exp(spread * noise) if base else spread * noise
        out[name] = jnp.asarray(drawn.astype(out[name].dtype))
    for name, factor in factors.items():
        out[name] = (out[name] * factor).astype(out[name].dtype)
    return out
```

```python
import math
from contextlib import ExitStack

import concourse.bass as bass
import numpy as np
from concourse import mybir

F32 = mybir.dt.float32
F32R = mybir.dt.float32r
ALU = mybir.AluOpType
ACT = mybir.ActivationFunctionType
AX_X = mybir.AxisListType.X

P = 128
B, N, D = 2, 1024, 128
TB = N // P
T = B * TB
H, KV, HD = 16, 4, 64
PAIRS = H // 2
GROUP = H // KV
HEADS = B * H
QW, KW = H * HD, KV * HD
DEPTH, FH, WIN = 2, 8, 64
INNER = FH * HD
HID = int(D * 4 * 2 / 3)
HC = -(-HID // P)
HLAST = HID - (HC - 1) * P
EPS = 1e-5
BIG = 3e38
POOL_SUMS = (0, 1, 2, 4, 6)
DVE_SUMS = (3, 5, 7)


def shape_constants():
    f = np.float32
    pos = np.arange(N, dtype=f)
    inv = (f(1.0) / f(10000.0) ** (np.arange(0, HD, 2, dtype=f) / f(HD))).astype(f)
    ang = (pos[:, None] * inv[None, :]).astype(f).astype(np.float64)
    cos, sin = np.cos(ang).astype(f), np.sin(ang).astype(f)
    rope = np.stack([np.concatenate([cos, cos], 1), np.concatenate([sin, -sin], 1)], 1)
    half = np.arange(0, HD, 2, dtype=f)
    base = ((half + f(0.4 * HD)) / f(1.4 * HD)).astype(f)
    power = ((pos - f(N // 2)) / f(WIN // 2)).astype(f)
    scale = np.power(base[None, :].astype(np.float64), power[:, None].astype(np.float64))
    xc, xs = [], []
    for s in (8.0 * scale, 1.0 / scale):
        xc.append(np.concatenate([cos * s, cos * s], 1))
        xs.append(np.concatenate([sin * s, -sin * s], 1))
    xpos = np.stack([np.concatenate(xc, 1), np.concatenate(xs, 1)], 1).astype(f)
    start = 2.0 ** (-2.0 ** (-(math.log2(H) - 3)))
    slopes = np.array([start * start ** i for i in range(H)])
    far = np.arange(N) - (N - 1)
    bias = slopes[None, :, None] * far.reshape(TB, P).T[:, None, :]
    i = (np.arange(P) % WIN)[:, None]
    j = np.arange(2 * WIN)[None, :]
    seen = (j <= i + WIN) & (j >= i)
    mask = np.zeros((P, TB, 2 * WIN), f)
    mask[:] = np.where(seen, 0.0, -1e30)[:, None, :]
    mask[:WIN, 0, :WIN] = -1e30
    first = np.ones((P, T), f)
    first[:, ::TB] = 0.0
    return {
        "ident": np.eye(P, dtype=f),
        "rope": rope.astype(f),
        "xpos": xpos,
        "far": far.astype(f)[None, :],
        "slope": np.tile(slopes.astype(f)[None, :], (P, B)),
        "keybias": np.tile(bias.astype(f), (1, B, 1)),
        "mask": mask,
        "notfirst": first,
    }


def need(eng, sem, count):
    if isinstance(count, int) and count <= 0:
        return
    eng.wait_ge(sem, count)


def over_tiles(eng, stages):
    deepest = max(lag for _, lag in stages)
    first = deepest + 2 + deepest % 2

    def step(s, parity):
        for fn, lag in stages:
            if isinstance(s, int) and not 0 <= s - lag < T:
                continue
            fn(s - lag, (parity - lag) % 2)

    for s in range(T + deepest):
        step(s, s % 2)


def over_heads(eng, head):
    for i in range(HEADS):
        head(i, i % 8)


def adaln_block(nc, x, wq, wk, wv, wo, f_wqkv, f_qs, f_ks, f_wo, f_lg, f_lb, f_w1, f_b1, f_w2, f_b2,
                c, wmod, ident_d, rope_d, xpos_d, far_d, slope_d, keybias_d, mask_d, notfirst_d, out):
    qa_d = nc.dram_tensor("qa_scratch", (B, H, P, TB, P), F32, kind="Internal").ap()
    ka_d = nc.dram_tensor("ka_scratch", (B, KV, P, TB, P), F32, kind="Internal").ap()
    kb_d = nc.dram_tensor("kb_scratch", (B, KV, P, TB, P), F32, kind="Internal").ap()
    v_d = nc.dram_tensor("v_scratch", (B, KV, P, TB, HD), F32, kind="Internal").ap()

    with ExitStack() as whole:
        whole.enter_context(nc.allow_non_contiguous_dma(reason="a few columns of biases"))

        def sb_in(ctx):
            return lambda name, shape, dt=F32: ctx.enter_context(nc.sbuf_tensor(name, shape, dt))

        def sem_in(ctx):
            return lambda name: ctx.enter_context(nc.semaphore(name))

        sb, gsem = sb_in(whole), sem_in(whole)
        psum = whole.enter_context(nc.psum_tensor("psum", [P, 8, 512], F32))

        def banks(a, n=1):
            return psum[:, a:a + n, :].rearrange("p b c -> p (b c)")

        X = sb("X", [P, T, D])
        XF = sb("XF", [P, T, D])
        ident = sb("ident", [P, P])
        rows = sb("rows", [P, B, 4, D])
        minus_half = sb("minus_half", [P, 2 * FH])
        cols = sb("cols", [P, B, 6])
        ga, sbr, cbr, gbr = range(4)
        wo_sb = sb("wo_sb", [P, PAIRS, D])
        fw_qkv = sb("fw_qkv", [P, DEPTH, 3 * INNER])
        fw_o = sb("fw_o", [P, DEPTH, FH // 2, D])
        fw_1 = sb("fw_1", [P, DEPTH, 2 * HID])
        fw_2 = sb("fw_2", [P, DEPTH, HC, D])
        fb_1 = sb("fb_1", [P, DEPTH, 2, HC])
        f_ln = sb("f_ln", [P, DEPTH, 2])
        loaded_late = gsem("loaded_late")
        late_loads = []

        with ExitStack() as ph:
            sb, sem = sb_in(ph), sem_in(ph)
            w_sb = sb("w_sb", [P, QW + 2 * KW])
            rope = sb("rope_sb", [P, TB, 2, HD])
            wmod_sb = sb("wmod_sb", [P, 6 * D])
            cT = sb("cT", [P, B])
            ec = sb("ec", [P, B])
            silu = sb("silu", [P, B])
            silu_wide = sb("silu_wide", [P, B, P])
            guard = sb("guard", [P, B, 2, 2, D])
            bn = sb("bn", [P, 2, 6])
            mv = sb("mv", [P, 2, 2])
            rstd = sb("rstd", [P, 2, 1])
            var_eps = sb("var_eps", [P, 2, 1])
            xn = sb("xn", [P, 2, D])
            hT = sb("hT", [P, 2, P])
            t1 = sb("t1", [P, H + KV, HD])
            t2 = sb("t2", [P, H + KV, HD])
            qk = sb("qk", [P, 2, H + KV, HD])
            qs_ = sb("q_split", [P, 2, H, P], F32R)
            ks_ = sb("k_split", [P, 2, 2, KV, P], F32R)
            v_sb = sb("v_sb", [P, 2, KW])
            tT = sb("tT", [P, 2, H + 2 * KV, P], F32R)
            zeros = sb("zeros", [P, KV, HD])
            ones = sb("ones", [P, KV, 1])

            ld_x = sem("ld_x")
            ld_c = sem("ld_c")
            ld_w = sem("ld_w")
            ld_mod = sem("ld_mod")
            ld_rope = sem("ld_rope")
            ec_done = sem("ec_done")
            silu_step = sem("silu_step")
            wide_done = sem("wide_done")
            mod_mm = sem("mod_mm")
            mod_step = sem("mod_step")
            const_step = sem("const_step")
            ln_step = sem("ln_step")
            rstd_done = sem("rstd_done")
            eps_done = sem("eps_done")
            half_set = sem("half_set")
            xn_done = sem("xn_done")
            xT_done = sem("xT_done")
            hT_done = sem("hT_done")
            qkv_done = sem("qkv_done")
            v_copied = sem("v_copied")
            rope_step = sem("rope_step")
            high_done = sem("high_done")
            low_done = sem("low_done")
            tr_done = sem("tr_done")
            tr_copied = sem("tr_copied")
            v_out = [sem("v_out0"), sem("v_out1")]
            t_out = [sem("t_out0"), sem("t_out1")]

            ps_qk = banks(0, 3)[:, 0:QW + KW].rearrange("p (h d) -> p h d", d=HD)
            ps_v = banks(3)[:, 0:KW]
            ps_x = banks(7)[:, 0:P]
            NTR = (H + 2 * KV) // 4

            with nc.Block() as block:
                @block.sync
                def _(sp):
                    sp.dma_start(X[:, 0:TB, :], x[0].rearrange("(t p) d -> p t d", p=P)).then_inc(ld_x, 16)
                    sp.dma_start(cT[:, :], c.rearrange("b d -> d b")).then_inc(ld_c, 16)
                    sp.dma_start(wmod_sb[:, :], wmod).then_inc(ld_mod, 16)
                    sp.dma_start(ident[:, :], ident_d).then_inc(ld_w, 16)
                    sp.dma_start(w_sb[:, 0:QW], wq).then_inc(ld_w, 16)
                    sp.dma_start(w_sb[:, QW:QW + KW], wk).then_inc(ld_w, 16)
                    sp.dma_start(w_sb[:, QW + KW:], wv).then_inc(ld_w, 16)
                    sp.dma_start(rope[:, :, :, :], rope_d.rearrange("(t p) s d -> p t s d", p=P)).then_inc(ld_rope, 16)
                    sp.dma_start(X[:, TB:T, :], x[1].rearrange("(t p) d -> p t d", p=P)).then_inc(ld_rope, 16)

                    def store(t, s):
                        need(sp, v_copied, t + 1)
                        sp.dma_start(v_d[t // TB, :, :, t % TB, :].rearrange("g p d -> p g d"),
                                     v_sb[:, s, :].rearrange("p (g d) -> p g d", d=HD)).then_inc(v_out[s], 16)
                        need(sp, tr_copied, NTR * (t + 1))
                        sp.dma_start(qa_d[t // TB, :, :, t % TB, :].rearrange("h p c -> p h c"),
                                     tT[:, s, 0:H, :].bitcast(F32)).then_inc(t_out[s], 16)
                        sp.dma_start(ka_d[t // TB, :, :, t % TB, :].rearrange("h p c -> p h c"),
                                     tT[:, s, H:H + KV, :].bitcast(F32)).then_inc(t_out[s], 16)
                        sp.dma_start(kb_d[t // TB, :, :, t % TB, :].rearrange("h p c -> p h c"),
                                     tT[:, s, H + KV:, :].bitcast(F32)).then_inc(t_out[s], 16)

                    over_tiles(sp, [(store, 0)])
                    for s in range(2):
                        sp.wait_ge(v_out[s], 16 * (T // 2))
                        sp.wait_ge(t_out[s], 48 * (T // 2))

                @block.gpsimd
                def _(pool):
                    def late(dst, src):
                        pool.dma_start(dst, src).then_inc(loaded_late, 16)
                        late_loads.append(1)

                    late(wo_sb[:, :, :], wo.rearrange("(j p) n -> p j n", p=P))
                    late(fw_qkv[:, :, :], f_wqkv.rearrange("l p n -> p l n"))
                    late(fw_o[:, :, :, :], f_wo.rearrange("l (j p) n -> p l j n", p=P))
                    late(fw_1[:, :, :], f_w1.rearrange("l p n -> p l n"))
                    late(f_ln[:, :, 0], f_lg.rearrange("l p -> p l"))
                    late(f_ln[:, :, 1], f_lb.rearrange("l p -> p l"))
                    for l in range(DEPTH):
                        late(fw_2[:, l, 0:HC - 1, :], f_w2[l, 0:(HC - 1) * P, :].rearrange("(j p) n -> p j n", p=P))
                        late(fw_2[0:HLAST, l, HC - 1, :], f_w2[l, (HC - 1) * P:HID, :])
                        late(fw_2[HLAST:HLAST + 1, l, HC - 1, :], f_b2[l:l + 1, :])
                        for s in range(2):
                            b1 = f_b1[l, s * HID:(s + 1) * HID]
                            late(fb_1[:, l, s, 0:HC - 1], b1[0:(HC - 1) * P].rearrange("(j p) -> p j", p=P))
                            late(fb_1[0:HLAST, l, s, HC - 1:HC], b1[(HC - 1) * P:HID].rearrange("(p o) -> p o", o=1))

                    def ln_rstd(t, s):
                        need(pool, ln_step, 2 * t + 2)
                        need(pool, xn_done, t - 1)
                        pool.tensor_scalar(var_eps[:, s, :], mv[:, s, 1:2], EPS, None, ALU.add).then_inc(eps_done, 1)
                        need(pool, eps_done, t + 1)
                        pool.tensor_tensor(rstd[:, s, :], var_eps[:, s, :], minus_half[:, 0:1], ALU.pow).then_inc(rstd_done, 1)

                    pool.memset(minus_half[:, :], -0.5).then_inc(half_set, 1)
                    pool.wait_ge(half_set, 1)
                    over_tiles(pool, [(ln_rstd, 0)])

                @block.scalar
                def _(act):
                    act.wait_ge(ld_c, 16)
                    act.activation(ec[:, :], cT[:, :], ACT.Exp, scale=-1.0).then_inc(ec_done, 1)

                    def modulate(t, s):
                        need(act, xT_done, t + 1)
                        if isinstance(t, int) and t == 0:
                            act.wait_ge(mod_step, 9)
                        need(act, qkv_done, t - 1)
                        act.activation(hT[:, s, :], ps_x, ACT.Identity, bias=cols[:, t // TB, 0:1],
                                       scale=cols[:, t // TB, 1:2]).then_inc(hT_done, 1)

                    def take_v(t, s):
                        need(act, qkv_done, t + 1)
                        need(act, v_out[s], 16 * (t // 2))
                        act.activation(v_sb[:, s, :], ps_v, ACT.Copy).then_inc(v_copied, 1)

                    def take_transposed(t, s):
                        need(act, t_out[s], 48 * (t // 2))
                        for g in range(NTR):
                            need(act, tr_done, NTR * t + g + 1)
                            act.activation(tT[:, s, 4 * g:4 * g + 4, :].rearrange("p h c -> p (h c)"),
                                           banks(4 + g % 3), ACT.Copy).then_inc(tr_copied, 1)

                    def high_parts(t, s):
                        need(act, rope_step, 4 * t + 4)
                        need(act, tr_done, NTR * (t - 1))
                        act.activation(qs_[:, s, :, 0:HD], qk[:, s, 0:H, :], ACT.Copy, scale=HD ** -0.5)\
                            .then_inc(high_done, 1)
                        for r in range(2):
                            act.activation(ks_[:, s, 0, :, r * HD:(r + 1) * HD], qk[:, s, H:, :], ACT.Copy)\
                                .then_inc(high_done, 1)

                    over_tiles(act, [(modulate, 0), (take_v, 0), (take_transposed, 1), (high_parts, 0)])

                @block.vector
                def _(dve):
                    dve.wait_ge(ec_done, 1)
                    dve.tensor_scalar(ec[:, :], ec[:, :], 1.0, None, ALU.add).then_inc(silu_step, 1)
                    dve.wait_ge(silu_step, 1)
                    dve.wait_ge(ld_c, 16)
                    dve.reciprocal(ec[:, :], ec[:, :]).then_inc(silu_step, 1)
                    dve.wait_ge(silu_step, 2)
                    dve.tensor_tensor(silu[:, :], cT[:, :], ec[:, :], ALU.mult).then_inc(silu_step, 1)
                    dve.wait_ge(silu_step, 3)
                    for b in range(B):
                        dve.tensor_copy(silu_wide[:, b, :], silu[:, b:b + 1].to_broadcast([P, P])).then_inc(wide_done, 1)
                    dve.memset(zeros[:, :, :], 0.0).then_inc(const_step, 1)
                    dve.memset(ones[:, :, :], 1.0).then_inc(const_step, 1)
                    dve.wait_ge(const_step, 2)
                    for s in range(2):
                        dve.tensor_copy(ks_[:, s, 1, :, HD:HD + 1], ones[:, :, :]).then_inc(const_step, 1)
                        dve.tensor_copy(ks_[:, s, 1, :, HD + 1:P], zeros[:, :, 0:HD - 1]).then_inc(const_step, 1)
                    dve.wait_ge(mod_mm, 1)
                    mod_ps = banks(7)[:, 0:6 * B].rearrange("p (m b) -> p m b", b=B)
                    dve.tensor_copy(cols[:, :, 0], mod_ps[:, 0, :]).then_inc(mod_step, 1)
                    dve.tensor_scalar(cols[:, :, 1], mod_ps[:, 1, :], 1.0, None, ALU.add).then_inc(mod_step, 1)
                    for b in range(B):
                        dve.wait_ge(mod_mm, 2 + b)
                        ps = banks(b).rearrange("p (m d) -> p m d", d=D)
                        gates = ps[:, 0:4:3, :]
                        dve.tensor_scalar(guard[:, b, 0, :, :], gates, 0.0, 2.0, ALU.is_ge, ALU.mult)\
                            .then_inc(const_step, 1)
                        dve.tensor_scalar(guard[:, b, 1, :, :], gates, 0.25, None, ALU.max).then_inc(const_step, 1)
                        dve.wait_ge(const_step, 8 + 3 * b)
                        dve.scalar_tensor_tensor(guard[:, b, 1, :, :], gates, -1.0, guard[:, b, 1, :, :],
                                                 ALU.mult, ALU.max).then_inc(const_step, 1)
                        dve.wait_ge(const_step, 9 + 3 * b)
                        dve.scalar_tensor_tensor(rows[:, b, 0:4:3, :], guard[:, b, 0, :, :], -1.0,
                                                 guard[:, b, 1, :, :], ALU.add, ALU.mult).then_inc(mod_step, 1)
                        dve.tensor_copy(rows[:, b, 1, :], ps[:, 1, :]).then_inc(mod_step, 1)
                        dve.tensor_scalar(rows[:, b, 2, :], ps[:, 2, :], 1.0, None, ALU.add).then_inc(mod_step, 1)
                    dve.tensor_copy(zeros[:, 0, 0:1], ones[:, 0, :]).then_inc(mod_step, 1)
                    dve.wait_ge(ld_x, 16)
                    dve.wait_ge(ld_rope, 32)

                    def ln_stats(t, s):
                        need(dve, xn_done, t - 1)
                        dve.bn_stats(bn[:, s, :], X[:, t, :]).then_inc(ln_step, 1)
                        dve.wait_ge(ln_step, 2 * t + 1)
                        dve.bn_aggr(mv[:, s, :], bn[:, s, :]).then_inc(ln_step, 1)

                    def ln_apply(t, s):
                        need(dve, rstd_done, t + 1)
                        need(dve, xT_done, t - 1)
                        dve.tensor_scalar(xn[:, s, :], X[:, t, :], mv[:, s, 0:1], rstd[:, s, :],
                                          ALU.subtract, ALU.mult).then_inc(xn_done, 1)

                    def rotate(t, s):
                        need(dve, qkv_done, t + 1)
                        cos = rope[:, t % TB, 0, :][:, None, :].to_broadcast([P, H + KV, HD])
                        sin = rope[:, t % TB, 1, :][:, None, :].to_broadcast([P, H + KV, HD])
                        dve.tensor_tensor(t1[:, :, :], ps_qk, cos, ALU.mult).then_inc(rope_step, 1)
                        dve.tensor_tensor(t2[:, :, :], ps_qk, sin, ALU.mult).then_inc(rope_step, 1)
                        dve.wait_ge(rope_step, 4 * t + 2)
                        need(dve, high_done, 3 * (t - 1))
                        need(dve, low_done, 2 * (t - 1))
                        m = HD // 2
                        dve.tensor_tensor(qk[:, s, :, 0:m], t1[:, :, 0:m], t2[:, :, m:HD], ALU.add).then_inc(rope_step, 1)
                        dve.tensor_tensor(qk[:, s, :, m:HD], t1[:, :, m:HD], t2[:, :, 0:m], ALU.add).then_inc(rope_step, 1)

                    def low_parts(t, s):
                        need(dve, high_done, 3 * t + 3)
                        need(dve, tr_done, NTR * (t - 1))
                        dve.scalar_tensor_tensor(qs_[:, s, :, HD:P], qk[:, s, 0:H, :], HD ** -0.5,
                                                 qs_[:, s, :, 0:HD].bitcast(F32), ALU.mult, ALU.subtract)\
                            .then_inc(low_done, 1)
                        dve.tensor_tensor(ks_[:, s, 1, :, 0:HD], qk[:, s, H:, :],
                                          ks_[:, s, 0, :, 0:HD].bitcast(F32), ALU.subtract).then_inc(low_done, 1)

                    over_tiles(dve, [(ln_stats, 0), (ln_apply, 0), (rotate, 0), (low_parts, 0)])

                @block.tensor
                def _(pe):
                    pe.wait_ge(ld_mod, 16)
                    pe.wait_ge(silu_step, 3)
                    for m in range(6):
                        last = pe.matmul(banks(7)[:, B * m:B * m + B], wmod_sb[:, m * D:(m + 1) * D],
                                         silu[:, :], start=True, stop=True)
                    last.then_inc(mod_mm, 1)
                    pe.wait_ge(wide_done, B)
                    for b in range(B):
                        pe.matmul(banks(b), silu_wide[:, b, :], wmod_sb[:, 2 * D:6 * D], start=True, stop=True)\
                            .then_inc(mod_mm, 1)
                    pe.wait_ge(ld_w, 64)
                    pe.wait_ge(mod_step, 9)

                    def x_transposed(t, s):
                        need(pe, xn_done, t + 1)
                        need(pe, hT_done, t)
                        pe.transpose(ps_x, xn[:, s, :], ident[:, :]).then_inc(xT_done, 1)

                    def project(t, s):
                        need(pe, hT_done, t + 1)
                        need(pe, rope_step, 4 * t - 2)
                        need(pe, v_copied, t)
                        for n in range(2):
                            pe.matmul(banks(n), hT[:, s, :], w_sb[:, n * 512:(n + 1) * 512], start=True, stop=True)
                        pe.matmul(banks(2)[:, 0:KW], hT[:, s, :], w_sb[:, QW:QW + KW], start=True, stop=True)
                        pe.matmul(ps_v, hT[:, s, :], w_sb[:, QW + KW:], start=True, stop=True).then_inc(qkv_done, 1)

                    def split_transposed(t, s):
                        need(pe, low_done, 2 * t + 2)
                        for g in range(NTR):
                            need(pe, tr_copied, NTR * t + g - 2)
                            for j in range(4):
                                h = 4 * g + j
                                src = qs_[:, s, h, :] if h < H else ks_[:, s, (h - H) // KV, (h - H) % KV, :]
                                last = pe.transpose(banks(4 + g % 3)[:, j * P:(j + 1) * P], src.bitcast(F32),
                                                    ident[:, :])
                            last.then_inc(tr_done, 1)

                    over_tiles(pe, [(x_transposed, 0), (project, 0), (split_transposed, 1)])

        mid = ExitStack()
        OT = sb_in(mid)("OT", [P, B, PAIRS, TB, P])
        with ExitStack() as ph:
            sb, sem = sb_in(ph), sem_in(ph)
            QA = sb("QA", [P, 4, N], F32R)
            QB = sb("QB", [P, 2, N], F32R)
            KA = sb("KA", [P, 2, N], F32R)
            KB = sb("KB", [P, 2, N], F32R)
            V = sb("V", [P, 2, TB, HD])
            far = sb("far_sb", [P, N])
            slope = sb("slope_sb", [P, HEADS])
            keybias = sb("keybias_sb", [P, HEADS, TB])
            alibi = sb("alibi", [P, 2, N])
            junk = sb("junk", [P, N], mybir.dt.bfloat16)
            M = sb("M", [P, 2, TB])
            mrow = sb("mrow", [TB, 2, P], F32R)
            E = sb("E", [P, 4, N])
            sum_p = sb("sum_p", [P, 2, N])
            sum_d = sb("sum_d", [P, 2, N])
            den_sb = XF[:, 0:4, :].rearrange("p t d -> p (t d)")
            den_inv = XF[:, 4:8, :].rearrange("p t d -> p (t d)")
            ones = sb("ones_m", [P, HD])

            ld_const = sem("ld_const")
            ld_qa = [sem(f"ld_qa{s}") for s in range(4)]
            ld_qb = [sem(f"ld_qb{s}") for s in range(2)]
            ld_m = [sem(f"ld_m{s}") for s in range(2)]
            ld_kv = [sem(f"ld_kv{s}") for s in range(2)]
            qb_zeroed = sem("qb_zeroed")
            alibi_done = sem("alibi_done")
            max_mm = sem("max_mm")
            max_done = sem("max_done")
            m_turned = sem("m_turned")
            mrow_done = sem("mrow_done")
            qk_done = sem("qk_done")
            exp_done = sem("exp_done")
            pv_done = sem("pv_done")
            sum_p_done = sem("sum_p_done")
            sum_d_done = sem("sum_d_done")
            den_mm = sem("den_mm")
            den_copied = sem("den_copied")
            inv_done = sem("inv_done")
            o_done = sem("o_done")
            NP, ND = len(POOL_SUMS) - 1, len(DVE_SUMS) - 1

            def scores(s):
                return banks(2 * s, 2)

            ps_max = banks(4, 2)

            with nc.Block() as block:
                @block.sync
                def _(sp):
                    sp.dma_start(far[:, :], far_d[0].partition_broadcast(P)).then_inc(ld_const, 16)
                    sp.dma_start(slope[:, :], slope_d).then_inc(ld_const, 16)
                    sp.dma_start(keybias[:, :, :], keybias_d).then_inc(ld_const, 16)

                    def load_qa(i, s):
                        sp.dma_start(QA[:, s, :].bitcast(F32).rearrange("p (t c) -> p t c", c=P), qa_d[i // H, i % H])\
                            .then_inc(ld_qa[s], 16)

                    def load_qb(i, s):
                        sp.dma_start(QB[0:HD, s, :].bitcast(F32).rearrange("p (t c) -> p t c", c=P), qa_d[i // H, i % H, 0:HD])\
                            .then_inc(ld_qb[s], 16)

                    def load_m(i, s):
                        need(sp, mrow_done, i + 1)
                        sp.dma_start(QB[HD:HD + 1, s, :].bitcast(F32).rearrange("p (t c) -> p t c", c=P),
                                     mrow[:, s, :].bitcast(F32)).then_inc(ld_m[s], 16)

                    def load_kv(g, s):
                        sp.dma_start(KA[:, s, :].bitcast(F32).rearrange("p (t c) -> p t c", c=P), ka_d[g // KV, g % KV])\
                            .then_inc(ld_kv[s], 16)
                        sp.dma_start(KB[:, s, :].bitcast(F32).rearrange("p (t c) -> p t c", c=P), kb_d[g // KV, g % KV])\
                            .then_inc(ld_kv[s], 16)
                        sp.dma_start(V[:, s, :, :], v_d[g // KV, g % KV]).then_inc(ld_kv[s], 16)

                    load_kv(0, 0)
                    for i in range(3):
                        load_qa(i, i)
                    sp.wait_ge(qb_zeroed, 4)
                    load_qb(0, 0)
                    load_m(0, 0)

                    def head(i, u):
                        fixed = isinstance(i, int)
                        need(sp, qk_done, TB * i)
                        if u % GROUP == 0 and not (fixed and i // GROUP + 1 >= HEADS // GROUP):
                            need(sp, pv_done, TB * i)
                            load_kv(i // GROUP + 1, (u // GROUP + 1) % 2)
                        if not (fixed and i + 3 >= HEADS):
                            load_qa(i + 3, (u + 3) % 4)
                        if not (fixed and i + 1 >= HEADS):
                            load_qb(i + 1, (u + 1) % 2)
                            load_m(i + 1, (u + 1) % 2)

                    over_heads(sp, head)

                @block.gpsimd
                def _(pool):
                    def head(i, u):
                        s = u % 2
                        need(pool, den_mm, i - 1)
                        for n, k in enumerate(POOL_SUMS[1:]):
                            need(pool, exp_done, TB * i + k + 1)
                            need(pool, sum_p_done, NP * i + n)
                            first = E[:, POOL_SUMS[0], :] if n == 0 else sum_p[:, s, :]
                            pool.tensor_tensor(sum_p[:, s, :], first, E[:, k % 4, :], ALU.add)\
                                .then_inc(sum_p_done, 1)

                    over_heads(pool, head)

                @block.scalar
                def _(act):
                    act.wait_ge(ld_const, 48)

                    def alibi_row(i, s):
                        need(act, max_done, TB * (i - 1))
                        act.activation(alibi[:, s, :], far[:, :], ACT.Identity,
                                       scale=slope[:, bass.ds(i, 1)])\
                            .then_inc(alibi_done, 1)

                    def take_m(i, s):
                        need(act, m_turned, i + 1)
                        need(act, ld_m[s], 16 * (i // 2))
                        act.activation(mrow[:, s, :], banks(5)[0:TB, 0:P], ACT.Copy).then_inc(mrow_done, 1)

                    def head(i, u):
                        fixed = isinstance(i, int)
                        if not (fixed and i + 2 >= HEADS):
                            alibi_row(i + 2, u % 2)
                        for k in range(TB):
                            need(act, qk_done, TB * i + k + 1)
                            need(act, pv_done, TB * i + k - 3)
                            j, old = (i, k - 4) if k >= 4 else (i - 1, k + 4)
                            if old in POOL_SUMS:
                                need(act, sum_p_done, NP * j + max(1, POOL_SUMS.index(old)))
                            else:
                                need(act, sum_d_done, ND * j + max(1, DVE_SUMS.index(old)))
                            kb = keybias[:, i, k:k + 1]
                            act.activation(E[:, k % 4, :], scores(k % 2), ACT.Exp, bias=kb).then_inc(exp_done, 1)
                            if k == 3:
                                if not (fixed and i == 0):
                                    need(act, den_mm, i)
                                    need(act, inv_done, i - 1)
                                    act.activation(den_sb[:, :], banks(4), ACT.Copy).then_inc(den_copied, 1)
                                if not (fixed and i + 1 >= HEADS):
                                    take_m(i + 1, (u + 1) % 2)

                    alibi_row(0, 0)
                    alibi_row(1, 1)
                    take_m(0, 0)
                    over_heads(act, head)
                    act.wait_ge(den_mm, HEADS)
                    act.wait_ge(inv_done, HEADS - 1)
                    act.activation(den_sb[:, :], banks(4), ACT.Copy).then_inc(den_copied, 1)

                @block.vector
                def _(dve):
                    dve.memset(ones[:, :], 1.0).then_inc(qb_zeroed, 1)
                    dve.memset(junk[:, :], 0.0).then_inc(qb_zeroed, 1)
                    dve.wait_ge(qb_zeroed, 2)
                    for s in range(2):
                        dve.tensor_copy(QB[HD:P, s, :], junk[HD:P, :]).then_inc(qb_zeroed, 1)

                    def max_step(i, s, k):
                        need(dve, max_mm, TB * i + k + 1)
                        if k == 0:
                            need(dve, alibi_done, i + 1)
                            need(dve, m_turned, i - 1)
                        need(dve, max_done, TB * i + k)
                        dve.tensor_tensor_reduce(junk[:, :], ps_max, alibi[:, s, :], -1.0, BIG, ALU.add, ALU.min,
                                                 M[:, s, k:k + 1]).then_inc(max_done, 1)

                    def sum_step(i, s, n):
                        k = DVE_SUMS[n + 1]
                        need(dve, exp_done, TB * i + k + 1)
                        need(dve, sum_d_done, ND * i + n)
                        if n == 0:
                            need(dve, den_mm, i - 1)
                        first = E[:, DVE_SUMS[0] % 4, :] if n == 0 else sum_d[:, s, :]
                        dve.tensor_tensor(sum_d[:, s, :], first, E[:, k % 4, :], ALU.add).then_inc(sum_d_done, 1)

                    def divide(i, u):
                        need(dve, den_copied, i + 1)
                        need(dve, o_done, i)
                        dve.reciprocal(den_inv[:, :], den_sb[:, :]).then_inc(inv_done, 1)
                        need(dve, inv_done, i + 1)
                        need(dve, pv_done, TB * (i + 1))
                        for ch in range(2):
                            a, r = HD * ch, HD * (u % 2)
                            dst = OT[r:r + HD, i // H, (i % H) // 2, 4 * ch:4 * ch + 4, :].rearrange("p t c -> p (t c)")
                            last = dve.tensor_tensor(dst, banks(6 + u % 2)[a:a + HD, :], den_inv[a:a + HD, :], ALU.mult)
                        last.then_inc(o_done, 1)

                    def head(i, u):
                        fixed = isinstance(i, int)
                        for k in range(TB):
                            if not (fixed and i + 2 >= HEADS):
                                max_step(i + 2, u % 2, k)
                            if k == 0 and not (fixed and i == 0):
                                sum_step(i - 1, (u - 1) % 2, 1)
                            if k == 4 and not (fixed and i == 0):
                                divide(i - 1, (u - 1) % 8)
                            if k == 6:
                                sum_step(i, u % 2, 0)

                    for i in range(2):
                        for k in range(TB):
                            max_step(i, i, k)
                    over_heads(dve, head)
                    sum_step(HEADS - 1, (HEADS - 1) % 2, 1)
                    divide(HEADS - 1, (HEADS - 1) % 8)

                @block.tensor
                def _(pe):
                    pe.wait_ge(qb_zeroed, 4)

                    def max_step(i, u, k):
                        s, g = u % 4, (u // GROUP) % 2
                        if k == 0:
                            need(pe, ld_qa[s], 16 * (i // 4 + 1))
                            if u % GROUP == 0:
                                need(pe, ld_kv[g], 48 * (i // 8 + 1))
                            need(pe, mrow_done, 1 if not isinstance(i, int) or i >= 2 else 0)
                        need(pe, max_done, TB * i + k)
                        if k == 3:
                            if not isinstance(i, int) or i >= 3:
                                need(pe, den_copied, i - 2)
                            if not isinstance(i, int) or i >= 2:
                                need(pe, mrow_done, i)
                        for ch in range(2):
                            last = pe.matmul(banks(4 + ch), QA[:, s, k * P:(k + 1) * P],
                                             KA[:, g, ch * 512:(ch + 1) * 512], start=True, stop=True)
                        last.then_inc(max_mm, 1)

                    def turn_m(i, s):
                        need(pe, max_done, TB * (i + 1))
                        pe.transpose(banks(5)[0:TB, 0:P], M[:, s, :], ident[:, :]).then_inc(m_turned, 1)

                    def qk_step(i, u, k):
                        g = (u // GROUP) % 2
                        if k == 0:
                            need(pe, ld_qb[u % 2], 16 * (i // 2 + 1))
                            need(pe, ld_m[u % 2], 16 * (i // 2 + 1))
                        need(pe, exp_done, TB * i + k - 1)
                        for ch in range(2):
                            pe.matmul(scores(k % 2)[:, ch * 512:(ch + 1) * 512], KA[:, g, k * P:(k + 1) * P],
                                      QA[:, u % 4, ch * 512:(ch + 1) * 512], start=True, stop=False)
                        for ch in range(2):
                            last = pe.matmul(scores(k % 2)[:, ch * 512:(ch + 1) * 512], KB[:, g, k * P:(k + 1) * P],
                                             QB[:, u % 2, ch * 512:(ch + 1) * 512], start=False, stop=True)
                        last.then_inc(qk_done, 1)

                    def pv_step(i, u, k):
                        g = (u // GROUP) % 2
                        need(pe, exp_done, TB * i + k + 1)
                        if k == 0:
                            need(pe, o_done, i - 1)
                        for ch in range(2):
                            last = pe.matmul(banks(6 + u % 2)[HD * ch:HD * ch + HD, :], V[:, g, k, :],
                                             E[:, k % 4, ch * 512:(ch + 1) * 512], start=(k == 0), stop=(k == TB - 1))
                        last.then_inc(pv_done, 1)

                    def denominators(i, s):
                        need(pe, sum_p_done, NP * (i + 1))
                        need(pe, sum_d_done, ND * (i + 1))
                        for n, part in enumerate((sum_p, sum_d)):
                            for ch in range(2):
                                last = pe.matmul(banks(4)[HD * ch:HD * ch + HD, :], ones[:, :],
                                                 part[:, s, ch * 512:(ch + 1) * 512], start=(n == 0), stop=(n == 1))
                        last.then_inc(den_mm, 1)

                    def head(i, u):
                        fixed = isinstance(i, int)
                        for k in range(TB):
                            qk_step(i, u, k)
                            if k == 3:
                                if fixed and i + 2 >= HEADS:
                                    need(pe, mrow_done, i + 1)
                                    need(pe, den_copied, i - 1)
                                need(pe, max_done, min(TB * (i + 2) + 3, TB * HEADS) if fixed else TB * (i + 2) + 3)
                                if not (fixed and i == 0):
                                    denominators(i - 1, (u - 1) % 2)
                                if not (fixed and i + 1 >= HEADS):
                                    turn_m(i + 1, (u + 1) % 2)
                            if not (fixed and i + 2 >= HEADS):
                                max_step(i + 2, (u + 2) % 8, k)
                            if k > 0:
                                pv_step(i, u, k - 1)
                            elif not (fixed and i == 0):
                                pv_step(i - 1, (u - 1) % 8, TB - 1)

                    for i in range(2):
                        for k in range(TB):
                            max_step(i, i, k)
                    need(pe, max_done, 2 * TB)
                    turn_m(0, 0)
                    over_heads(pe, head)
                    pv_step(HEADS - 1, (HEADS - 1) % 8, TB - 1)
                    pe.wait_ge(den_copied, HEADS - 1)
                    denominators(HEADS - 1, (HEADS - 1) % 2)

        with ExitStack() as ph:
            sb, sem = sb_in(ph), sem_in(ph)
            ot = sb("ot", [P, 2, PAIRS, P])
            y = sb("y", [P, 2, D])
            bn = sb("bn_o", [P, 2, 6])
            mv = sb("mv_o", [P, 2, 2])
            rstd = sb("rstd_o", [P, 2, 1])
            var_eps = sb("var_eps_o", [P, 2, 1])
            xn = sb("xn_o", [P, 2, D])
            staged = sem("staged")
            proj_done = sem("proj_done")
            res_step = sem("res_step")
            rstd_done = sem("rstd_done_o")
            eps_done = sem("eps_done_o")
            mod_step = sem("mod_step_o")

            with nc.Block() as block:
                @block.gpsimd
                def _(pool):
                    def ln_rstd(t, s):
                        need(pool, res_step, 4 * t + 4)
                        need(pool, mod_step, 3 * (t - 1))
                        pool.tensor_scalar(var_eps[:, s, :], mv[:, s, 1:2], EPS, None, ALU.add).then_inc(eps_done, 1)
                        need(pool, eps_done, t + 1)
                        pool.tensor_tensor(rstd[:, s, :], var_eps[:, s, :], minus_half[:, 0:1], ALU.pow).then_inc(rstd_done, 1)

                    over_tiles(pool, [(ln_rstd, 0)])

                @block.scalar
                def _(act):
                    def stage(t, s):
                        need(act, proj_done, t - 1)
                        act.activation(ot[:, s, :, :], OT[:, t // TB, :, t % TB, :], ACT.Copy).then_inc(staged, 1)

                    over_tiles(act, [(stage, 0)])

                @block.tensor
                def _(pe):
                    pe.wait_ge(loaded_late, 16 * len(late_loads))

                    def project(t, s):
                        need(pe, staged, t + 1)
                        need(pe, res_step, 4 * (t - 2) + 1)
                        for j in range(PAIRS):
                            last = pe.matmul(banks(s)[:, 0:D], ot[:, s, j, :], wo_sb[:, j, :],
                                             start=(j == 0), stop=(j == PAIRS - 1))
                        last.then_inc(proj_done, 1)

                    over_tiles(pe, [(project, 0)])

                @block.vector
                def _(dve):
                    def residual(t, s):
                        need(dve, proj_done, t + 1)
                        dve.tensor_tensor(y[:, s, :], banks(s)[:, 0:D], rows[:, t // TB, ga, :], ALU.mult)\
                            .then_inc(res_step, 1)
                        dve.wait_ge(res_step, 4 * t + 1)
                        dve.tensor_tensor(X[:, t, :], X[:, t, :], y[:, s, :], ALU.add).then_inc(res_step, 1)
                        dve.wait_ge(res_step, 4 * t + 2)
                        dve.bn_stats(bn[:, s, :], X[:, t, :]).then_inc(res_step, 1)
                        dve.wait_ge(res_step, 4 * t + 3)
                        dve.bn_aggr(mv[:, s, :], bn[:, s, :]).then_inc(res_step, 1)

                    def modulate(t, s):
                        need(dve, rstd_done, t + 1)
                        dve.tensor_scalar(xn[:, s, :], X[:, t, :], mv[:, s, 0:1], rstd[:, s, :],
                                          ALU.subtract, ALU.mult).then_inc(mod_step, 1)
                        dve.wait_ge(mod_step, 3 * t + 1)
                        dve.tensor_tensor(xn[:, s, :], xn[:, s, :], rows[:, t // TB, cbr, :], ALU.mult)\
                            .then_inc(mod_step, 1)
                        dve.wait_ge(mod_step, 3 * t + 2)
                        dve.tensor_tensor(XF[:, t, :], xn[:, s, :], rows[:, t // TB, sbr, :], ALU.add)\
                            .then_inc(mod_step, 1)

                    over_tiles(dve, [(residual, 0), (modulate, 1)])
        mid.close()

        fsb = sb_in(whole)
        XA = fsb("XA", [P, T, D])
        XS = fsb("XS", [P, T, D // 2])
        for l in range(DEPTH):
            local_attention_phase(nc, l, psum, X, XF, XA, XS, ident, minus_half, fw_qkv, fw_o, f_qs, f_ks, xpos_d,
                                  mask_d, notfirst_d)
            mlp_phase(nc, l, psum, X, XF, XA, XS, ident, minus_half, fw_1, fw_2, fb_1, f_ln, rows, out)


def local_attention_phase(nc, l, psum, X, XF, XA, XS, ident, minus_half, fw_qkv, fw_o, f_qs, f_ks, xpos_d,
                          mask_d, notfirst_d):
    def banks(a, n=1):
        return psum[:, a:a + n, :].rearrange("p b c -> p (b c)")

    with ExitStack() as ph:
        def sb(name, shape, dt=F32):
            return ph.enter_context(nc.sbuf_tensor(f"{name}_a{l}", shape, dt))

        def sem(name):
            return ph.enter_context(nc.semaphore(f"{name}_a{l}"))

        NH = 2 * FH
        xpos_raw = sb("xpos_raw", [P, TB, 2, 2, HD])
        xpos = sb("xpos", [P, TB, 2, 2, HD])
        scale_row = sb("scale_row", [P, 2, HD])
        mask = sb("mask", [P, TB, 2 * WIN])
        notfirst = sb("notfirst", [P, T])
        xst = sb("xst", [P, 2, D])
        hT = sb("hT", [P, 2, P + 1])
        sq = sb("sq", [P, NH, HD])
        ss = sb("ss", [P, 2, NH])
        rinv = sb("rinv", [P, 2, NH])
        ss_up = sb("ss_up", [P, 2, NH])
        qn = sb("qn", [P, NH, HD])
        t1 = sb("t1", [P, NH, HD])
        t2 = sb("t2", [P, NH, HD])
        qk = sb("qk", [P, 2, NH, HD])
        v = sb("v", [P, 2, INNER])
        vp = sb("vp", [P, 2, INNER])
        qT = sb("qT", [P, 2, FH // 2, P])
        kT = sb("kT", [P, 2, FH // 2, WIN + P])
        S = sb("S", [P, FH, 2 * WIN])
        nmax = sb("nmax", [P, 2, FH])
        E = sb("E", [P, 2, FH, 2 * WIN])
        den = sb("den", [P, 2, FH])
        den_inv = sb("den_inv", [P, 2, FH])
        EN = sb("EN", [P, 2, FH, 2 * WIN])
        ET = sb("ET", [P, FH, P])
        oT = sb("oT", [P, FH // 2, P])

        ld = sem("ld")
        tab_step = sem("tab_step")
        xst_done = sem("xst_done")
        x_turned = sem("x_turned")
        hT_done = sem("hT_done")
        qkv_done = sem("qkv_done")
        sq_done = sem("sq_done")
        v_done = sem("v_done")
        vp_done = sem("vp_done")
        ss_done = sem("ss_done")
        rinv_step = sem("rinv_step")
        up_done = sem("up_done")
        rope_step = sem("rope_step")
        qk_turned = sem("qk_turned")
        qkT_done = sem("qkT_done")
        qk_mm = sem("qk_mm")
        max_done = sem("max_done")
        exp_done = sem("exp_done")
        norm_done = sem("norm_done")
        inv_done = sem("inv_done")
        e_turned = sem("e_turned")
        eT_done = sem("eT_done")
        pv_mm = sem("pv_mm")
        oT_done = sem("oT_done")
        wo_mm = sem("wo_mm")
        xa_done = sem("xa_done")
        sin_done = sem("sin_done")

        ps_qk = banks(0, 2).rearrange("p (h d) -> p h d", d=HD)
        ps_x = banks(7)[:, 0:P]

        with nc.Block() as block:
            @block.sync
            def _(sp):
                xs = xpos_d.rearrange("(t p) s (q d) -> p t s q d", p=P, d=HD)
                for t in range(TB):
                    sp.dma_start(xpos_raw[:, t], xs[:, t]).then_inc(ld, 16)
                sp.dma_start(scale_row[:, 0, :], f_qs[l].partition_broadcast(P)).then_inc(ld, 16)
                sp.dma_start(scale_row[:, 1, :], f_ks[l].partition_broadcast(P)).then_inc(ld, 16)
                sp.dma_start(mask[:, :, :], mask_d).then_inc(ld, 16)
                sp.dma_start(notfirst[:, :], notfirst_d).then_inc(ld, 16)

            @block.gpsimd
            def _(pool):
                def inverse_norms(t, s):
                    need(pool, ss_done, t + 1)
                    need(pool, rope_step, 4 * (t - 2) + 1)
                    pool.tensor_scalar(ss_up[:, s, :], ss[:, s, :], 1e-24, None, ALU.max).then_inc(up_done, 1)
                    need(pool, up_done, t + 1)
                    pool.tensor_tensor(rinv[:, s, :], ss_up[:, s, :], minus_half[:, 0:NH], ALU.pow).then_inc(rinv_step, 1)

                def sin_part(t, s):
                    need(pool, rope_step, 4 * t + 1)
                    need(pool, rope_step, 4 * (t - 1) + 4)
                    sin = xpos[:, t % TB, 1, :, :][:, :, None, :].to_broadcast([P, 2, FH, HD])
                    pool.tensor_tensor(t2[:, :, :].rearrange("p (q h) d -> p q h d", q=2),
                                       qn[:, :, :].rearrange("p (q h) d -> p q h d", q=2), sin, ALU.mult)\
                        .then_inc(sin_done, 1)

                pool.wait_ge(tab_step, 2)
                over_tiles(pool, [(inverse_norms, 0), (sin_part, 0)])

            @block.scalar
            def _(act):
                act.wait_ge(tab_step, 2)
                act.wait_ge(ld, 16 * (TB + 4))

                def take_qkT(t, s):
                    need(act, qk_turned, 2 * t + 1)
                    need(act, qk_mm, t - 1)
                    act.activation(qT[:, s, :, :], banks(3).rearrange("p (j c) -> p j c", c=P), ACT.Copy)\
                        .then_inc(qkT_done, 1)
                    need(act, qkT_done, 3 * t)
                    act.activation(kT[:, s, :, 0:WIN], kT[:, 1 - s, :, P:P + WIN], ACT.Copy).then_inc(qkT_done, 1)
                    need(act, qk_turned, 2 * t + 2)
                    act.activation(kT[:, s, :, WIN:WIN + P], banks(4).rearrange("p (j c) -> p j c", c=P), ACT.Copy)\
                        .then_inc(qkT_done, 1)

                def take_hT(t, s):
                    need(act, hT_done, 3 * t)
                    need(act, qkv_done, t - 1)
                    act.activation(hT[HD:P, s, 0:1], hT[HD:P, 1 - s, P:P + 1], ACT.Copy,
                                   scale=notfirst[HD:P, bass.ds(t, 1)]).then_inc(hT_done, 1)
                    need(act, x_turned, t + 1)
                    act.activation(hT[0:HD, s, 0:P], ps_x[0:HD, :], ACT.Copy).then_inc(hT_done, 1)
                    act.activation(hT[HD:P, s, 1:P + 1], ps_x[HD:P, :], ACT.Copy).then_inc(hT_done, 1)

                def take_qkv(t, s):
                    need(act, qkv_done, t + 1)
                    need(act, ss_done, t)
                    act.activation(sq[:, :, :], ps_qk, ACT.Square).then_inc(sq_done, 1)

                def take_v(t, s):
                    need(act, pv_mm, t - 1)
                    act.activation(v[:, s, :], banks(2), ACT.Copy).then_inc(v_done, 1)
                    need(act, v_done, t + 1)
                    act.activation(vp[0:WIN, s, :], v[WIN:P, 1 - s, :], ACT.Copy).then_inc(vp_done, 1)
                    act.activation(vp[WIN:P, s, :], v[0:WIN, s, :], ACT.Copy).then_inc(vp_done, 1)

                def take_eT(t, s):
                    need(act, pv_mm, t)
                    for n in range(2):
                        need(act, e_turned, 2 * t + n + 1)
                        act.activation(ET[:, 4 * n:4 * n + 4, :], banks(3 + n).rearrange("p (h c) -> p h c", c=P),
                                       ACT.Copy).then_inc(eT_done, 1)

                def take_oT(t, s):
                    need(act, pv_mm, t + 1)
                    need(act, wo_mm, t)
                    act.activation(oT[:, :, :], banks(7).rearrange("p (j c) -> p j c", c=P), ACT.Copy)\
                        .then_inc(oT_done, 1)

                def exponentials(t, s):
                    need(act, max_done, FH * (t + 1))
                    need(act, norm_done, t - 1)
                    for h in range(FH):
                        act.activation(E[:, s, h, :], S[:, h, :], ACT.Exp, bias=nmax[:, s, h:h + 1],
                                       scale=-1.0, accum_out=den[:, s, h:h + 1]).then_inc(exp_done, 1)

                over_tiles(act, [(take_qkT, 1), (take_hT, 0), (take_qkv, 0), (exponentials, 1), (take_eT, 2),
                                 (take_oT, 2), (take_v, 0)])

            @block.vector
            def _(dve):
                dve.memset(kT[:, :, :, :], 0.0)
                dve.memset(v[:, :, :], 0.0)
                dve.memset(hT[:, :, :], 0.0).then_inc(tab_step, 1)
                dve.wait_ge(ld, 16 * (TB + 4))
                dve.tensor_tensor(xpos[:, :, :, :, :].rearrange("p t s q d -> p (t s) (q d)"),
                                  xpos_raw[:, :, :, :, :].rearrange("p t s q d -> p (t s) (q d)"),
                                  scale_row[:, :, :].rearrange("p q d -> p (q d)")[:, None, :]
                                  .to_broadcast([P, 2 * TB, 2 * HD]), ALU.mult).then_inc(tab_step, 1)
                dve.wait_ge(tab_step, 2)

                def stage(t, s):
                    need(dve, x_turned, t - 1)
                    dve.tensor_copy(xst[:, s, :], XF[:, t, :]).then_inc(xst_done, 1)

                def masked_max(t, s):
                    need(dve, qk_mm, t + 1)
                    need(dve, exp_done, FH * t)
                    for h in range(FH):
                        dve.tensor_tensor_reduce(S[:, h, :], banks(5 + h % 2)[:, (h // 2) * P:(h // 2 + 1) * P],
                                                 mask[:, t % TB, :], -1.0, BIG, ALU.add, ALU.min,
                                                 nmax[:, s, h:h + 1]).then_inc(max_done, 1)

                def rotate(t, s):
                    need(dve, sq_done, t + 1)
                    need(dve, rinv_step, t - 1)
                    dve.tensor_reduce(ss[:, s, :], sq[:, :, :], AX_X, ALU.add).then_inc(ss_done, 1)
                    need(dve, rinv_step, t + 1)
                    need(dve, sin_done, t)
                    dve.tensor_tensor(qn[:, :, :], ps_qk, rinv[:, s, :][:, :, None].to_broadcast([P, NH, HD]),
                                      ALU.mult).then_inc(rope_step, 1)
                    dve.wait_ge(rope_step, 4 * t + 1)
                    cos = xpos[:, t % TB, 0, :, :][:, :, None, :].to_broadcast([P, 2, FH, HD])
                    dve.tensor_tensor(t1[:, :, :].rearrange("p (q h) d -> p q h d", q=2),
                                      qn[:, :, :].rearrange("p (q h) d -> p q h d", q=2), cos, ALU.mult)\
                        .then_inc(rope_step, 1)
                    normalise(t - 1, 1 - s)
                    dve.wait_ge(rope_step, 4 * t + 2)
                    need(dve, sin_done, t + 1)
                    need(dve, qk_turned, 2 * (t - 1))
                    m = HD // 2
                    dve.tensor_tensor(qk[:, s, :, 0:m], t1[:, :, 0:m], t2[:, :, m:HD], ALU.add).then_inc(rope_step, 1)
                    dve.tensor_tensor(qk[:, s, :, m:HD], t1[:, :, m:HD], t2[:, :, 0:m], ALU.add).then_inc(rope_step, 1)

                def normalise(t, s):
                    if isinstance(t, int) and t < 0:
                        return
                    need(dve, exp_done, FH * (t + 1))
                    need(dve, e_turned, 2 * (t - 1))
                    dve.reciprocal(den_inv[:, s, :], den[:, s, :]).then_inc(inv_done, 1)
                    need(dve, inv_done, t + 1)
                    dve.tensor_tensor(EN[:, s, :, :], E[:, s, :, :],
                                      den_inv[:, s, :][:, :, None].to_broadcast([P, FH, 2 * WIN]), ALU.mult)\
                        .then_inc(norm_done, 1)

                def last_normalise(t, s):
                    if isinstance(t, int) and t == T - 1:
                        normalise(t, s)

                def residual(t, s):
                    need(dve, wo_mm, t + 1)
                    dve.tensor_tensor(XA[:, t, :], banks(5)[:, 0:D], XF[:, t, :], ALU.add).then_inc(xa_done, 1)

                over_tiles(dve, [(stage, 0), (masked_max, 1), (rotate, 0), (last_normalise, 1), (residual, 2)])

            @block.tensor
            def _(pe):
                def turn_qk(t, s):
                    need(pe, rope_step, 4 * t + 4)
                    for n in range(2):
                        need(pe, eT_done, 2 * (t - 1) + n - 1)
                        for j in range(4):
                            src = qk[:, s, 8 * n + 2 * j:8 * n + 2 * j + 2, :].rearrange("p h d -> p (h d)")
                            last = pe.transpose(banks(3 + n)[:, j * P:(j + 1) * P], src, ident[:, :])
                        last.then_inc(qk_turned, 1)

                def turn_x(t, s):
                    need(pe, xst_done, t + 1)
                    need(pe, oT_done, t - 2)
                    pe.transpose(ps_x, xst[:, s, :], ident[:, :]).then_inc(x_turned, 1)

                def multiply_qk(t, s):
                    need(pe, qkT_done, 3 * (t + 1))
                    need(pe, max_done, FH * t)
                    need(pe, xa_done, t - 1)
                    for h in range(FH):
                        a = HD * (h % 2)
                        for w in range(2):
                            last = pe.matmul(banks(5 + h % 2)[WIN * w:WIN * w + WIN, (h // 2) * P:(h // 2 + 1) * P],
                                             qT[a:a + HD, s, h // 2, WIN * w:WIN * w + WIN],
                                             kT[a:a + HD, s, h // 2, WIN * w:WIN * w + 2 * WIN],
                                             start=True, stop=True)
                    last.then_inc(qk_mm, 1)

                def project(t, s):
                    need(pe, hT_done, 3 * (t + 1))
                    need(pe, rope_step, 4 * (t - 1) + 1)
                    need(pe, v_done, t)
                    for n in range(3):
                        last = pe.matmul(banks(n), hT[:, s, 0:P], fw_qkv[:, l, n * INNER:(n + 1) * INNER],
                                         start=True, stop=True)
                    last.then_inc(qkv_done, 1)

                def turn_e(t, s):
                    need(pe, norm_done, t + 1)
                    for n in range(2):
                        need(pe, qkT_done, 3 * (t + 2) if not isinstance(t, int) else min(3 * (t + 2), 3 * T))
                        for j in range(4):
                            last = pe.transpose(banks(3 + n)[:, j * P:(j + 1) * P], EN[:, s, 4 * n + j, :], ident[:, :])
                        last.then_inc(e_turned, 1)

                def multiply_v(t, s):
                    need(pe, vp_done, 2 * (t + 1))
                    need(pe, hT_done, 3 * (t + 3) if not isinstance(t, int) else min(3 * (t + 3), 3 * T))
                    need(pe, oT_done, t)
                    for h in range(FH):
                        need(pe, eT_done, 2 * t + h // 4 + 1)
                        a = HD * (h % 2)
                        for w in range(2):
                            last = pe.matmul(banks(7)[a:a + HD, (h // 2) * P + WIN * w:(h // 2) * P + WIN * w + WIN],
                                             (v if w else vp)[:, s, h * HD:(h + 1) * HD],
                                             ET[:, h, WIN * w:WIN * w + WIN], start=True, stop=True)
                    last.then_inc(pv_mm, 1)

                def project_out(t, s):
                    need(pe, oT_done, t + 1)
                    need(pe, xa_done, t)
                    need(pe, max_done, FH * (t + 2) if not isinstance(t, int) else min(FH * (t + 2), FH * T))
                    for j in range(FH // 2):
                        last = pe.matmul(banks(5)[:, 0:D], oT[:, j, :], fw_o[:, l, j, :], start=(j == 0),
                                         stop=(j == FH // 2 - 1))
                    last.then_inc(wo_mm, 1)

                pe.wait_ge(tab_step, 2)
                over_tiles(pe, [(turn_qk, 1), (turn_x, 0), (multiply_qk, 1), (project, 0), (turn_e, 2),
                                (multiply_v, 2), (project_out, 2)])


def mlp_phase(nc, l, psum, X, XF, XA, XS, ident, minus_half, fw_1, fw_2, fb_1, f_ln, rows, out):
    def banks(a, n=1):
        return psum[:, a:a + n, :].rearrange("p b c -> p (b c)")

    with ExitStack() as ph:
        def sb(name, shape, dt=F32):
            return ph.enter_context(nc.sbuf_tensor(f"{name}_m{l}", shape, dt))

        def sem(name):
            return ph.enter_context(nc.semaphore(f"{name}_m{l}"))

        bn = sb("bn", [P, 2, 2, 6])
        mv = sb("mv", [P, 2, 2])
        rstd = sb("rstd", [P, 2, 1])
        var_eps = sb("var_eps", [P, 2, 1])
        xn = sb("xn", [P, 2, D])
        hT = sb("hT", [P, 2, P])
        gate = sb("gate", [P, 2, HC, P])
        act_in = sb("act_in", [P, 2, HC, P])
        y = sb("y", [P, 2, D])
        res = sb("res", [P, 2, D])

        zeroed = sem("zeroed")
        shifted = sem("shifted")
        ln_step = sem("ln_step")
        rstd_done = sem("rstd_done")
        eps_done = sem("eps_done")
        xn_done = sem("xn_done")
        x_turned = sem("x_turned")
        hT_done = sem("hT_done")
        w1_mm = sem("w1_mm")
        gelu_done = sem("gelu_done")
        u_done = sem("u_done")
        w2_mm = sem("w2_mm")
        xf_done = sem("xf_done")
        y_done = sem("y_done")
        res_done = sem("res_done")
        res_out = [sem("res_out0"), sem("res_out1")]
        last_layer = l == DEPTH - 1
        width = [P] * (HC - 1) + [HLAST]

        with nc.Block() as block:
            @block.sync
            def _(sp):
                sp.dma_start(XS[1:P, :, :], XA[0:P - 1, :, D // 2:D]).then_inc(shifted, 16)
                for b in range(B):
                    a = b * TB
                    sp.dma_start(XS[0:1, a + 1:a + TB, :], XA[P - 1:P, a:a + TB - 1, D // 2:D]).then_inc(shifted, 16)
                if last_layer:
                    def store(t, s):
                        need(sp, res_done, t + 1)
                        sp.dma_start(out[t // TB, bass.ts(t % TB, P), :], res[:, s, :]).then_inc(res_out[s], 16)

                    over_tiles(sp, [(store, 0)])
                    for s in range(2):
                        sp.wait_ge(res_out[s], 16 * (T // 2))

            @block.gpsimd
            def _(pool):
                def ln_rstd(t, s):
                    need(pool, ln_step, 3 * t + 3)
                    need(pool, xn_done, 2 * (t - 1))
                    pool.tensor_scalar(var_eps[:, s, :], mv[:, s, 1:2], EPS, None, ALU.add).then_inc(eps_done, 1)
                    need(pool, eps_done, t + 1)
                    pool.tensor_tensor(rstd[:, s, :], var_eps[:, s, :], minus_half[:, 0:1], ALU.pow).then_inc(rstd_done, 1)

                over_tiles(pool, [(ln_rstd, 0)])

            @block.scalar
            def _(act):
                def take_hT(t, s):
                    need(act, x_turned, t + 1)
                    need(act, w1_mm, 2 * (t - 1))
                    act.activation(hT[:, s, :], banks(6 + s)[:, 0:P], ACT.Identity, bias=f_ln[:, l, 1:2],
                                   scale=f_ln[:, l, 0:1]).then_inc(hT_done, 1)

                def gelu(t, s):
                    need(act, w1_mm, 2 * t + 1)
                    need(act, u_done, HC * (t - 1))
                    for j, n in enumerate(width):
                        act.activation(gate[0:n, s, j, :], banks(2 * s)[0:n, j * P:(j + 1) * P], ACT.Gelu,
                                       bias=fb_1[0:n, l, 1, j:j + 1]).then_inc(gelu_done, 1)

                over_tiles(act, [(take_hT, 0), (gelu, 0)])

            @block.vector
            def _(dve):
                for b in range(B):
                    dve.memset(XS[0:1, b * TB, :], 0.0).then_inc(zeroed, 1)
                for s in range(2):
                    dve.memset(act_in[:, s, HC - 1, :], 1.0).then_inc(zeroed, 1)
                dve.wait_ge(zeroed, 4)
                dve.wait_ge(shifted, 48)

                def ln_stats(t, s):
                    need(dve, xn_done, 2 * (t - 1))
                    dve.bn_stats(bn[:, s, 0, :], XA[:, t, 0:D // 2]).then_inc(ln_step, 1)
                    dve.bn_stats(bn[:, s, 1, :], XS[:, t, :]).then_inc(ln_step, 1)
                    dve.wait_ge(ln_step, 3 * t + 2)
                    dve.bn_aggr(mv[:, s, :], bn[:, s, :, :].rearrange("p a b -> p (a b)")).then_inc(ln_step, 1)

                def ln_apply(t, s):
                    need(dve, rstd_done, t + 1)
                    need(dve, x_turned, t - 1)
                    for n, src in enumerate((XA[:, t, 0:D // 2], XS[:, t, :])):
                        dve.tensor_scalar(xn[:, s, n * (D // 2):(n + 1) * (D // 2)], src, mv[:, s, 0:1], rstd[:, s, :],
                                          ALU.subtract, ALU.mult).then_inc(xn_done, 1)

                def gated(t, s):
                    need(dve, w1_mm, 2 * t + 2)
                    need(dve, w2_mm, t - 1)
                    for j, n in enumerate(width):
                        need(dve, gelu_done, HC * t + j + 1)
                        dve.scalar_tensor_tensor(act_in[0:n, s, j, :], banks(2 * s + 1)[0:n, j * P:(j + 1) * P],
                                                 fb_1[0:n, l, 0, j:j + 1], gate[0:n, s, j, :], ALU.add, ALU.mult)\
                            .then_inc(u_done, 1)

                def residual(t, s):
                    need(dve, w2_mm, t + 1)
                    dve.tensor_tensor(XF[:, t, :], banks(4 + s)[:, 0:D], XA[:, t, :], ALU.add).then_inc(xf_done, 1)
                    if last_layer:
                        dve.wait_ge(xf_done, t + 1)
                        dve.tensor_tensor(y[:, s, :], XF[:, t, :], rows[:, t // TB, 3, :], ALU.mult).then_inc(y_done, 1)
                        dve.wait_ge(y_done, t + 1)
                        need(dve, res_out[s], 16 * (t // 2))
                        dve.tensor_tensor(res[:, s, :], y[:, s, :], X[:, t, :], ALU.add).then_inc(res_done, 1)

                over_tiles(dve, [(ln_stats, 0), (ln_apply, 1), (gated, 2), (residual, 3)])

            @block.tensor
            def _(pe):
                def turn_x(t, s):
                    need(pe, xn_done, 2 * (t + 1))
                    need(pe, hT_done, t - 1)
                    pe.transpose(banks(6 + s)[:, 0:P], xn[:, s, :], ident[:, :]).then_inc(x_turned, 1)

                def hidden(t, s):
                    need(pe, hT_done, t + 1)
                    for m in range(2):
                        need(pe, u_done if m else gelu_done, HC * (t - 1))
                        off = 0 if m else HID
                        for j, n in enumerate(width):
                            last = pe.matmul(banks(2 * s + m)[0:n, j * P:(j + 1) * P],
                                             fw_1[:, l, off + j * P:off + j * P + n], hT[:, s, :],
                                             start=True, stop=True)
                        last.then_inc(w1_mm, 1)

                def project(t, s):
                    need(pe, u_done, HC * (t + 1))
                    need(pe, (res_done if last_layer else xf_done), t - 1)
                    for j, n in enumerate(width):
                        rows_in = n + (j == HC - 1)
                        last = pe.matmul(banks(4 + s)[:, 0:D], act_in[0:rows_in, s, j, :], fw_2[0:rows_in, l, j, :],
                                         start=(j == 0), stop=(j == HC - 1))
                    last.then_inc(w2_mm, 1)

                over_tiles(pe, [(turn_x, 0), (hidden, 0), (project, 1)])


_INS = ['L0_attn_x', 'L0_attn_Wq', 'L0_attn_Wk', 'L0_attn_Wv', 'L0_attn_Wo', 'L0_ffn_wqkv', 'L0_ffn_q_scale',
        'L0_ffn_k_scale', 'L0_ffn_wo', 'L0_ffn_ln_g', 'L0_ffn_ln_b', 'L0_ffn_w1', 'L0_ffn_b1', 'L0_ffn_w2',
        'L0_ffn_b2', 'L0_c', 'L0_wmod']
_OUTS = [((B, N, D), 'float32')]


def kernel(**inputs):
    import concourse.bacc as bacc
    from concourse.bass_utils import run_bass_kernel_spmd

    nc = bacc.Bacc("TRN2", target_bir_lowering=False, num_devices=1)
    arrays, args = {}, []
    given = {name: np.ascontiguousarray(inputs[name]) for name in _INS} | shape_constants()
    for name, a in given.items():
        arrays[f"in_{name}_dram"] = a
        args.append(nc.dram_tensor(f"in_{name}_dram", a.shape, mybir.dt.from_np(a.dtype), kind="ExternalInput").ap())
    for i, (shape, dtype) in enumerate(_OUTS):
        args.append(nc.dram_tensor(f"out_{i}_dram", shape, mybir.dt.from_np(np.dtype(dtype)),
                                   kind="ExternalOutput").ap())
    adaln_block(nc, *args)
    r = run_bass_kernel_spmd(nc, [arrays], core_ids=[0])
    return r.results[0]["out_0_dram"]
```

```python
import math
from contextlib import ExitStack

import concourse.bass as bass
import numpy as np
from concourse import mybir

F32 = mybir.dt.float32
F32R = mybir.dt.float32r
ALU = mybir.AluOpType
ACT = mybir.ActivationFunctionType
AX_X = mybir.AxisListType.X

P = 128
B, N, D = 2, 1024, 128
TB = N // P
T = B * TB
H, KV, HD = 16, 4, 64
PAIRS = H // 2
GROUP = H // KV
HEADS = B * H
QW, KW = H * HD, KV * HD
DEPTH, FH, WIN = 2, 8, 64
INNER = FH * HD
HID = int(D * 4 * 2 / 3)
HC = -(-HID // P)
HLAST = HID - (HC - 1) * P
EPS = 1e-5
BIG = 3e38
POOL_SUMS = (0, 1, 2, 4, 6)
DVE_SUMS = (3, 5, 7)


def shape_constants():
    f = np.float32
    pos = np.arange(N, dtype=f)
    inv = (f(1.0) / f(10000.0) ** (np.arange(0, HD, 2, dtype=f) / f(HD))).astype(f)
    ang = (pos[:, None] * inv[None, :]).astype(f).astype(np.float64)
    cos, sin = np.cos(ang).astype(f), np.sin(ang).astype(f)
    rope = np.stack([np.concatenate([cos, cos], 1), np.concatenate([sin, -sin], 1)], 1)
    half = np.arange(0, HD, 2, dtype=f)
    base = ((half + f(0.4 * HD)) / f(1.4 * HD)).astype(f)
    power = ((pos - f(N // 2)) / f(WIN // 2)).astype(f)
    scale = np.power(base[None, :].astype(np.float64), power[:, None].astype(np.float64))
    xc, xs = [], []
    for s in (8.0 * scale, 1.0 / scale):
        xc.append(np.concatenate([cos * s, cos * s], 1))
        xs.append(np.concatenate([sin * s, -sin * s], 1))
    xpos = np.stack([np.concatenate(xc, 1), np.concatenate(xs, 1)], 1).astype(f)
    start = 2.0 ** (-2.0 ** (-(math.log2(H) - 3)))
    slopes = np.array([start * start ** i for i in range(H)])
    far = np.arange(N) - (N - 1)
    bias = slopes[None, :, None] * far.reshape(TB, P).T[:, None, :]
    i = (np.arange(P) % WIN)[:, None]
    j = np.arange(2 * WIN)[None, :]
    seen = (j <= i + WIN) & (j >= i)
    mask = np.zeros((P, TB, 2 * WIN), f)
    mask[:] = np.where(seen, 0.0, -1e30)[:, None, :]
    mask[:WIN, 0, :WIN] = -1e30
    first = np.ones((P, T), f)
    first[:, ::TB] = 0.0
    return {
        "ident": np.eye(P, dtype=f),
        "rope": rope.astype(f),
        "xpos": xpos,
        "far": far.astype(f)[None, :],
        "slope": np.tile(slopes.astype(f)[None, :], (P, B)),
        "keybias": np.tile(bias.astype(f), (1, B, 1)),
        "mask": mask,
        "notfirst": first,
    }


def need(eng, sem, count):
    if count > 0:
        eng.wait_ge(sem, count)


def over_tiles(stages, tiles=T):
    for step in range(tiles + max(lag for _, lag in stages)):
        for fn, lag in stages:
            if 0 <= step - lag < tiles:
                fn(step - lag, (step - lag) % 2)


def adaln_block(nc, x, wq, wk, wv, wo, f_wqkv, f_qs, f_ks, f_wo, f_lg, f_lb, f_w1, f_b1, f_w2, f_b2,
                c, wmod, ident_d, rope_d, xpos_d, far_d, slope_d, keybias_d, mask_d, notfirst_d, out):
    qa_d = nc.dram_tensor("qa_scratch", (B, H, P, TB, P), F32, kind="Internal").ap()
    k_d = nc.dram_tensor("k_scratch", (B, KV, P, TB, P), F32, kind="Internal").ap()
    v_d = nc.dram_tensor("v_scratch", (B, KV, P, TB, HD), F32, kind="Internal").ap()
    inv_d = nc.dram_tensor("inverse_scratch", (2, N), F32, kind="Internal").ap()

    with ExitStack() as whole:
        whole.enter_context(nc.allow_non_contiguous_dma(reason="a few columns of biases"))

        def sb_in(ctx):
            return lambda name, shape, dt=F32: ctx.enter_context(nc.sbuf_tensor(name, shape, dt))

        def sem(name):
            early_sems.append(nc.alloc_semaphore(name))
            return early_sems[-1]

        early_sems = []
        sb = sb_in(whole)
        psum = whole.enter_context(nc.psum_tensor("psum", [P, 8, 512], F32))

        def banks(a, n=1):
            return psum[:, a:a + n, :].rearrange("p b c -> p (b c)")

        X = sb("X", [P, T, D])
        XF = sb("XF", [P, T, D])
        ident = sb("ident", [P, P])
        rows = sb("rows", [P, B, 4, D])
        minus_half = sb("minus_half", [P, 2 * FH])
        cols = sb("cols", [P, B, 6])
        ga, sbr, cbr, gbr = range(4)
        wo_sb = sb("wo_sb", [P, PAIRS, D])
        fw_qkv = sb("fw_qkv", [P, DEPTH, 3 * INNER])
        fw_o = sb("fw_o", [P, DEPTH, FH // 2, D])
        fw_1 = sb("fw_1", [P, DEPTH, 2 * HID])
        fw_2 = sb("fw_2", [P, DEPTH, HC, D])
        fb_1 = sb("fb_1", [P, DEPTH, 2, HC])
        f_ln = sb("f_ln", [P, DEPTH, 2])
        loaded_late = sem("loaded_late")
        late_loads = []

        with ExitStack() as ph:
            sb = sb_in(ph)
            w_sb = sb("w_sb", [P, QW + 2 * KW])
            rope = sb("rope_sb", [P, TB, 2, HD])
            wmod_sb = sb("wmod_sb", [P, 6 * D])
            cT = sb("cT", [P, B])
            ec = sb("ec", [P, B])
            silu = sb("silu", [P, B])
            silu_wide = sb("silu_wide", [P, B, P])
            guard = sb("guard", [P, B, 2, 2, D])
            bn = sb("bn", [P, 2, 6])
            mv = sb("mv", [P, 2, 2])
            rstd = sb("rstd", [P, 2, 1])
            var_eps = sb("var_eps", [P, 2, 1])
            xn = sb("xn", [P, 2, D])
            hT = sb("hT", [P, 2, P])
            raw = sb("raw", [P, 2, H + KV, HD])
            t1 = sb("t1", [P, H + KV, HD])
            t2 = sb("t2", [P, 2, H + KV, HD])
            qk = sb("qk", [P, 2, H + KV, HD])
            qs_ = sb("q_split", [P, 2, H, P], F32R)
            ks_ = sb("k_split", [P, 2, KV, P], F32R)
            v_sb = sb("v_sb", [P, 2, KW])
            tT = sb("tT", [P, 2, H + KV, P], F32R)

            ld_x = [sem(f"ld_x{b}") for b in range(B)]
            ld_ident = sem("ld_ident")
            ld_c = sem("ld_c")
            ld_w = sem("ld_w")
            ld_mod = sem("ld_mod")
            ld_rope = sem("ld_rope")
            ec_done = sem("ec_done")
            silu_step = sem("silu_step")
            wide_done = sem("wide_done")
            mod_mm = sem("mod_mm")
            mod_step = sem("mod_step")
            const_step = sem("const_step")
            ln_step = sem("ln_step")
            rstd_done = sem("rstd_done")
            eps_done = sem("eps_done")
            half_set = sem("half_set")
            xn_done = sem("xn_done")
            xT_done = sem("xT_done")
            hT_done = sem("hT_done")
            qkv_done = sem("qkv_done")
            v_copied = sem("v_copied")
            raw_done = sem("raw_done")
            cos_done = sem("cos_done")
            sin_done = sem("sin_done")
            sum_done = sem("sum_done")
            high_done = sem("high_done")
            low_done = sem("low_done")
            tr_done = sem("tr_done")
            tr_copied = sem("tr_copied")
            v_out = [sem("v_out0"), sem("v_out1")]
            t_out = [sem("t_out0"), sem("t_out1")]

            ps_qk = banks(0, 3)[:, 0:QW + KW].rearrange("p (h d) -> p h d", d=HD)
            ps_v = banks(3)[:, 0:KW]
            ps_x = banks(7)[:, 0:P]
            NTR = (H + KV) // 4

            with nc.Block() as block:
                @block.sync
                def _(sp):
                    sp.dma_start(cT[:, :], c.rearrange("b d -> d b")).then_inc(ld_c, 16)
                    sp.dma_start(wmod_sb[:, :], wmod).then_inc(ld_mod, 16)
                    sp.dma_start(X[:, 0:TB, :], x[0].rearrange("(t p) d -> p t d", p=P)).then_inc(ld_x[0], 16)
                    sp.dma_start(ident[:, :], ident_d).then_inc(ld_ident, 16)
                    sp.dma_start(w_sb[:, 0:QW], wq).then_inc(ld_w, 16)
                    sp.dma_start(w_sb[:, QW:QW + KW], wk).then_inc(ld_w, 16)
                    sp.dma_start(w_sb[:, QW + KW:], wv).then_inc(ld_w, 16)
                    sp.dma_start(rope[:, :, :, :], rope_d.rearrange("(t p) s d -> p t s d", p=P)).then_inc(ld_rope, 16)
                    sp.dma_start(X[:, TB:T, :], x[1].rearrange("(t p) d -> p t d", p=P)).then_inc(ld_x[1], 16)

                    def late(dst, src):
                        sp.dma_start(dst, src).then_inc(loaded_late, 16)
                        late_loads.append(1)

                    late(wo_sb[:, :, :], wo.rearrange("(j p) n -> p j n", p=P))
                    late(fw_qkv[:, :, :], f_wqkv.rearrange("l p n -> p l n"))
                    late(fw_o[:, :, :, :], f_wo.rearrange("l (j p) n -> p l j n", p=P))
                    late(fw_1[:, :, :], f_w1.rearrange("l p n -> p l n"))
                    late(f_ln[:, :, 0], f_lg.rearrange("l p -> p l"))
                    late(f_ln[:, :, 1], f_lb.rearrange("l p -> p l"))
                    for l in range(DEPTH):
                        late(fw_2[:, l, 0:HC - 1, :], f_w2[l, 0:(HC - 1) * P, :].rearrange("(j p) n -> p j n", p=P))
                        late(fw_2[0:HLAST, l, HC - 1, :], f_w2[l, (HC - 1) * P:HID, :])
                        late(fw_2[HLAST:HLAST + 1, l, HC - 1, :], f_b2[l:l + 1, :])
                        for s in range(2):
                            b1 = f_b1[l, s * HID:(s + 1) * HID]
                            late(fb_1[:, l, s, 0:HC - 1], b1[0:(HC - 1) * P].rearrange("(j p) -> p j", p=P))
                            late(fb_1[0:HLAST, l, s, HC - 1:HC], b1[(HC - 1) * P:HID].rearrange("(p o) -> p o", o=1))

                    def store_v(t, s):
                        need(sp, v_copied, t + 1)
                        sp.dma_start(v_d[t // TB, :, :, t % TB, :].rearrange("g p d -> p g d"),
                                     v_sb[:, s, :].rearrange("p (g d) -> p g d", d=HD)).then_inc(v_out[s], 16)
                    def store_qk(t, s):
                        for a in range(0, H, H // 2):
                            need(sp, tr_copied, NTR * t + (a + H // 2) // 4)
                            sp.dma_start(qa_d[t // TB, a:a + H // 2, :, t % TB, :].rearrange("h p c -> p h c"),
                                         tT[:, s, a:a + H // 2, :].bitcast(F32)).then_inc(t_out[s], 16)
                        need(sp, tr_copied, NTR * (t + 1))
                        sp.dma_start(k_d[t // TB, :, :, t % TB, :].rearrange("h p c -> p h c"),
                                     tT[:, s, H:, :].bitcast(F32)).then_inc(t_out[s], 16)

                    over_tiles([(store_qk, 3), (store_v, 0)])
                    for s in range(2):
                        sp.wait_ge(v_out[s], 16 * (T // 2))
                        sp.wait_ge(t_out[s], 48 * (T // 2))

                @block.gpsimd
                def _(pool):
                    def ln_rstd(t, s):
                        need(pool, ln_step, 2 * t + 2)
                        need(pool, xn_done, t - 1)
                        pool.tensor_scalar(var_eps[:, s, :], mv[:, s, 1:2], EPS, None, ALU.add).then_inc(eps_done, 1)
                        need(pool, eps_done, t + 1)
                        pool.tensor_tensor(rstd[:, s, :], var_eps[:, s, :], minus_half[:, 0:1], ALU.pow).then_inc(rstd_done, 1)

                    def sin_part(t, s):
                        pool.wait_ge(ld_rope, 16)
                        need(pool, raw_done, t + 1)
                        need(pool, sum_done, 2 * (t - 1))
                        sin = rope[:, t % TB, 1, :][:, None, :].to_broadcast([P, H + KV, HD])
                        pool.tensor_tensor(t2[:, s], raw[:, s], sin, ALU.mult).then_inc(sin_done, 1)

                    pool.memset(minus_half[:, :], -0.5).then_inc(half_set, 1)
                    pool.wait_ge(half_set, 1)
                    over_tiles([(ln_rstd, 0), (sin_part, 2)])

                @block.scalar
                def _(act):
                    act.wait_ge(ld_c, 16)
                    act.activation(ec[:, :], cT[:, :], ACT.Exp, scale=-1.0).then_inc(ec_done, 1)

                    def modulate(t, s):
                        need(act, xT_done, t + 1)
                        if isinstance(t, int) and t == 0:
                            act.wait_ge(mod_step, 2)
                        need(act, qkv_done, t - 1)
                        act.activation(hT[:, s, :], ps_x, ACT.Identity, bias=cols[:, t // TB, 0:1],
                                       scale=cols[:, t // TB, 1:2]).then_inc(hT_done, 1)

                    def take_v(t, s):
                        need(act, qkv_done, t + 1)
                        need(act, v_out[s], 16 * (t // 2))
                        act.activation(v_sb[:, s, :], ps_v, ACT.Copy).then_inc(v_copied, 1)

                    def take_raw(t, s):
                        need(act, qkv_done, t + 1)
                        need(act, cos_done, t - 1)
                        need(act, sin_done, t - 1)
                        act.activation(raw[:, s], ps_qk, ACT.Copy).then_inc(raw_done, 1)

                    def take_transposed(t, s):
                        need(act, t_out[s], 48 * (t // 2))
                        for g in range(NTR):
                            need(act, tr_done, NTR * t + g + 1)
                            act.activation(tT[:, s, 4 * g:4 * g + 4, :].rearrange("p h c -> p (h c)"),
                                           banks(4 + (NTR * t + g) % 3), ACT.Copy).then_inc(tr_copied, 1)

                    def high_parts(t, s):
                        need(act, sum_done, 2 * t + 2)
                        need(act, tr_done, NTR * (t - 1))
                        act.activation(qs_[:, s, :, 0:HD], qk[:, s, 0:H, :], ACT.Copy, scale=HD ** -0.5)\
                            .then_inc(high_done, 1)
                        act.activation(ks_[:, s, :, 0:HD], qk[:, s, H:, :], ACT.Copy).then_inc(high_done, 1)

                    over_tiles([(high_parts, 4), (take_raw, 2), (take_v, 2), (modulate, 1), (take_transposed, 5)])

                @block.vector
                def _(dve):
                    dve.wait_ge(ec_done, 1)
                    dve.tensor_scalar(ec[:, :], ec[:, :], 1.0, None, ALU.add).then_inc(silu_step, 1)
                    dve.wait_ge(silu_step, 1)
                    dve.wait_ge(ld_c, 16)
                    dve.reciprocal(ec[:, :], ec[:, :]).then_inc(silu_step, 1)
                    dve.wait_ge(silu_step, 2)
                    dve.tensor_tensor(silu[:, :], cT[:, :], ec[:, :], ALU.mult).then_inc(silu_step, 1)
                    dve.wait_ge(silu_step, 3)
                    for b in range(B):
                        dve.tensor_copy(silu_wide[:, b, :], silu[:, b:b + 1].to_broadcast([P, P])).then_inc(wide_done, 1)
                    dve.wait_ge(mod_mm, 1)
                    mod_ps = banks(7)[:, 0:6 * B].rearrange("p (m b) -> p m b", b=B)
                    dve.tensor_copy(cols[:, :, 0], mod_ps[:, 0, :]).then_inc(mod_step, 1)
                    dve.tensor_scalar(cols[:, :, 1], mod_ps[:, 1, :], 1.0, None, ALU.add).then_inc(mod_step, 1)

                    def make_rows(b, s):
                        dve.wait_ge(mod_mm, 2 + b)
                        ps = banks(4 + b).rearrange("p (m d) -> p m d", d=D)
                        gates = ps[:, 0:4:3, :]
                        dve.tensor_scalar(guard[:, b, 0, :, :], gates, 0.0, 2.0, ALU.is_ge, ALU.mult)\
                            .then_inc(const_step, 1)
                        dve.tensor_scalar(guard[:, b, 1, :, :], gates, 0.25, None, ALU.max).then_inc(const_step, 1)
                        dve.wait_ge(const_step, 2 + 3 * b)
                        dve.scalar_tensor_tensor(guard[:, b, 1, :, :], gates, -1.0, guard[:, b, 1, :, :],
                                                 ALU.mult, ALU.max).then_inc(const_step, 1)
                        dve.wait_ge(const_step, 3 + 3 * b)
                        dve.scalar_tensor_tensor(rows[:, b, 0:4:3, :], guard[:, b, 0, :, :], -1.0,
                                                 guard[:, b, 1, :, :], ALU.add, ALU.mult).then_inc(mod_step, 1)
                        dve.tensor_copy(rows[:, b, 1, :], ps[:, 1, :]).then_inc(mod_step, 1)
                        dve.tensor_scalar(rows[:, b, 2, :], ps[:, 2, :], 1.0, None, ALU.add).then_inc(mod_step, 1)

                    def first_rows(t, s):
                        if t < B:
                            make_rows(t, s)

                    def ln_stats(t, s):
                        dve.wait_ge(ld_x[t // TB], 16)
                        need(dve, xn_done, t - 1)
                        dve.bn_stats(bn[:, s, :], X[:, t, :]).then_inc(ln_step, 1)
                        dve.wait_ge(ln_step, 2 * t + 1)
                        dve.bn_aggr(mv[:, s, :], bn[:, s, :]).then_inc(ln_step, 1)

                    def ln_apply(t, s):
                        need(dve, rstd_done, t + 1)
                        need(dve, xT_done, t - 1)
                        dve.tensor_scalar(xn[:, s, :], X[:, t, :], mv[:, s, 0:1], rstd[:, s, :],
                                          ALU.subtract, ALU.mult).then_inc(xn_done, 1)

                    def cos_part(t, s):
                        dve.wait_ge(ld_rope, 16)
                        need(dve, raw_done, t + 1)
                        need(dve, sum_done, 2 * t)
                        cos = rope[:, t % TB, 0, :][:, None, :].to_broadcast([P, H + KV, HD])
                        dve.tensor_tensor(t1[:, :, :], raw[:, s], cos, ALU.mult).then_inc(cos_done, 1)

                    def rotated(t, s):
                        need(dve, cos_done, t + 1)
                        need(dve, sin_done, t + 1)
                        need(dve, high_done, 2 * (t - 1))
                        need(dve, low_done, 2 * (t - 1))
                        m = HD // 2
                        dve.tensor_tensor(qk[:, s, :, 0:m], t1[:, :, 0:m], t2[:, s, :, m:HD], ALU.add)\
                            .then_inc(sum_done, 1)
                        dve.tensor_tensor(qk[:, s, :, m:HD], t1[:, :, m:HD], t2[:, s, :, 0:m], ALU.add)\
                            .then_inc(sum_done, 1)

                    def low_parts(t, s):
                        need(dve, high_done, 2 * t + 2)
                        need(dve, tr_done, NTR * (t - 1))
                        dve.scalar_tensor_tensor(qs_[:, s, :, HD:P], qk[:, s, 0:H, :], HD ** -0.5,
                                                 qs_[:, s, :, 0:HD].bitcast(F32), ALU.mult, ALU.subtract)\
                            .then_inc(low_done, 1)
                        dve.tensor_tensor(ks_[:, s, :, HD:P], qk[:, s, H:, :],
                                          ks_[:, s, :, 0:HD].bitcast(F32), ALU.subtract).then_inc(low_done, 1)

                    over_tiles([(ln_apply, 1), (low_parts, 5), (rotated, 3), (ln_stats, 0), (first_rows, 1),
                                (cos_part, 2)])

                @block.tensor
                def _(pe):
                    pe.wait_ge(ld_mod, 16)
                    pe.wait_ge(silu_step, 3)
                    for m in range(6):
                        last = pe.matmul(banks(7)[:, B * m:B * m + B], wmod_sb[:, m * D:(m + 1) * D],
                                         silu[:, :], start=True, stop=True)
                    last.then_inc(mod_mm, 1)
                    pe.wait_ge(wide_done, B)
                    for b in range(B):
                        pe.matmul(banks(4 + b), silu_wide[:, b, :], wmod_sb[:, 2 * D:6 * D], start=True, stop=True)\
                            .then_inc(mod_mm, 1)
                    pe.wait_ge(ld_ident, 16)
                    pe.wait_ge(mod_step, 2)

                    def x_transposed(t, s):
                        need(pe, xn_done, t + 1)
                        need(pe, hT_done, t)
                        pe.transpose(ps_x, xn[:, s, :], ident[:, :]).then_inc(xT_done, 1)

                    def project(t, s):
                        pe.wait_ge(ld_w, 48)
                        need(pe, hT_done, t + 1)
                        need(pe, raw_done, t)
                        need(pe, v_copied, t)
                        for n in range(2):
                            pe.matmul(banks(n), hT[:, s, :], w_sb[:, n * 512:(n + 1) * 512], start=True, stop=True)
                        pe.matmul(banks(2)[:, 0:KW], hT[:, s, :], w_sb[:, QW:QW + KW], start=True, stop=True)
                        pe.matmul(ps_v, hT[:, s, :], w_sb[:, QW + KW:], start=True, stop=True).then_inc(qkv_done, 1)

                    def split_transposed(t, s):
                        pe.wait_ge(mod_step, 2 + 3 * B)
                        need(pe, low_done, 2 * t + 2)
                        for g in range(NTR):
                            need(pe, tr_copied, NTR * t + g - 2)
                            for j in range(4):
                                h = 4 * g + j
                                src = qs_[:, s, h, :] if h < H else ks_[:, s, h - H, :]
                                last = pe.transpose(banks(4 + (NTR * t + g) % 3)[:, j * P:(j + 1) * P], src.bitcast(F32),
                                                    ident[:, :])
                            last.then_inc(tr_done, 1)

                    over_tiles([(project, 2), (x_transposed, 1), (split_transposed, 5)])

        fsb = sb_in(whole)
        xpos = fsb("xpos_sb", [P, DEPTH, TB, 2, 2, HD])
        mask = fsb("mask_sb", [P, 2, 2 * WIN])
        mid = ExitStack()
        OT = sb_in(mid)("OT", [P, B, PAIRS, TB, P])
        DQ = N // 4
        with ExitStack() as ph:
            sb = sb_in(ph)
            QA = sb("QA", [P, 4, N], F32R)
            QB = sb("QB", [P, 2, N], F32R)
            KA = sb("KA", [P, 2, N], F32R)
            KB = sb("KB", [P, 2, N], F32R)
            V = sb("V", [P, 2, TB, HD])
            far = sb("far_sb", [P, N])
            slope = sb("slope_sb", [P, HEADS])
            keybias = sb("keybias_sb", [P, HEADS, TB])
            alibi = sb("alibi", [P, 2, N])
            junk = sb("junk", [P, N], mybir.dt.bfloat16)
            M = sb("M", [P, 2, TB])
            mrow = sb("mrow", [TB, 2, P], F32R)
            E = sb("E", [P, 4, N])
            sum_p, sum_d = (xpos[:, n].rearrange("p t s q d -> p (t s q d)").rearrange("p (s n) -> p s n", n=N)
                            for n in range(2))
            den_sb = XF[:, 2:2 + DQ // P, :].rearrange("p t d -> p (t d)")
            den_inv = XF[:, 0:DQ // P, :].rearrange("p t d -> p (t d)")
            inv_wide = XF[:, 4:8, :].rearrange("p t d -> p (t d)")
            ones = sb("ones_m", [P, 32])

            ld_const = sem("ld_const")
            ld_qa = [sem(f"ld_qa{s}") for s in range(4)]
            ld_qb = [sem(f"ld_qb{s}") for s in range(2)]
            ld_m = [sem(f"ld_m{s}") for s in range(2)]
            ld_kv = [sem(f"ld_kv{s}") for s in range(2)]
            qb_zeroed = sem("qb_zeroed")
            alibi_done = sem("alibi_done")
            max_mm = sem("max_mm")
            max_done = sem("max_done")
            m_turned = sem("m_turned")
            mrow_done = sem("mrow_done")
            qk_done = sem("qk_done")
            exp_done = sem("exp_done")
            pv_done = sem("pv_done")
            sum_p_done = sem("sum_p_done")
            sum_d_done = sem("sum_d_done")
            den_mm = sem("den_mm")
            den_taken = sem("den_taken")
            inv_out = sem("inv_out")
            inv_in = sem("inv_in")
            inv_done = sem("inv_done")
            o_done = sem("o_done")
            NP, ND = len(POOL_SUMS) - 1, len(DVE_SUMS) - 1

            def scores(s):
                return banks(2 * s, 2)

            def max_bank(i, k):
                return 4 if i >= 2 else 2 * ((TB * i + k) % 3)

            with nc.Block() as block:
                @block.sync
                def _(sp):
                    def load_qa(i, s):
                        sp.dma_start(QA[:, s, :].bitcast(F32).rearrange("p (t c) -> p t c", c=P), qa_d[i // H, i % H])\
                            .then_inc(ld_qa[s], 16)

                    def load_qb(i, s):
                        sp.dma_start(QB[0:HD, s, :].bitcast(F32).rearrange("p (t c) -> p t c", c=P), qa_d[i // H, i % H, 0:HD])\
                            .then_inc(ld_qb[s], 16)

                    def load_m(i, s):
                        need(sp, mrow_done, i + 1)
                        sp.dma_start(QB[HD:HD + 1, s, :].bitcast(F32).rearrange("p (t c) -> p t c", c=P),
                                     mrow[:, s, :].bitcast(F32)).then_inc(ld_m[s], 16)

                    def load_kv(g, s):
                        high, low = k_d[g // KV, g % KV, 0:HD], k_d[g // KV, g % KV, HD:P]
                        for dst, src in ((KA[0:HD], high), (KA[HD:P], high), (KB[0:HD], low)):
                            sp.dma_start(dst[:, s, :].bitcast(F32).rearrange("p (t c) -> p t c", c=P), src)\
                                .then_inc(ld_kv[s], 16)
                        sp.dma_start(V[:, s, :, :], v_d[g // KV, g % KV]).then_inc(ld_kv[s], 16)

                    def spread_inverse(i, s):
                        need(sp, inv_done, i + 1)
                        sp.dma_start(inv_d[s].rearrange("(c n) -> c n", n=DQ), den_inv[0:P:32, :]).then_inc(inv_out, 16)
                        need(sp, inv_out, 16 * (i + 1))
                        need(sp, o_done, 2 * i)
                        for ch in range(2):
                            sp.dma_start(inv_wide[HD * ch:HD * ch + HD, :],
                                         inv_d[s, ch * 512:(ch + 1) * 512].partition_broadcast(HD)).then_inc(inv_in, 16)

                    load_kv(0, 0)
                    load_qa(0, 0)
                    sp.dma_start(far[:, :], far_d[0].partition_broadcast(P)).then_inc(ld_const, 16)
                    sp.dma_start(slope[:, :], slope_d).then_inc(ld_const, 16)
                    sp.dma_start(keybias[:, :, :], keybias_d).then_inc(ld_const, 16)
                    load_qa(1, 1)
                    load_qa(2, 2)
                    sp.wait_ge(qb_zeroed, 6)
                    load_qb(0, 0)
                    load_m(0, 0)

                    def head(i, u):
                        fixed = isinstance(i, int)
                        need(sp, qk_done, TB * i)
                        if u % GROUP == 0 and not (fixed and i // GROUP + 1 >= HEADS // GROUP):
                            need(sp, pv_done, TB * i)
                            load_kv(i // GROUP + 1, (u // GROUP + 1) % 2)
                        if not (fixed and i + 3 >= HEADS):
                            load_qa(i + 3, (u + 3) % 4)
                        if not (fixed and i + 1 >= HEADS):
                            load_qb(i + 1, (u + 1) % 2)
                            load_m(i + 1, (u + 1) % 2)
                        if i > 0:
                            spread_inverse(i - 1, (i - 1) % 2)

                    for i in range(HEADS):
                        head(i, i % 8)
                    spread_inverse(HEADS - 1, (HEADS - 1) % 2)

                @block.gpsimd
                def _(pool):
                    def head(i, u):
                        s = u % 2
                        need(pool, den_mm, i - 1)
                        for n, k in enumerate(POOL_SUMS[1:]):
                            need(pool, exp_done, TB * i + k + 1)
                            need(pool, sum_p_done, NP * i + n)
                            first = E[:, POOL_SUMS[0], :] if n == 0 else sum_p[:, s, :]
                            pool.tensor_tensor(sum_p[:, s, :], first, E[:, k % 4, :], ALU.add)\
                                .then_inc(sum_p_done, 1)

                    for i in range(HEADS):
                        head(i, i % 8)

                @block.scalar
                def _(act):
                    act.wait_ge(ld_const, 48)

                    def alibi_row(i, s):
                        need(act, max_done, TB * (i - 1))
                        act.activation(alibi[:, s, :], far[:, :], ACT.Identity,
                                       scale=slope[:, bass.ds(i, 1)])\
                            .then_inc(alibi_done, 1)

                    def take_denominators(i):
                        need(act, den_mm, i + 1)
                        need(act, inv_done, i)
                        act.activation(den_sb[:, :], banks(4)[:, 0:DQ], ACT.Copy).then_inc(den_taken, 1)

                    def take_m(i, s):
                        need(act, m_turned, i + 1)
                        need(act, ld_m[s], 16 * (i // 2))
                        act.activation(mrow[:, s, :], banks(5)[0:TB, 0:P], ACT.Copy).then_inc(mrow_done, 1)

                    def head(i, u):
                        fixed = isinstance(i, int)
                        for k in range(TB):
                            if k == 3 and i > 0:
                                take_denominators(i - 1)
                            if k == 3 and i + 1 < HEADS:
                                take_m(i + 1, (u + 1) % 2)
                            need(act, qk_done, TB * i + k + 1)
                            need(act, pv_done, TB * i + k - 3)
                            j, old = (i, k - 4) if k >= 4 else (i - 1, k + 4)
                            if old in POOL_SUMS:
                                need(act, sum_p_done, NP * j + max(1, POOL_SUMS.index(old)))
                            else:
                                need(act, sum_d_done, ND * j + max(1, DVE_SUMS.index(old)))
                            kb = keybias[:, i, k:k + 1]
                            act.activation(E[:, k % 4, :], scores(k % 2), ACT.Exp, bias=kb).then_inc(exp_done, 1)
                            if k == 5 and i + 3 < HEADS:
                                alibi_row(i + 3, (u + 3) % 2)

                    alibi_row(0, 0)
                    alibi_row(1, 1)
                    alibi_row(2, 0)
                    take_m(0, 0)
                    for i in range(HEADS):
                        head(i, i % 8)
                    take_denominators(HEADS - 1)

                @block.vector
                def _(dve):
                    dve.memset(ones[:, :], 1.0).then_inc(qb_zeroed, 1)
                    dve.memset(junk[:, :], 0.0).then_inc(qb_zeroed, 1)
                    dve.wait_ge(qb_zeroed, 2)
                    for s in range(2):
                        dve.tensor_copy(QB[HD:P, s, :], junk[HD:P, :]).then_inc(qb_zeroed, 1)
                        dve.tensor_scalar(KB[HD:P, s, :], junk[HD:P, :], 1.0, None, ALU.add).then_inc(qb_zeroed, 1)

                    def max_step(i, s, k):
                        need(dve, max_mm, TB * i + k + 1)
                        if k == 0:
                            need(dve, alibi_done, i + 1)
                            need(dve, m_turned, i - 1)
                        need(dve, max_done, TB * i + k)
                        dve.tensor_tensor_reduce(junk[:, :], banks(max_bank(i, k), 2), alibi[:, s, :], -1.0, BIG, ALU.add, ALU.min,
                                                 M[:, s, k:k + 1]).then_inc(max_done, 1)

                    def sum_step(i, s, n):
                        k = DVE_SUMS[n + 1]
                        need(dve, exp_done, TB * i + k + 1)
                        need(dve, sum_d_done, ND * i + n)
                        if n == 0:
                            need(dve, den_mm, i - 1)
                        first = E[:, DVE_SUMS[0] % 4, :] if n == 0 else sum_d[:, s, :]
                        dve.tensor_tensor(sum_d[:, s, :], first, E[:, k % 4, :], ALU.add).then_inc(sum_d_done, 1)

                    def invert(i):
                        need(dve, den_taken, i + 1)
                        need(dve, inv_out, 16 * i)
                        dve.reciprocal(den_inv[:, :], den_sb[:, :]).then_inc(inv_done, 1)

                    def divide(i, u):
                        need(dve, inv_in, 32 * (i + 1))
                        need(dve, pv_done, TB * (i + 1))
                        for ch in range(2):
                            a, r = HD * ch, HD * (u % 2)
                            dst = OT[r:r + HD, i // H, (i % H) // 2, 4 * ch:4 * ch + 4, :].rearrange("p t c -> p (t c)")
                            dve.tensor_tensor(dst, banks(6 + u % 2)[a:a + HD, :], inv_wide[a:a + HD, :], ALU.mult)\
                                .then_inc(o_done, 1)

                    def head(i, u):
                        fixed = isinstance(i, int)
                        for k in range(TB):
                            if not (fixed and i + 2 >= HEADS):
                                max_step(i + 2, u % 2, k)
                            if k == 0 and not (fixed and i == 0):
                                sum_step(i - 1, (u - 1) % 2, 1)
                            if k == 3 and i > 0:
                                invert(i - 1)
                            if k == 7 and i > 0:
                                divide(i - 1, (u - 1) % 8)
                            if k == 5:
                                sum_step(i, u % 2, 0)

                    for i in range(2):
                        for k in range(TB):
                            max_step(i, i, k)
                    for i in range(HEADS):
                        head(i, i % 8)
                    sum_step(HEADS - 1, (HEADS - 1) % 2, 1)
                    invert(HEADS - 1)
                    divide(HEADS - 1, (HEADS - 1) % 8)

                @block.tensor
                def _(pe):
                    pe.wait_ge(qb_zeroed, 6)

                    def max_step(i, u, k):
                        s, g = u % 4, (u // GROUP) % 2
                        if k == 0:
                            need(pe, ld_qa[s], 16 * (i // 4 + 1))
                            if u % GROUP == 0:
                                need(pe, ld_kv[g], 64 * (i // 8 + 1))
                            need(pe, mrow_done, 1 if not isinstance(i, int) or i >= 2 else 0)
                        need(pe, max_done, TB * i + k - (2 if i < 2 else 0))
                        if k == 3:
                            if not isinstance(i, int) or i >= 3:
                                need(pe, den_taken, i - 2)
                            if not isinstance(i, int) or i >= 2:
                                need(pe, mrow_done, i)
                        for ch in range(2):
                            last = pe.matmul(banks(max_bank(i, k) + ch), QA[:, s, k * P:(k + 1) * P],
                                             KA[:, g, ch * 512:(ch + 1) * 512], start=True, stop=True)
                        last.then_inc(max_mm, 1)

                    def turn_m(i, s):
                        need(pe, max_done, TB * (i + 1))
                        pe.transpose(banks(5)[0:TB, 0:P], M[:, s, :], ident[:, :]).then_inc(m_turned, 1)

                    def qk_step(i, u, k):
                        g = (u // GROUP) % 2
                        if k == 0:
                            need(pe, ld_qb[u % 2], 16 * (i // 2 + 1))
                            need(pe, ld_m[u % 2], 16 * (i // 2 + 1))
                        need(pe, exp_done, TB * i + k - 1)
                        for ch in range(2):
                            pe.matmul(scores(k % 2)[:, ch * 512:(ch + 1) * 512], KA[:, g, k * P:(k + 1) * P],
                                      QA[:, u % 4, ch * 512:(ch + 1) * 512], start=True, stop=False)
                        for ch in range(2):
                            last = pe.matmul(scores(k % 2)[:, ch * 512:(ch + 1) * 512], KB[:, g, k * P:(k + 1) * P],
                                             QB[:, u % 2, ch * 512:(ch + 1) * 512], start=False, stop=True)
                        last.then_inc(qk_done, 1)

                    def pv_step(i, u, k):
                        g = (u // GROUP) % 2
                        need(pe, exp_done, TB * i + k + 1)
                        if k == 0:
                            need(pe, o_done, 2 * (i - 1))
                        for ch in range(2):
                            last = pe.matmul(banks(6 + u % 2)[HD * ch:HD * ch + HD, :], V[:, g, k, :],
                                             E[:, k % 4, ch * 512:(ch + 1) * 512], start=(k == 0), stop=(k == TB - 1))
                        last.then_inc(pv_done, 1)

                    def denominators(i, s):
                        need(pe, sum_p_done, NP * (i + 1))
                        need(pe, sum_d_done, ND * (i + 1))
                        for n, part in enumerate((sum_p, sum_d)):
                            for c in range(4):
                                last = pe.matmul(banks(4)[32 * c:32 * c + 32, 0:DQ], ones[:, :],
                                                 part[:, s, c * DQ:(c + 1) * DQ], start=(n == 0), stop=(n == 1))
                        last.then_inc(den_mm, 1)

                    def head(i, u):
                        fixed = isinstance(i, int)
                        for k in range(TB):
                            qk_step(i, u, k)
                            if k == 3:
                                if fixed and i + 2 >= HEADS:
                                    need(pe, mrow_done, i + 1)
                                    need(pe, den_taken, i - 1)
                                need(pe, max_done, min(TB * (i + 2) + 3, TB * HEADS) if fixed else TB * (i + 2) + 3)
                                if not (fixed and i == 0):
                                    denominators(i - 1, (u - 1) % 2)
                                if not (fixed and i + 1 >= HEADS):
                                    turn_m(i + 1, (u + 1) % 2)
                            if k > 0:
                                pv_step(i, u, k - 1)
                            elif not (fixed and i == 0):
                                pv_step(i - 1, (u - 1) % 8, TB - 1)
                            if not (fixed and i + 2 >= HEADS):
                                max_step(i + 2, (u + 2) % 8, k)

                    for i in range(2):
                        for k in range(TB):
                            max_step(i, i, k)
                    need(pe, max_done, 2 * TB)
                    turn_m(0, 0)
                    for i in range(HEADS):
                        head(i, i % 8)
                    pv_step(HEADS - 1, (HEADS - 1) % 8, TB - 1)
                    pe.wait_ge(den_taken, HEADS - 1)
                    denominators(HEADS - 1, (HEADS - 1) % 2)

        with ExitStack() as ph:
            sb = sb_in(ph)
            scale_row = sb("scale_row", [P, DEPTH, 2, HD])
            y = sb("y", [P, 2, D])
            bn = sb("bn_o", [P, 2, 6])
            mv = sb("mv_o", [P, 2, 2])
            rstd = sb("rstd_o", [P, 2, 1])
            var_eps = sb("var_eps_o", [P, 2, 1])
            xn = sb("xn_o", [P, 2, D])
            def osem(name):
                return ph.enter_context(nc.semaphore(name))

            proj_done = osem("proj_done")
            ld_tab = osem("ld_tab")
            LD_TAB = 16 * (DEPTH * (TB + 2) + 1)
            res_step = osem("res_step")
            rstd_done = osem("rstd_done_o")
            eps_done = osem("eps_done_o")
            mod_step = osem("mod_step_o")

            early_sems.remove(loaded_late)
            nc.clear_and_free_semaphores(early_sems)

            with nc.Block() as block:
                @block.sync
                def _(sp):
                    xs = xpos_d.rearrange("(t p) s (q d) -> p t s q d", p=P, d=HD)
                    for l in range(DEPTH):
                        sp.dma_start(scale_row[:, l, 0, :], f_qs[l].partition_broadcast(P)).then_inc(ld_tab, 16)
                        sp.dma_start(scale_row[:, l, 1, :], f_ks[l].partition_broadcast(P)).then_inc(ld_tab, 16)
                        for t in range(TB):
                            sp.dma_start(xpos[:, l, t], xs[:, t]).then_inc(ld_tab, 16)
                    sp.dma_start(mask[:, :, :], mask_d[:, 0:2, :]).then_inc(ld_tab, 16)
                    sp.wait_ge(ld_tab, LD_TAB)

                @block.gpsimd
                def _(pool):
                    def scale_tables(l):
                        if l == 0:
                            pool.wait_ge(ld_tab, LD_TAB)
                        tables = xpos[:, l].rearrange("p t s q d -> p (t s) (q d)")
                        pool.tensor_tensor(tables, tables, scale_row[:, l].rearrange("p q d -> p (q d)")[:, None, :]
                                           .to_broadcast([P, 2 * TB, 2 * HD]), ALU.mult)

                    def tables(t, s):
                        if t in (TB, TB + 4):
                            scale_tables((t - TB) // 4)

                    def ln_rstd(t, s):
                        need(pool, res_step, 4 * t + 4)
                        need(pool, mod_step, 3 * (t - 1))
                        pool.tensor_scalar(var_eps[:, s, :], mv[:, s, 1:2], EPS, None, ALU.add).then_inc(eps_done, 1)
                        need(pool, eps_done, t + 1)
                        pool.tensor_tensor(rstd[:, s, :], var_eps[:, s, :], minus_half[:, 0:1], ALU.pow).then_inc(rstd_done, 1)

                    over_tiles([(ln_rstd, 0), (tables, 0)])

                @block.tensor
                def _(pe):
                    pe.wait_ge(loaded_late, 16 * len(late_loads))

                    def project(t, s):
                        need(pe, res_step, 4 * (t - 2) + 1)
                        for j in range(PAIRS):
                            last = pe.matmul(banks(s)[:, 0:D], OT[:, t // TB, j, t % TB, :], wo_sb[:, j, :],
                                             start=(j == 0), stop=(j == PAIRS - 1))
                        last.then_inc(proj_done, 1)

                    over_tiles([(project, 0)])

                @block.vector
                def _(dve):
                    def residual(t, s):
                        need(dve, proj_done, t + 1)
                        dve.tensor_tensor(y[:, s, :], banks(s)[:, 0:D], rows[:, t // TB, ga, :], ALU.mult)\
                            .then_inc(res_step, 1)
                        dve.wait_ge(res_step, 4 * t + 1)
                        dve.tensor_tensor(X[:, t, :], X[:, t, :], y[:, s, :], ALU.add).then_inc(res_step, 1)
                        dve.wait_ge(res_step, 4 * t + 2)
                        dve.bn_stats(bn[:, s, :], X[:, t, :]).then_inc(res_step, 1)
                        dve.wait_ge(res_step, 4 * t + 3)
                        dve.bn_aggr(mv[:, s, :], bn[:, s, :]).then_inc(res_step, 1)

                    def modulate(t, s):
                        need(dve, rstd_done, t + 1)
                        dve.tensor_scalar(xn[:, s, :], X[:, t, :], mv[:, s, 0:1], rstd[:, s, :],
                                          ALU.subtract, ALU.mult).then_inc(mod_step, 1)
                        dve.wait_ge(mod_step, 3 * t + 1)
                        dve.tensor_tensor(xn[:, s, :], xn[:, s, :], rows[:, t // TB, cbr, :], ALU.mult)\
                            .then_inc(mod_step, 1)
                        dve.wait_ge(mod_step, 3 * t + 2)
                        dve.tensor_tensor(XF[:, t, :], xn[:, s, :], rows[:, t // TB, sbr, :], ALU.add)\
                            .then_inc(mod_step, 1)

                    over_tiles([(residual, 0), (modulate, 1)])
        mid.close()

        XA = fsb("XA", [P, T, D])
        XS = fsb("XS", [P, T, D // 2])
        for l in range(DEPTH):
            local_attention_phase(nc, l, psum, X, XF, XA, XS, ident, minus_half, fw_qkv, fw_o, xpos[:, l],
                                  mask)
            mlp_phase(nc, l, psum, X, XF, XA, XS, ident, minus_half, fw_1, fw_2, fb_1, f_ln, rows, out)


def local_attention_phase(nc, l, psum, X, XF, XA, XS, ident, minus_half, fw_qkv, fw_o, xpos, mask):
    def banks(a, n=1):
        return psum[:, a:a + n, :].rearrange("p b c -> p (b c)")

    with ExitStack() as ph:
        def sb(name, shape, dt=F32):
            return ph.enter_context(nc.sbuf_tensor(f"{name}_a{l}", shape, dt))

        def sem(name):
            return ph.enter_context(nc.semaphore(f"{name}_a{l}"))

        NH = 2 * FH
        HR = 8
        hT = sb("hT", [P, HR, P + 1])
        raw = sb("raw", [P, 2, NH, HD])
        sq = sb("sq", [P, NH, HD])
        ss = sb("ss", [P, 2, NH])
        ss_up = sb("ss_up", [P, 2, NH])
        rinv = sb("rinv", [P, 2, NH])
        t1 = sb("t1", [P, NH, HD])
        t2 = sb("t2", [P, 2, NH, HD])
        qk = sb("qk", [P, 2, NH, HD])
        v = sb("v", [P, 2, INNER])
        vp = sb("vp", [P, 2, INNER])
        qT = sb("qT", [P, 2, FH // 2, P])
        kT = sb("kT", [P, 2, FH // 2, WIN + P])
        S = sb("S", [P, 2, FH, 2 * WIN])
        nmax = sb("nmax", [P, 2, FH])
        E = sb("E", [P, 2, FH, 2 * WIN])
        den = sb("den", [P, 2, FH])
        den_inv = sb("den_inv", [P, 2, FH])
        EN = sb("EN", [P, 2, FH, 2 * WIN])
        ET = sb("ET", [P, 2, FH, P])
        oT = sb("oT", [P, 2, FH // 2, P])

        cleared = sem("cleared")
        x_turned = sem("x_turned")
        hT_done = sem("hT_done")
        qk_proj = sem("qk_proj")
        raw_done = sem("raw_done")
        sq_done = sem("sq_done")
        ss_done = sem("ss_done")
        up_done = sem("up_done")
        rinv_done = sem("rinv_done")
        sin_done = sem("sin_done")
        cos_done = sem("cos_done")
        sum_done = sem("sum_done")
        qk_done = sem("qk_done")
        qk_turned = sem("qk_turned")
        qkT_done = sem("qkT_done")
        scores_done = sem("scores_done")
        max_done = sem("max_done")
        exp_done = sem("exp_done")
        inv_done = sem("inv_done")
        norm_done = sem("norm_done")
        e_turned = sem("e_turned")
        eT_done = sem("eT_done")
        v_proj = sem("v_proj")
        v_done = sem("v_done")
        vp_in = [sem("vp_in0"), sem("vp_in1")]
        pv_done = sem("pv_done")
        oT_done = sem("oT_done")
        out_proj = sem("out_proj")
        xa_done = sem("xa_done")
        xs_in = sem("xs_in")

        ps_qk = banks(0, 2).rearrange("p (h d) -> p h d", d=HD)
        ps_x = banks(7)[:, 0:P]

        PROJECT, NORMS, FINISH, SCORES, SOFTMAX, TURN_E, PV, OUT = 1, 2, 3, 4, 5, 6, 7, 8

        with nc.Block() as block:
            @block.sync
            def _(sp):
                sp.wait_ge(cleared, 1)

                def shift_v(t, s):
                    need(sp, v_done, t + 1)
                    need(sp, pv_done, t - 1)
                    sp.dma_start(vp[0:WIN, s, :], v[WIN:P, 1 - s, :]).then_inc(vp_in[s], 16)
                    sp.dma_start(vp[WIN:P, s, :], v[0:WIN, s, :]).then_inc(vp_in[s], 16)

                def shift_x(t, s):
                    need(sp, xa_done, t + 1)
                    sp.dma_start(XS[1:P, t, :], XA[0:P - 1, t, D // 2:D]).then_inc(xs_in, 16)
                    if t % TB > 0:
                        sp.dma_start(XS[0:1, t, :], XA[P - 1:P, t - 1, D // 2:D]).then_inc(xs_in, 16)

                over_tiles([(shift_v, 0), (shift_x, OUT - TURN_E)])
                sp.wait_ge(xs_in, 16 * (2 * T - B))
                for s in range(2):
                    sp.wait_ge(vp_in[s], 32 * (T // 2))

            @block.gpsimd
            def _(pool):
                def square(t, s):
                    need(pool, raw_done, t + 1)
                    need(pool, ss_done, t)
                    pool.tensor_tensor(sq[:, :, :], raw[:, s], raw[:, s], ALU.mult).then_inc(sq_done, 1)

                def sin_part(t, s):
                    need(pool, sum_done, 2 * (t - 1))
                    sin = xpos[:, t % TB, 1, :, :][:, :, None, :].to_broadcast([P, 2, FH, HD])
                    pool.tensor_tensor(t2[:, s].rearrange("p (q h) d -> p q h d", q=2),
                                       raw[:, s].rearrange("p (q h) d -> p q h d", q=2), sin, ALU.mult)\
                        .then_inc(sin_done, 1)

                def inverse_norms(t, s):
                    need(pool, ss_done, t + 1)
                    pool.tensor_scalar(ss_up[:, s, :], ss[:, s, :], 1e-24, None, ALU.max).then_inc(up_done, 1)
                    need(pool, up_done, t + 1)
                    need(pool, qk_done, t - 1)
                    pool.tensor_tensor(rinv[:, s, :], ss_up[:, s, :], minus_half[:, 0:NH], ALU.pow)\
                        .then_inc(rinv_done, 1)

                over_tiles([(square, NORMS), (sin_part, NORMS), (inverse_norms, NORMS)])

            @block.scalar
            def _(act):
                act.wait_ge(cleared, 1)

                def take_oT(t, s):
                    need(act, pv_done, t + 1)
                    need(act, out_proj, t - 1)
                    act.activation(oT[:, s], banks(7).rearrange("p (j c) -> p j c", c=P), ACT.Copy)\
                        .then_inc(oT_done, 1)

                def take_v(t, s):
                    need(act, v_proj, t + 1)
                    need(act, pv_done, t - 1)
                    if t > 0:
                        act.wait_ge(vp_in[1 - s], 32 * ((t - 1) // 2 + 1))
                    act.activation(v[:, s, :], banks(2), ACT.Copy).then_inc(v_done, 1)

                def take_qkT(t, s):
                    need(act, qk_turned, 2 * t + 1)
                    need(act, scores_done, t - 1)
                    act.activation(qT[:, s, :, :], banks(3).rearrange("p (j c) -> p j c", c=P), ACT.Copy)\
                        .then_inc(qkT_done, 1)
                    need(act, qkT_done, 3 * t)
                    act.activation(kT[:, s, :, 0:WIN], kT[:, 1 - s, :, P:P + WIN], ACT.Copy).then_inc(qkT_done, 1)
                    need(act, qk_turned, 2 * t + 2)
                    act.activation(kT[:, s, :, WIN:WIN + P], banks(4).rearrange("p (j c) -> p j c", c=P), ACT.Copy)\
                        .then_inc(qkT_done, 1)

                def take_hT(t, s):
                    need(act, v_proj, t - HR + 1)
                    need(act, hT_done, 3 * t)
                    act.activation(hT[HD:P, t % HR, 0:1], hT[HD:P, (t - 1) % HR, P:P + 1], ACT.Copy,
                                   scale=0.0 if t % TB == 0 else 1.0).then_inc(hT_done, 1)
                    need(act, x_turned, t + 1)
                    act.activation(hT[0:HD, t % HR, 0:P], ps_x[0:HD, :], ACT.Copy).then_inc(hT_done, 1)
                    act.activation(hT[HD:P, t % HR, 1:P + 1], ps_x[HD:P, :], ACT.Copy).then_inc(hT_done, 1)

                def exponentials(t, s):
                    need(act, norm_done, t - 1)
                    for h in range(FH):
                        need(act, max_done, FH * t + h + 1)
                        act.activation(E[:, s, h, :], S[:, s, h, :], ACT.Exp, bias=nmax[:, s, h:h + 1],
                                       scale=-1.0, accum_out=den[:, s, h:h + 1]).then_inc(exp_done, 1)

                def take_raw(t, s):
                    need(act, qk_proj, t + 1)
                    need(act, cos_done, t - 1)
                    need(act, sin_done, t - 1)
                    act.activation(raw[:, s], ps_qk, ACT.Copy).then_inc(raw_done, 1)

                def take_eT(t, s):
                    need(act, pv_done, t - 1)
                    for n in range(2):
                        need(act, e_turned, 2 * t + n + 1)
                        act.activation(ET[:, s, 4 * n:4 * n + 4, :], banks(3 + n).rearrange("p (h c) -> p h c", c=P),
                                       ACT.Copy).then_inc(eT_done, 1)

                over_tiles([(take_oT, OUT), (take_v, TURN_E), (take_qkT, SCORES), (take_hT, 0),
                            (exponentials, SOFTMAX), (take_raw, PROJECT), (take_eT, TURN_E)])

            @block.vector
            def _(dve):
                dve.memset(kT[:, 1, :, P:P + WIN], 0.0)
                dve.memset(v[WIN:P, 1, :], 0.0)
                for b in range(B):
                    dve.memset(XS[0:1, b * TB, :], 0.0)
                dve.memset(hT[HD:P, HR - 1, P:P + 1], 0.0).then_inc(cleared, 1)
                def masked_max(t, s):
                    need(dve, scores_done, t + 1)
                    need(dve, exp_done, FH * (t - 1))
                    for h in range(FH):
                        dve.tensor_tensor_reduce(S[:, s, h, :], banks(5 + h % 2)[:, (h // 2) * P:(h // 2 + 1) * P],
                                                 mask[:, min(t % TB, 1), :], -1.0, BIG, ALU.add, ALU.min,
                                                 nmax[:, s, h:h + 1]).then_inc(max_done, 1)

                def residual(t, s):
                    need(dve, out_proj, t + 1)
                    dve.tensor_tensor(XA[:, t, :], banks(2)[:, 0:D], XF[:, t, :], ALU.add).then_inc(xa_done, 1)

                def finish(t, s):
                    need(dve, cos_done, t + 1)
                    need(dve, sin_done, t + 1)
                    need(dve, qk_turned, 2 * (t - 1))
                    m = HD // 2
                    dve.tensor_tensor(qk[:, s, :, 0:m], t1[:, :, 0:m], t2[:, s, :, m:HD], ALU.add).then_inc(sum_done, 1)
                    dve.tensor_tensor(qk[:, s, :, m:HD], t1[:, :, m:HD], t2[:, s, :, 0:m], ALU.add).then_inc(sum_done, 1)
                    need(dve, sum_done, 2 * (t + 1))
                    need(dve, rinv_done, t + 1)
                    dve.tensor_tensor(qk[:, s], qk[:, s], rinv[:, s, :][:, :, None].to_broadcast([P, NH, HD]),
                                      ALU.mult).then_inc(qk_done, 1)

                def square_sums(t, s):
                    need(dve, sq_done, t + 1)
                    need(dve, up_done, t - 1)
                    dve.tensor_reduce(ss[:, s, :], sq[:, :, :], AX_X, ALU.add).then_inc(ss_done, 1)

                def cos_part(t, s):
                    need(dve, raw_done, t + 1)
                    need(dve, sum_done, 2 * t)
                    cos = xpos[:, t % TB, 0, :, :][:, :, None, :].to_broadcast([P, 2, FH, HD])
                    dve.tensor_tensor(t1[:, :, :].rearrange("p (q h) d -> p q h d", q=2),
                                      raw[:, s].rearrange("p (q h) d -> p q h d", q=2), cos, ALU.mult)\
                        .then_inc(cos_done, 1)

                def normalise(t, s):
                    need(dve, exp_done, FH * (t + 1))
                    need(dve, norm_done, t - 1)
                    dve.reciprocal(den_inv[:, s, :], den[:, s, :]).then_inc(inv_done, 1)
                    need(dve, inv_done, t + 1)
                    need(dve, e_turned, 2 * (t - 1))
                    dve.tensor_tensor(EN[:, s, :, :], E[:, s, :, :],
                                      den_inv[:, s, :][:, :, None].to_broadcast([P, FH, 2 * WIN]), ALU.mult)\
                        .then_inc(norm_done, 1)

                over_tiles([(masked_max, SOFTMAX), (residual, OUT), (finish, FINISH), (square_sums, NORMS),
                            (cos_part, NORMS), (normalise, SOFTMAX)])

            @block.tensor
            def _(pe):
                def turn_qk(t, s):
                    need(pe, qk_done, t + 1)
                    need(pe, qkT_done, 3 * t)
                    for n in range(2):
                        need(pe, eT_done, 2 * (t + SCORES - 1 - TURN_E) + n + 1)
                        for j in range(4):
                            src = qk[:, s, 8 * n + 2 * j:8 * n + 2 * j + 2, :].rearrange("p h d -> p (h d)")
                            last = pe.transpose(banks(3 + n)[:, j * P:(j + 1) * P], src, ident[:, :])
                        last.then_inc(qk_turned, 1)

                def project_out(t, s):
                    need(pe, oT_done, t + 1)
                    need(pe, v_done, min(t + OUT - TURN_E + 1, T))
                    need(pe, xa_done, t)
                    for j in range(FH // 2):
                        last = pe.matmul(banks(2)[:, 0:D], oT[:, s, j, :], fw_o[:, l, j, :], start=(j == 0),
                                         stop=(j == FH // 2 - 1))
                    last.then_inc(out_proj, 1)

                def turn_x(t, s):
                    need(pe, hT_done, 3 * t)
                    need(pe, oT_done, t - OUT + 1)
                    pe.transpose(ps_x, XF[:, t, :], ident[:, :]).then_inc(x_turned, 1)

                def project_qk(t, s):
                    need(pe, hT_done, 3 * (t + 1))
                    need(pe, raw_done, t)
                    for n in range(2):
                        last = pe.matmul(banks(n), hT[:, t % HR, 0:P], fw_qkv[:, l, n * INNER:(n + 1) * INNER],
                                         start=True, stop=True)
                    last.then_inc(qk_proj, 1)

                def multiply_qk(t, s):
                    need(pe, qkT_done, 3 * (t + 1))
                    need(pe, max_done, FH * t)
                    for h in range(FH):
                        a = HD * (h % 2)
                        for w in range(2):
                            last = pe.matmul(banks(5 + h % 2)[WIN * w:WIN * w + WIN, (h // 2) * P:(h // 2 + 1) * P],
                                             qT[a:a + HD, s, h // 2, WIN * w:WIN * w + WIN],
                                             kT[a:a + HD, s, h // 2, WIN * w:WIN * w + 2 * WIN],
                                             start=True, stop=True)
                    last.then_inc(scores_done, 1)

                def turn_e(t, s):
                    need(pe, norm_done, t + 1)
                    need(pe, qkT_done, 3 * min(t + TURN_E - SCORES + 1, T))
                    need(pe, eT_done, 2 * t)
                    for n in range(2):
                        for j in range(4):
                            last = pe.transpose(banks(3 + n)[:, j * P:(j + 1) * P], EN[:, s, 4 * n + j, :], ident[:, :])
                        last.then_inc(e_turned, 1)

                def multiply_v(t, s):
                    need(pe, vp_in[s], 32 * (t // 2 + 1))
                    need(pe, hT_done, 3 * min(t + PV + 1, T))
                    need(pe, oT_done, t)
                    for h in range(FH):
                        need(pe, eT_done, 2 * t + h // 4 + 1)
                        a = HD * (h % 2)
                        for w in range(2):
                            last = pe.matmul(banks(7)[a:a + HD, (h // 2) * P + WIN * w:(h // 2) * P + WIN * w + WIN],
                                             (v if w else vp)[:, s, h * HD:(h + 1) * HD],
                                             ET[:, s, h, WIN * w:WIN * w + WIN], start=True, stop=True)
                    last.then_inc(pv_done, 1)

                def project_v(t, s):
                    need(pe, v_done, t)
                    need(pe, xa_done, t - (OUT - SOFTMAX) + 1)
                    pe.matmul(banks(2), hT[:, t % HR, 0:P], fw_qkv[:, l, 2 * INNER:3 * INNER], start=True, stop=True)\
                        .then_inc(v_proj, 1)

                over_tiles([(turn_qk, SCORES), (project_out, OUT), (turn_x, 0), (project_qk, PROJECT),
                            (multiply_qk, SCORES), (turn_e, TURN_E), (multiply_v, PV), (project_v, SOFTMAX)])


def mlp_phase(nc, l, psum, X, XF, XA, XS, ident, minus_half, fw_1, fw_2, fb_1, f_ln, rows, out):
    def banks(a, n=1):
        return psum[:, a:a + n, :].rearrange("p b c -> p (b c)")

    with ExitStack() as ph:
        def sb(name, shape, dt=F32):
            return ph.enter_context(nc.sbuf_tensor(f"{name}_m{l}", shape, dt))

        def sem(name):
            return ph.enter_context(nc.semaphore(f"{name}_m{l}"))

        bn = sb("bn", [P, 2, 2, 6])
        mv = sb("mv", [P, 2, 2])
        rstd = sb("rstd", [P, 2, 1])
        var_eps = sb("var_eps", [P, 2, 1])
        xn = sb("xn", [P, 2, D])
        hT = sb("hT", [P, 2, P])
        gate = sb("gate", [P, 2, HC, P])
        act_in = sb("act_in", [P, 2, HC, P])
        y = sb("y", [P, 2, D])
        res = sb("res", [P, 2, D])

        zeroed = sem("zeroed")
        ln_step = sem("ln_step")
        rstd_done = sem("rstd_done")
        eps_done = sem("eps_done")
        xn_done = sem("xn_done")
        x_turned = sem("x_turned")
        hT_done = sem("hT_done")
        w1_mm = sem("w1_mm")
        gelu_done = sem("gelu_done")
        u_done = sem("u_done")
        w2_mm = sem("w2_mm")
        xf_done = sem("xf_done")
        y_done = sem("y_done")
        res_done = sem("res_done")
        res_out = [sem("res_out0"), sem("res_out1")]
        last_layer = l == DEPTH - 1
        width = [P] * (HC - 1) + [HLAST]

        with nc.Block() as block:
            @block.sync
            def _(sp):
                if last_layer:
                    def store(t, s):
                        need(sp, res_done, t + 1)
                        sp.dma_start(out[t // TB, bass.ts(t % TB, P), :], res[:, s, :]).then_inc(res_out[s], 16)

                    over_tiles([(store, 0)])
                    for s in range(2):
                        sp.wait_ge(res_out[s], 16 * (T // 2))

            @block.gpsimd
            def _(pool):
                def ln_rstd(t, s):
                    need(pool, ln_step, 3 * t + 3)
                    need(pool, xn_done, 2 * (t - 1))
                    pool.tensor_scalar(var_eps[:, s, :], mv[:, s, 1:2], EPS, None, ALU.add).then_inc(eps_done, 1)
                    need(pool, eps_done, t + 1)
                    pool.tensor_tensor(rstd[:, s, :], var_eps[:, s, :], minus_half[:, 0:1], ALU.pow).then_inc(rstd_done, 1)

                over_tiles([(ln_rstd, 0)])

            @block.scalar
            def _(act):
                def take_hT(t, s):
                    need(act, x_turned, t + 1)
                    need(act, w1_mm, 2 * (t - 1))
                    act.activation(hT[:, s, :], banks(6 + s)[:, 0:P], ACT.Identity, bias=f_ln[:, l, 1:2],
                                   scale=f_ln[:, l, 0:1]).then_inc(hT_done, 1)

                def gelu(t, s):
                    need(act, w1_mm, 2 * t + 1)
                    need(act, u_done, HC * (t - 1))
                    for j, n in enumerate(width):
                        act.activation(gate[0:n, s, j, :], banks(2 * s)[0:n, j * P:(j + 1) * P], ACT.Gelu,
                                       bias=fb_1[0:n, l, 1, j:j + 1]).then_inc(gelu_done, 1)

                over_tiles([(gelu, 3), (take_hT, 2)])

            @block.vector
            def _(dve):
                for s in range(2):
                    dve.memset(act_in[:, s, HC - 1, :], 1.0).then_inc(zeroed, 1)
                dve.wait_ge(zeroed, 2)

                def ln_stats(t, s):
                    need(dve, xn_done, 2 * (t - 1))
                    dve.bn_stats(bn[:, s, 0, :], XA[:, t, 0:D // 2]).then_inc(ln_step, 1)
                    dve.bn_stats(bn[:, s, 1, :], XS[:, t, :]).then_inc(ln_step, 1)
                    dve.wait_ge(ln_step, 3 * t + 2)
                    dve.bn_aggr(mv[:, s, :], bn[:, s, :, :].rearrange("p a b -> p (a b)")).then_inc(ln_step, 1)

                def ln_apply(t, s):
                    need(dve, rstd_done, t + 1)
                    need(dve, x_turned, t - 1)
                    for n, src in enumerate((XA[:, t, 0:D // 2], XS[:, t, :])):
                        dve.tensor_scalar(xn[:, s, n * (D // 2):(n + 1) * (D // 2)], src, mv[:, s, 0:1], rstd[:, s, :],
                                          ALU.subtract, ALU.mult).then_inc(xn_done, 1)

                def gated(t, s):
                    need(dve, w1_mm, 2 * t + 2)
                    need(dve, w2_mm, t - 1)
                    for j, n in enumerate(width):
                        need(dve, gelu_done, HC * t + j + 1)
                        dve.scalar_tensor_tensor(act_in[0:n, s, j, :], banks(2 * s + 1)[0:n, j * P:(j + 1) * P],
                                                 fb_1[0:n, l, 0, j:j + 1], gate[0:n, s, j, :], ALU.add, ALU.mult)\
                            .then_inc(u_done, 1)

                def residual(t, s):
                    need(dve, w2_mm, t + 1)
                    dve.tensor_tensor(XF[:, t, :], banks(4 + s)[:, 0:D], XA[:, t, :], ALU.add).then_inc(xf_done, 1)
                    if last_layer:
                        dve.wait_ge(xf_done, t + 1)
                        dve.tensor_tensor(y[:, s, :], XF[:, t, :], rows[:, t // TB, 3, :], ALU.mult).then_inc(y_done, 1)
                        dve.wait_ge(y_done, t + 1)
                        need(dve, res_out[s], 16 * (t // 2))
                        dve.tensor_tensor(res[:, s, :], y[:, s, :], X[:, t, :], ALU.add).then_inc(res_done, 1)

                over_tiles([(gated, 4), (ln_apply, 2), (ln_stats, 0), (residual, 5)])

            @block.tensor
            def _(pe):
                def turn_x(t, s):
                    need(pe, xn_done, 2 * (t + 1))
                    need(pe, hT_done, t - 1)
                    pe.transpose(banks(6 + s)[:, 0:P], xn[:, s, :], ident[:, :]).then_inc(x_turned, 1)

                def hidden(t, s):
                    need(pe, hT_done, t + 1)
                    for m in range(2):
                        need(pe, u_done if m else gelu_done, HC * (t - 1))
                        off = 0 if m else HID
                        for j, n in enumerate(width):
                            last = pe.matmul(banks(2 * s + m)[0:n, j * P:(j + 1) * P],
                                             fw_1[:, l, off + j * P:off + j * P + n], hT[:, s, :],
                                             start=True, stop=True)
                        last.then_inc(w1_mm, 1)

                def project(t, s):
                    need(pe, u_done, HC * (t + 1))
                    need(pe, (res_done if last_layer else xf_done), t - 1)
                    for j, n in enumerate(width):
                        rows_in = n + (j == HC - 1)
                        last = pe.matmul(banks(4 + s)[:, 0:D], act_in[0:rows_in, s, j, :], fw_2[0:rows_in, l, j, :],
                                         start=(j == 0), stop=(j == HC - 1))
                    last.then_inc(w2_mm, 1)

                over_tiles([(project, 5), (hidden, 3), (turn_x, 2)])


_INS = ['L0_attn_x', 'L0_attn_Wq', 'L0_attn_Wk', 'L0_attn_Wv', 'L0_attn_Wo', 'L0_ffn_wqkv', 'L0_ffn_q_scale',
        'L0_ffn_k_scale', 'L0_ffn_wo', 'L0_ffn_ln_g', 'L0_ffn_ln_b', 'L0_ffn_w1', 'L0_ffn_b1', 'L0_ffn_w2',
        'L0_ffn_b2', 'L0_c', 'L0_wmod']
_OUTS = [((B, N, D), 'float32')]


def kernel(**inputs):
    import concourse.bacc as bacc
    from concourse.bass_utils import run_bass_kernel_spmd

    nc = bacc.Bacc("TRN2", target_bir_lowering=False, num_devices=1)
    arrays, args = {}, []
    given = {name: np.ascontiguousarray(inputs[name]) for name in _INS} | shape_constants()
    for name, a in given.items():
        arrays[f"in_{name}_dram"] = a
        args.append(nc.dram_tensor(f"in_{name}_dram", a.shape, mybir.dt.from_np(a.dtype), kind="ExternalInput").ap())
    for i, (shape, dtype) in enumerate(_OUTS):
        args.append(nc.dram_tensor(f"out_{i}_dram", shape, mybir.dt.from_np(np.dtype(dtype)),
                                   kind="ExternalOutput").ap())
    adaln_block(nc, *args)
    r = run_bass_kernel_spmd(nc, [arrays], core_ids=[0])
    return r.results[0]["out_0_dram"]
```

```python
import math
from contextlib import ExitStack

import concourse.bass as bass
import numpy as np
from concourse import mybir

F32 = mybir.dt.float32
F32R = mybir.dt.float32r
ALU = mybir.AluOpType
ACT = mybir.ActivationFunctionType
AX_X = mybir.AxisListType.X

P = 128
B, N, D = 2, 1024, 128
TB = N // P
T = B * TB
H, KV, HD = 16, 4, 64
PAIRS = H // 2
GROUP = H // KV
HEADS = B * H
QW, KW = H * HD, KV * HD
DEPTH, FH, WIN = 2, 8, 64
INNER = FH * HD
HID = int(D * 4 * 2 / 3)
HC = -(-HID // P)
HLAST = HID - (HC - 1) * P
EPS = 1e-5
BIG = 3e38
POOL_SUMS = (0, 1, 2, 4, 6)
DVE_SUMS = (3, 5, 7)
MLP_STEP, LAYER_STEPS = T + 3, 2 * T + 2
AHEAD = 2


def shape_constants():
    f = np.float32
    pos = np.arange(N, dtype=f)
    inv = (f(1.0) / f(10000.0) ** (np.arange(0, HD, 2, dtype=f) / f(HD))).astype(f)
    ang = (pos[:, None] * inv[None, :]).astype(f).astype(np.float64)
    cos, sin = np.cos(ang).astype(f), np.sin(ang).astype(f)
    rope = np.stack([np.concatenate([cos, cos], 1), np.concatenate([sin, -sin], 1)], 1)
    half = np.arange(0, HD, 2, dtype=f)
    base = ((half + f(0.4 * HD)) / f(1.4 * HD)).astype(f)
    power = ((pos - f(N // 2)) / f(WIN // 2)).astype(f)
    scale = np.power(base[None, :].astype(np.float64), power[:, None].astype(np.float64))
    xc, xs = [], []
    for s in (8.0 * scale, 1.0 / scale):
        xc.append(np.concatenate([cos * s, cos * s], 1))
        xs.append(np.concatenate([sin * s, -sin * s], 1))
    xpos = np.stack([np.concatenate(xc, 1), np.concatenate(xs, 1)], 1).astype(f)
    start = 2.0 ** (-2.0 ** (-(math.log2(H) - 3)))
    slopes = np.array([start * start ** i for i in range(H)])
    far = np.arange(N) - (N - 1)
    bias = slopes[None, :, None] * far.reshape(TB, P).T[:, None, :]
    i = (np.arange(P) % WIN)[:, None]
    j = np.arange(2 * WIN)[None, :]
    seen = (j <= i + WIN) & (j >= i)
    mask = np.zeros((P, TB, 2 * WIN), f)
    mask[:] = np.where(seen, 0.0, -1e30)[:, None, :]
    mask[:WIN, 0, :WIN] = -1e30
    return {
        "ident": np.eye(P, dtype=f),
        "rope": rope.astype(f),
        "xpos": xpos,
        "far": far.astype(f)[None, :],
        "slope": np.tile(slopes.astype(f)[None, :], (P, B)),
        "keybias": np.tile(bias.astype(f), (1, B, 1)),
        "mask": mask,
    }


def need(eng, sem, count):
    if count > 0:
        eng.wait_ge(sem, count)


def over_tiles(stages, tiles=T):
    for step in range(tiles + max(lag for _, lag in stages)):
        for fn, lag in stages:
            if 0 <= step - lag < tiles:
                fn(step - lag, (step - lag) % 2)


def adaln_block(nc, x, wq, wk, wv, wo, f_wqkv, f_qs, f_ks, f_wo, f_lg, f_lb, f_w1, f_b1, f_w2, f_b2,
                c, wmod, ident_d, rope_d, xpos_d, far_d, slope_d, keybias_d, mask_d, out):
    qa_d = nc.dram_tensor("qa_scratch", (B, H, P, TB, P), F32, kind="Internal").ap()
    k_d = nc.dram_tensor("k_scratch", (B, KV, P, TB, P), F32, kind="Internal").ap()
    v_d = nc.dram_tensor("v_scratch", (B, KV, P, TB, HD), F32, kind="Internal").ap()
    inv_d = nc.dram_tensor("inverse_scratch", (2, N), F32, kind="Internal").ap()

    with ExitStack() as whole:
        whole.enter_context(nc.allow_non_contiguous_dma(reason="a few columns of biases"))

        def sb_in(ctx, side="left"):
            return lambda name, shape, dt=F32: ctx.enter_context(nc.sbuf_tensor(name, shape, dt, side=side))

        def sem(name):
            early_sems.append(nc.alloc_semaphore(name))
            return early_sems[-1]

        early_sems = []
        sb = sb_in(whole)
        psum = whole.enter_context(nc.psum_tensor("psum", [P, 8, 512], F32))

        def banks(a, n=1):
            return psum[:, a:a + n, :].rearrange("p b c -> p (b c)")

        X = sb("X", [P, T, D])
        XF = sb("XF", [P, T, D])
        ident = sb("ident", [P, P])
        rows = sb("rows", [P, B, 4, D])
        minus_half = sb("minus_half", [P, 2 * FH])
        cols = sb("cols", [P, B, 6])
        ga, sbr, cbr, gbr = range(4)
        wo_sb = sb("wo_sb", [P, PAIRS, D])
        fw_qkv = sb("fw_qkv", [P, DEPTH, 3 * INNER])
        fw_o = sb("fw_o", [P, DEPTH, FH // 2, D])
        fw_1 = sb("fw_1", [P, DEPTH, 2 * HID])
        fw_2 = sb("fw_2", [P, DEPTH, HC, D])
        fb_1 = sb("fb_1", [P, DEPTH, 2, HC])
        f_ln = sb("f_ln", [P, DEPTH, 2])

        ahead = ExitStack()
        sb = sb_in(ahead, "right")
        QA = sb("QA", [P, 4, N], F32R)
        KA = sb("KA", [P, 2, N], F32R)
        KB = sb("KB", [P, 2, N], F32R)
        V = sb("V", [P, 2, TB, HD])
        far = sb("far_sb", [P, N])
        slope = sb("slope_sb", [P, HEADS])
        keybias = sb("keybias_sb", [P, HEADS, TB])
        ld_const = sem("ld_const")
        ld_qa = [sem(f"ld_qa{s}") for s in range(4)]
        ld_kv = [sem(f"ld_kv{s}") for s in range(2)]
        loaded_late = sem("loaded_late")
        late_loads = []

        def load_qa(sp, i, s):
            sp.dma_start(QA[:, s, :].bitcast(F32).rearrange("p (t c) -> p t c", c=P), qa_d[i // H, i % H])\
                .then_inc(ld_qa[s], 16)

        def load_kv(sp, g, s):
            high, low = k_d[g // KV, g % KV, 0:HD], k_d[g // KV, g % KV, HD:P]
            for dst, src in ((KA[0:HD], high), (KA[HD:P], high), (KB[0:HD], low)):
                sp.dma_start(dst[:, s, :].bitcast(F32).rearrange("p (t c) -> p t c", c=P), src)\
                    .then_inc(ld_kv[s], 16)
            sp.dma_start(V[:, s, :, :], v_d[g // KV, g % KV]).then_inc(ld_kv[s], 16)

        with ExitStack() as ph:
            sb = sb_in(ph)
            v_sb = sb("v_sb", [P, 2, KW])
            tT = sb("tT", [P, 2, H + KV, P], F32R)
            w_sb = sb("w_sb", [P, QW + 2 * KW])
            rope = sb("rope_sb", [P, TB, 2, HD])
            wmod_sb = sb("wmod_sb", [P, 6 * D])
            cT = sb("cT", [P, B])
            ec = sb("ec", [P, B])
            silu = sb("silu", [P, B])
            silu_wide = sb("silu_wide", [P, B, P])
            guard = sb("guard", [P, B, 2, 2, D])
            bn = sb("bn", [P, 2, 6])
            mv = sb("mv", [P, 2, 2])
            rstd = sb("rstd", [P, 2, 1])
            var_eps = sb("var_eps", [P, 2, 1])
            xn = sb("xn", [P, 2, D])
            hT = sb("hT", [P, 2, P])
            raw = sb("raw", [P, 2, H + KV, HD])
            t1 = sb("t1", [P, H + KV, HD])
            t2 = sb("t2", [P, 2, H + KV, HD])
            qk = sb("qk", [P, 2, H + KV, HD])
            qs_ = sb("q_split", [P, 2, H, P], F32R)
            ks_ = sb("k_split", [P, 2, KV, P], F32R)

            ld_x = [sem(f"ld_x{b}") for b in range(B)]
            ld_ident = sem("ld_ident")
            ld_c = sem("ld_c")
            ld_w = sem("ld_w")
            ld_mod = sem("ld_mod")
            ld_rope = sem("ld_rope")
            ec_done = sem("ec_done")
            silu_step = sem("silu_step")
            wide_done = sem("wide_done")
            mod_mm = sem("mod_mm")
            mod_step = sem("mod_step")
            const_step = sem("const_step")
            ln_step = sem("ln_step")
            rstd_done = sem("rstd_done")
            eps_done = sem("eps_done")
            half_set = sem("half_set")
            xn_done = sem("xn_done")
            xT_done = sem("xT_done")
            hT_done = sem("hT_done")
            qkv_done = sem("qkv_done")
            v_copied = sem("v_copied")
            raw_done = sem("raw_done")
            cos_done = sem("cos_done")
            sin_done = sem("sin_done")
            sum_done = sem("sum_done")
            high_done = sem("high_done")
            low_done = sem("low_done")
            tr_done = sem("tr_done")
            tr_copied = sem("tr_copied")

            v_out, t_out = ([[sem(f"{name}{b}{s}") for s in range(2)] for b in range(B)] for name in ("v_out", "t_out"))

            def need_sent(eng, sems, count, t):
                if t >= 2:
                    eng.wait_ge(sems[(t - 2) // TB][t % 2], count * ((t - 2) % TB // 2 + 1))

            def need_landed(eng, b):
                for s in range(2):
                    eng.wait_ge(t_out[b][s], 48 * (TB // 2))
                    eng.wait_ge(v_out[b][s], 16 * (TB // 2))

            ps_qk = banks(0, 3)[:, 0:QW + KW].rearrange("p (h d) -> p h d", d=HD)
            ps_v = banks(3)[:, 0:KW]
            ps_x = banks(7)[:, 0:P]
            NTR = (H + KV) // 4

            with nc.Block() as block:
                @block.sync
                def _(sp):
                    sp.dma_start(cT[:, :], c.rearrange("b d -> d b")).then_inc(ld_c, 16)
                    sp.dma_start(wmod_sb[:, :], wmod).then_inc(ld_mod, 16)
                    sp.dma_start(X[:, 0:TB, :], x[0].rearrange("(t p) d -> p t d", p=P)).then_inc(ld_x[0], 16)
                    sp.dma_start(ident[:, :], ident_d).then_inc(ld_ident, 16)
                    sp.dma_start(w_sb[:, 0:QW], wq).then_inc(ld_w, 16)
                    sp.dma_start(w_sb[:, QW:QW + KW], wk).then_inc(ld_w, 16)
                    sp.dma_start(w_sb[:, QW + KW:], wv).then_inc(ld_w, 16)
                    sp.dma_start(rope[:, :, :, :], rope_d.rearrange("(t p) s d -> p t s d", p=P)).then_inc(ld_rope, 16)
                    sp.dma_start(X[:, TB:T, :], x[1].rearrange("(t p) d -> p t d", p=P)).then_inc(ld_x[1], 16)

                    def late(dst, src):
                        sp.dma_start(dst, src).then_inc(loaded_late, 16)
                        late_loads.append(1)

                    late(wo_sb[:, :, :], wo.rearrange("(j p) n -> p j n", p=P))
                    late(fw_qkv[:, :, :], f_wqkv.rearrange("l p n -> p l n"))
                    late(fw_o[:, :, :, :], f_wo.rearrange("l (j p) n -> p l j n", p=P))
                    late(fw_1[:, :, :], f_w1.rearrange("l p n -> p l n"))
                    late(f_ln[:, :, 0], f_lg.rearrange("l p -> p l"))
                    late(f_ln[:, :, 1], f_lb.rearrange("l p -> p l"))
                    for l in range(DEPTH):
                        late(fw_2[:, l, 0:HC - 1, :], f_w2[l, 0:(HC - 1) * P, :].rearrange("(j p) n -> p j n", p=P))
                        late(fw_2[0:HLAST, l, HC - 1, :], f_w2[l, (HC - 1) * P:HID, :])
                        late(fw_2[HLAST:HLAST + 1, l, HC - 1, :], f_b2[l:l + 1, :])
                        for s in range(2):
                            b1 = f_b1[l, s * HID:(s + 1) * HID]
                            late(fb_1[:, l, s, 0:HC - 1], b1[0:(HC - 1) * P].rearrange("(j p) -> p j", p=P))
                            late(fb_1[0:HLAST, l, s, HC - 1:HC], b1[(HC - 1) * P:HID].rearrange("(p o) -> p o", o=1))

                    sp.dma_start(far[:, :], far_d[0].partition_broadcast(P)).then_inc(ld_const, 16)
                    sp.dma_start(slope[:, :], slope_d).then_inc(ld_const, 16)
                    sp.dma_start(keybias[:, :, :], keybias_d).then_inc(ld_const, 16)

                    def store_v(t, s):
                        need(sp, v_copied, t + 1)
                        sp.dma_start(v_d[t // TB, :, :, t % TB, :].rearrange("g p d -> p g d"),
                                     v_sb[:, s, :].rearrange("p (g d) -> p g d", d=HD)).then_inc(v_out[t // TB][s], 16)

                    def first_heads(t, s):
                        if t == TB + 2:
                            need_landed(sp, 0)
                            load_kv(sp, 0, 0)
                            for i in range(3):
                                load_qa(sp, i, i)

                    def store_qk(t, s):
                        for a in range(0, H, H // 2):
                            need(sp, tr_copied, NTR * t + (a + H // 2) // 4)
                            sp.dma_start(qa_d[t // TB, a:a + H // 2, :, t % TB, :].rearrange("h p c -> p h c"),
                                         tT[:, s, a:a + H // 2, :].bitcast(F32)).then_inc(t_out[t // TB][s], 16)
                        need(sp, tr_copied, NTR * (t + 1))
                        sp.dma_start(k_d[t // TB, :, :, t % TB, :].rearrange("h p c -> p h c"),
                                     tT[:, s, H:, :].bitcast(F32)).then_inc(t_out[t // TB][s], 16)

                    over_tiles([(first_heads, 3), (store_qk, 3), (store_v, 0)])

                @block.gpsimd
                def _(pool):
                    def ln_rstd(t, s):
                        need(pool, ln_step, 2 * t + 2)
                        need(pool, xn_done, t - 1)
                        pool.tensor_scalar(var_eps[:, s, :], mv[:, s, 1:2], EPS, None, ALU.add).then_inc(eps_done, 1)
                        need(pool, eps_done, t + 1)
                        pool.tensor_tensor(rstd[:, s, :], var_eps[:, s, :], minus_half[:, 0:1], ALU.pow).then_inc(rstd_done, 1)

                    def sin_part(t, s):
                        pool.wait_ge(ld_rope, 16)
                        need(pool, raw_done, t + 1)
                        need(pool, sum_done, 2 * (t - 1))
                        sin = rope[:, t % TB, 1, :][:, None, :].to_broadcast([P, H + KV, HD])
                        pool.tensor_tensor(t2[:, s], raw[:, s], sin, ALU.mult).then_inc(sin_done, 1)

                    pool.memset(minus_half[:, :], -0.5).then_inc(half_set, 1)
                    pool.wait_ge(half_set, 1)
                    over_tiles([(ln_rstd, 0), (sin_part, 2)])

                @block.scalar
                def _(act):
                    act.wait_ge(ld_c, 16)
                    act.activation(ec[:, :], cT[:, :], ACT.Exp, scale=-1.0).then_inc(ec_done, 1)

                    def modulate(t, s):
                        need(act, xT_done, t + 1)
                        if t == 0:
                            act.wait_ge(mod_step, 2)
                        need(act, qkv_done, t - 1)
                        act.activation(hT[:, s, :], ps_x, ACT.Identity, bias=cols[:, t // TB, 0:1],
                                       scale=cols[:, t // TB, 1:2]).then_inc(hT_done, 1)

                    def take_v(t, s):
                        need(act, qkv_done, t + 1)
                        need_sent(act, v_out, 16, t)
                        act.activation(v_sb[:, s, :], ps_v, ACT.Copy).then_inc(v_copied, 1)

                    def take_raw(t, s):
                        need(act, qkv_done, t + 1)
                        need(act, cos_done, t - 1)
                        need(act, sin_done, t - 1)
                        act.activation(raw[:, s], ps_qk, ACT.Copy).then_inc(raw_done, 1)

                    def take_transposed(t, s):
                        need_sent(act, t_out, 48, t)
                        for g in range(NTR):
                            need(act, tr_done, NTR * t + g + 1)
                            act.activation(tT[:, s, 4 * g:4 * g + 4, :].rearrange("p h c -> p (h c)"),
                                           banks(4 + (NTR * t + g) % 3), ACT.Copy).then_inc(tr_copied, 1)

                    def high_parts(t, s):
                        need(act, sum_done, 2 * t + 2)
                        need(act, tr_done, NTR * (t - 1))
                        act.activation(qs_[:, s, :, 0:HD], qk[:, s, 0:H, :], ACT.Copy, scale=HD ** -0.5)\
                            .then_inc(high_done, 1)
                        act.activation(ks_[:, s, :, 0:HD], qk[:, s, H:, :], ACT.Copy).then_inc(high_done, 1)

                    over_tiles([(high_parts, 4), (take_raw, 2), (take_v, 2), (modulate, 1), (take_transposed, 5)])

                @block.vector
                def _(dve):
                    dve.wait_ge(ec_done, 1)
                    dve.tensor_scalar(ec[:, :], ec[:, :], 1.0, None, ALU.add).then_inc(silu_step, 1)
                    dve.wait_ge(silu_step, 1)
                    dve.wait_ge(ld_c, 16)
                    dve.reciprocal(ec[:, :], ec[:, :]).then_inc(silu_step, 1)
                    dve.wait_ge(silu_step, 2)
                    dve.tensor_tensor(silu[:, :], cT[:, :], ec[:, :], ALU.mult).then_inc(silu_step, 1)
                    dve.wait_ge(silu_step, 3)
                    for b in range(B):
                        dve.tensor_copy(silu_wide[:, b, :], silu[:, b:b + 1].to_broadcast([P, P])).then_inc(wide_done, 1)
                    dve.wait_ge(mod_mm, 1)
                    mod_ps = banks(7)[:, 0:6 * B].rearrange("p (m b) -> p m b", b=B)
                    dve.tensor_copy(cols[:, :, 0], mod_ps[:, 0, :]).then_inc(mod_step, 1)
                    dve.tensor_scalar(cols[:, :, 1], mod_ps[:, 1, :], 1.0, None, ALU.add).then_inc(mod_step, 1)

                    def make_rows(b, s):
                        dve.wait_ge(mod_mm, 2 + b)
                        ps = banks(4 + b).rearrange("p (m d) -> p m d", d=D)
                        gates = ps[:, 0:4:3, :]
                        dve.tensor_scalar(guard[:, b, 0, :, :], gates, 0.0, 2.0, ALU.is_ge, ALU.mult)\
                            .then_inc(const_step, 1)
                        dve.tensor_scalar(guard[:, b, 1, :, :], gates, 0.25, None, ALU.max).then_inc(const_step, 1)
                        dve.wait_ge(const_step, 2 + 3 * b)
                        dve.scalar_tensor_tensor(guard[:, b, 1, :, :], gates, -1.0, guard[:, b, 1, :, :],
                                                 ALU.mult, ALU.max).then_inc(const_step, 1)
                        dve.wait_ge(const_step, 3 + 3 * b)
                        dve.scalar_tensor_tensor(rows[:, b, 0:4:3, :], guard[:, b, 0, :, :], -1.0,
                                                 guard[:, b, 1, :, :], ALU.add, ALU.mult).then_inc(mod_step, 1)
                        dve.tensor_copy(rows[:, b, 1, :], ps[:, 1, :]).then_inc(mod_step, 1)
                        dve.tensor_scalar(rows[:, b, 2, :], ps[:, 2, :], 1.0, None, ALU.add).then_inc(mod_step, 1)

                    def first_rows(t, s):
                        if t < B:
                            make_rows(t, s)

                    def ln_stats(t, s):
                        dve.wait_ge(ld_x[t // TB], 16)
                        need(dve, xn_done, t - 1)
                        dve.bn_stats(bn[:, s, :], X[:, t, :]).then_inc(ln_step, 1)
                        dve.wait_ge(ln_step, 2 * t + 1)
                        dve.bn_aggr(mv[:, s, :], bn[:, s, :]).then_inc(ln_step, 1)

                    def ln_apply(t, s):
                        need(dve, rstd_done, t + 1)
                        need(dve, xT_done, t - 1)
                        dve.tensor_scalar(xn[:, s, :], X[:, t, :], mv[:, s, 0:1], rstd[:, s, :],
                                          ALU.subtract, ALU.mult).then_inc(xn_done, 1)

                    def cos_part(t, s):
                        dve.wait_ge(ld_rope, 16)
                        need(dve, raw_done, t + 1)
                        need(dve, sum_done, 2 * t)
                        cos = rope[:, t % TB, 0, :][:, None, :].to_broadcast([P, H + KV, HD])
                        dve.tensor_tensor(t1[:, :, :], raw[:, s], cos, ALU.mult).then_inc(cos_done, 1)

                    def rotated(t, s):
                        need(dve, cos_done, t + 1)
                        need(dve, sin_done, t + 1)
                        need(dve, high_done, 2 * (t - 1))
                        need(dve, low_done, 2 * (t - 1))
                        m = HD // 2
                        dve.tensor_tensor(qk[:, s, :, 0:m], t1[:, :, 0:m], t2[:, s, :, m:HD], ALU.add)\
                            .then_inc(sum_done, 1)
                        dve.tensor_tensor(qk[:, s, :, m:HD], t1[:, :, m:HD], t2[:, s, :, 0:m], ALU.add)\
                            .then_inc(sum_done, 1)

                    def low_parts(t, s):
                        need(dve, high_done, 2 * t + 2)
                        need(dve, tr_done, NTR * (t - 1))
                        dve.scalar_tensor_tensor(qs_[:, s, :, HD:P], qk[:, s, 0:H, :], HD ** -0.5,
                                                 qs_[:, s, :, 0:HD].bitcast(F32), ALU.mult, ALU.subtract)\
                            .then_inc(low_done, 1)
                        dve.tensor_tensor(ks_[:, s, :, HD:P], qk[:, s, H:, :],
                                          ks_[:, s, :, 0:HD].bitcast(F32), ALU.subtract).then_inc(low_done, 1)

                    over_tiles([(ln_apply, 1), (low_parts, 5), (rotated, 3), (ln_stats, 0), (first_rows, 1),
                                (cos_part, 2)])

                @block.tensor
                def _(pe):
                    pe.wait_ge(ld_mod, 16)
                    pe.wait_ge(silu_step, 3)
                    for m in range(6):
                        last = pe.matmul(banks(7)[:, B * m:B * m + B], wmod_sb[:, m * D:(m + 1) * D],
                                         silu[:, :], start=True, stop=True)
                    last.then_inc(mod_mm, 1)
                    pe.wait_ge(wide_done, B)
                    for b in range(B):
                        pe.matmul(banks(4 + b), silu_wide[:, b, :], wmod_sb[:, 2 * D:6 * D], start=True, stop=True)\
                            .then_inc(mod_mm, 1)
                    pe.wait_ge(ld_ident, 16)
                    pe.wait_ge(mod_step, 2)

                    def x_transposed(t, s):
                        need(pe, xn_done, t + 1)
                        need(pe, hT_done, t)
                        pe.transpose(ps_x, xn[:, s, :], ident[:, :]).then_inc(xT_done, 1)

                    def project(t, s):
                        pe.wait_ge(ld_w, 48)
                        need(pe, hT_done, t + 1)
                        need(pe, raw_done, t)
                        need(pe, v_copied, t)
                        for n in range(2):
                            pe.matmul(banks(n), hT[:, s, :], w_sb[:, n * 512:(n + 1) * 512], start=True, stop=True)
                        pe.matmul(banks(2)[:, 0:KW], hT[:, s, :], w_sb[:, QW:QW + KW], start=True, stop=True)
                        pe.matmul(ps_v, hT[:, s, :], w_sb[:, QW + KW:], start=True, stop=True).then_inc(qkv_done, 1)

                    def split_transposed(t, s):
                        pe.wait_ge(mod_step, 2 + 3 * B)
                        need(pe, low_done, 2 * t + 2)
                        for g in range(NTR):
                            need(pe, tr_copied, NTR * t + g - 2)
                            for j in range(4):
                                h = 4 * g + j
                                src = qs_[:, s, h, :] if h < H else ks_[:, s, h - H, :]
                                last = pe.transpose(banks(4 + (NTR * t + g) % 3)[:, j * P:(j + 1) * P], src.bitcast(F32),
                                                    ident[:, :])
                            last.then_inc(tr_done, 1)

                    over_tiles([(project, 2), (x_transposed, 1), (split_transposed, 5)])

        fsb = sb_in(whole)
        xpos = fsb("xpos_sb", [P, DEPTH, TB, 2, 2, HD])
        mask = fsb("mask_sb", [P, 2, 2 * WIN])
        scale_row = fsb("scale_row", [P, DEPTH, 2, HD])

        ld_tab = whole.enter_context(nc.semaphore("ld_tab"))
        LD_TAB = 16 * 3

        def scale_tables(pool, l, a, b):
            tables = xpos[:, l, a:b].rearrange("p t s q d -> p (t s) (q d)")
            pool.wait_ge(ld_tab, LD_TAB * (l + 1))
            scales = scale_row[:, l].rearrange("p q d -> p (q d)")[:, None, :].to_broadcast([P, 2 * (b - a), 2 * HD])
            pool.tensor_tensor(tables, tables, scales, ALU.mult)

        mid = ExitStack()
        mv = fsb("mv_o", [P, T, 2])
        rstd = fsb("rstd_o", [P, T, 1])
        var_eps = fsb("var_eps_o", [P, T, 1])
        xf_done, res_step, rstd_done, eps_done, mod_step = (
            whole.enter_context(nc.semaphore(name)) for name in
            ("xf_done_o", "res_step", "rstd_done_o", "eps_done_o", "mod_step_o"))
        sb = sb_in(mid)
        OT = sb("OT", [P, B, PAIRS, TB, P])
        y = far[:, 0:2 * D].rearrange("p (s d) -> p s d", d=D)
        bn = sb("bn_o", [P, 2, 6])
        proj_done, ld_mask = (mid.enter_context(nc.semaphore(name)) for name in ("proj_done", "ld_mask"))

        EARLY = 4

        def projected(t):
            bank, n = (t // 4, t % 4) if t < TB else (2 + t % 4, (t - TB) // 4)
            return banks(bank)[:, n * D:(n + 1) * D]

        def project_out(pe, t):
            need(pe, res_step, 4 * (t - 4) + 1 if t >= TB + 4 else 0)
            for j in range(PAIRS):
                last = pe.matmul(projected(t), OT[:, t // TB, j, t % TB, :], wo_sb[:, j, :],
                                 start=(j == 0), stop=(j == PAIRS - 1))
            last.then_inc(proj_done, 1)

        def residual(dve, t):
            s = t % 2
            need(dve, proj_done, t // 4 * 4 + 4 if t < TB else t + 1)
            dve.tensor_tensor(y[:, s, :], projected(t), rows[:, t // TB, ga, :], ALU.mult).then_inc(res_step, 1)
            dve.wait_ge(res_step, 4 * t + 1)
            dve.tensor_tensor(X[:, t, :], X[:, t, :], y[:, s, :], ALU.add).then_inc(res_step, 1)
            dve.wait_ge(res_step, 4 * t + 2)
            dve.bn_stats(bn[:, s, :], X[:, t, :]).then_inc(res_step, 1)
            dve.wait_ge(res_step, 4 * t + 3)
            dve.bn_aggr(mv[:, t, :], bn[:, s, :]).then_inc(res_step, 1)

        def second_rstd(pool, t):
            need(pool, res_step, 4 * t + 4)
            pool.tensor_scalar(var_eps[:, t, :], mv[:, t, 1:2], EPS, None, ALU.add).then_inc(eps_done, 1)
            need(pool, eps_done, t + 1)
            need(pool, rstd_done, t)
            pool.tensor_tensor(rstd[:, t, :], var_eps[:, t, :], minus_half[:, 0:1], ALU.pow).then_inc(rstd_done, 1)

        def modulate_out(dve, t):
            s = t % 2
            need(dve, rstd_done, t + 1)
            need(dve, xf_done, t - 1)
            dve.tensor_scalar(xn[:, s, :], X[:, t, :], mv[:, t, 0:1], rstd[:, t, :], ALU.subtract, ALU.mult)\
                .then_inc(mod_step, 1)
            dve.wait_ge(mod_step, 2 * t + 1)
            dve.tensor_tensor(xn[:, s, :], xn[:, s, :], rows[:, t // TB, cbr, :], ALU.mult).then_inc(mod_step, 1)

        def shifted_out(dve, t):
            need(dve, mod_step, 2 * t + 2)
            dve.tensor_tensor(XF[:, t, :], xn[:, t % 2, :], rows[:, t // TB, sbr, :], ALU.add).then_inc(xf_done, 1)

        DQ = N // 4
        with ExitStack() as ph:
            sb = sb_in(ph)
            QB = sb("QB", [P, 2, N], F32R)
            alibi = sb("alibi", [P, 2, N])
            junk = sb("junk", [P, N], mybir.dt.bfloat16)
            M = sb("M", [P, 2, TB])
            mrow = sb("mrow", [TB, 2, P], F32R)
            E = sb("E", [P, 4, N])
            sum_p, sum_d = (xpos[:, n].rearrange("p t s q d -> p (t s q d)").rearrange("p (s n) -> p s n", n=N)
                            for n in range(2))
            den_sb = XF[:, TB + 2:TB + 2 + DQ // P, :].rearrange("p t d -> p (t d)")
            den_inv = XF[:, TB:TB + DQ // P, :].rearrange("p t d -> p (t d)")
            inv_wide = XF[:, TB + 4:TB + 8, :].rearrange("p t d -> p (t d)")
            ones = sb("ones_m", [P, 32])
            zero_rows, one_rows = E[HD:P, 2, :], E[HD:P, 3, :]

            ld_qb = [sem(f"ld_qb{s}") for s in range(2)]
            ld_m = [sem(f"ld_m{s}") for s in range(2)]
            filled = sem("filled")
            qb_filled = sem("qb_filled")
            alibi_done = sem("alibi_done")
            max_mm = sem("max_mm")
            max_done = sem("max_done")
            m_turned = sem("m_turned")
            mrow_done = sem("mrow_done")
            qk_done = sem("qk_done")
            exp_done = sem("exp_done")
            pv_done = sem("pv_done")
            sum_p_done = sem("sum_p_done")
            sum_d_done = sem("sum_d_done")
            den_mm = sem("den_mm")
            den_taken = sem("den_taken")
            inv_out = sem("inv_out")
            inv_in = sem("inv_in")
            inv_done = sem("inv_done")
            o_done = sem("o_done")
            NP, ND = len(POOL_SUMS), len(DVE_SUMS) - 1

            def scores(s):
                return banks(2 * s, 2)

            def max_bank(i, k):
                return 4 if i >= 2 else (4, 0, 2)[(TB * i + k) % 3]

            def m_bank(i):
                return 5 if i > 0 else 7

            with nc.Block() as block:
                @block.sync
                def _(sp):
                    def load_qb(i, s):
                        sp.dma_start(QB[0:HD, s, :].bitcast(F32).rearrange("p (t c) -> p t c", c=P), qa_d[i // H, i % H, 0:HD])\
                            .then_inc(ld_qb[s], 16)

                    def load_m(i, s):
                        sp.wait_ge(qb_filled, 4)
                        need(sp, mrow_done, i + 1)
                        sp.dma_start(QB[HD:HD + 1, s, :].bitcast(F32).rearrange("p (t c) -> p t c", c=P),
                                     mrow[:, s, :].bitcast(F32)).then_inc(ld_m[s], 16)

                    def spread_inverse(i, s):
                        need(sp, inv_done, 2 * (i + 1))
                        sp.dma_start(inv_d[s].rearrange("(c n) -> c n", n=DQ), den_inv[0:P:32, :]).then_inc(inv_out, 16)
                        need(sp, inv_out, 16 * (i + 1))
                        need(sp, o_done, 2 * i)
                        for ch in range(2):
                            sp.dma_start(inv_wide[HD * ch:HD * ch + HD, :],
                                         inv_d[s, ch * 512:(ch + 1) * 512].partition_broadcast(HD)).then_inc(inv_in, 16)

                    load_qb(0, 0)
                    load_m(0, 0)

                    def head(i):
                        need(sp, qk_done, TB * i)
                        if i % GROUP == 0 and i // GROUP + 1 < HEADS // GROUP:
                            need(sp, pv_done, TB * i)
                            if i // GROUP + 1 == KV:
                                need_landed(sp, 1)
                            load_kv(sp, i // GROUP + 1, (i // GROUP + 1) % 2)
                        if i + 3 < HEADS:
                            if i + 3 == H:
                                need_landed(sp, 1)
                            load_qa(sp, i + 3, (i + 3) % 4)
                        if i + 1 < HEADS:
                            load_qb(i + 1, (i + 1) % 2)
                            load_m(i + 1, (i + 1) % 2)
                        if i > 0:
                            spread_inverse(i - 1, (i - 1) % 2)

                    for i in range(HEADS):
                        head(i)
                    spread_inverse(HEADS - 1, (HEADS - 1) % 2)

                @block.gpsimd
                def _(pool):
                    def head(i):
                        s = i % 2
                        need(pool, den_mm, i - 1)
                        for n, k in enumerate(POOL_SUMS[1:]):
                            need(pool, exp_done, TB * i + k + 1)
                            need(pool, sum_p_done, NP * i + n)
                            first = E[:, POOL_SUMS[0], :] if n == 0 else sum_p[:, s, :]
                            pool.tensor_tensor(sum_p[:, s, :], first, E[:, k % 4, :], ALU.add)\
                                .then_inc(sum_p_done, 1)
                        need(pool, sum_d_done, ND * (i + 1))
                        need(pool, sum_p_done, NP * (i + 1) - 1)
                        pool.tensor_tensor(sum_p[:, s, :], sum_p[:, s, :], sum_d[:, s, :], ALU.add)\
                            .then_inc(sum_p_done, 1)

                    fills = ((ones[:, :], 1.0), (zero_rows, 0.0), (one_rows, 1.0))
                    for n, (dst, value) in enumerate(fills):
                        need(pool, filled, n)
                        pool.memset(dst, value).then_inc(filled, 1)
                    need_landed(pool, 1)
                    for i in range(HEADS):
                        head(i)
                    for t in range(EARLY):
                        second_rstd(pool, t)

                @block.scalar
                def _(act):
                    act.wait_ge(ld_const, 48)

                    def alibi_row(i, s):
                        need(act, max_done, TB * (i - 1))
                        act.activation(alibi[:, s, :], far[:, :], ACT.Identity,
                                       scale=slope[:, i:i + 1])\
                            .then_inc(alibi_done, 1)

                    def take_denominators(i):
                        need(act, den_mm, i + 1)
                        need(act, inv_done, 2 * i)
                        act.activation(den_sb[:, :], banks(4)[:, 0:DQ], ACT.Copy).then_inc(den_taken, 1)

                    def take_m(i, s):
                        need(act, m_turned, i + 1)
                        need(act, ld_m[s], 16 * (i // 2))
                        act.activation(mrow[:, s, :], banks(m_bank(i))[0:TB, 0:P], ACT.Copy).then_inc(mrow_done, 1)

                    def head(i):
                        for k in range(TB):
                            if k == 3 and i > 0:
                                take_denominators(i - 1)
                            if k == 3 and i + 1 < HEADS:
                                take_m(i + 1, (i + 1) % 2)
                            need(act, qk_done, TB * i + k + 1)
                            need(act, pv_done, TB * i + k - 3)
                            j, old = (i, k - 4) if k >= 4 else (i - 1, k + 4)
                            if old in POOL_SUMS:
                                need(act, sum_p_done, NP * j + max(1, POOL_SUMS.index(old)))
                            else:
                                need(act, sum_d_done, ND * j + max(1, DVE_SUMS.index(old)))
                            kb = keybias[:, i, k:k + 1]
                            act.activation(E[:, k % 4, :], scores(k % 2), ACT.Exp, bias=kb).then_inc(exp_done, 1)
                            if k == 5 and i + 3 < HEADS:
                                alibi_row(i + 3, (i + 3) % 2)

                    alibi_row(0, 0)
                    alibi_row(1, 1)
                    act.wait_ge(filled, 3)
                    for s in range(2):
                        act.activation(QB[HD:P, s, :], zero_rows, ACT.Copy).then_inc(qb_filled, 1)
                        act.activation(KB[HD:P, s, :], one_rows, ACT.Copy).then_inc(qb_filled, 1)
                    alibi_row(2, 0)
                    take_m(0, 0)
                    act.wait_ge(qb_filled, 4)
                    for i in range(HEADS):
                        head(i)
                    take_denominators(HEADS - 1)

                @block.vector
                def _(dve):
                    def max_step(i, s, k):
                        need(dve, max_mm, TB * i + k + 1)
                        if k == 0:
                            need(dve, alibi_done, i + 1)
                            need(dve, m_turned, i - 1)
                        need(dve, max_done, TB * i + k)
                        dve.tensor_tensor_reduce(junk[:, :], banks(max_bank(i, k), 2), alibi[:, s, :], -1.0, BIG, ALU.add, ALU.min,
                                                 M[:, s, k:k + 1]).then_inc(max_done, 1)

                    def sum_step(i, s, n):
                        k = DVE_SUMS[n + 1]
                        need(dve, exp_done, TB * i + k + 1)
                        need(dve, sum_d_done, ND * i + n)
                        if n == 0:
                            need(dve, sum_p_done, NP * (i - 1))
                        first = E[:, DVE_SUMS[0] % 4, :] if n == 0 else sum_d[:, s, :]
                        dve.tensor_tensor(sum_d[:, s, :], first, E[:, k % 4, :], ALU.add).then_inc(sum_d_done, 1)

                    def invert(i, half):
                        need(dve, den_taken, i + 1)
                        need(dve, inv_out, 16 * i)
                        part = slice(half * DQ // 2, (half + 1) * DQ // 2)
                        dve.reciprocal(den_inv[:, part], den_sb[:, part]).then_inc(inv_done, 1)

                    def divide(i, ch):
                        need(dve, inv_in, 32 * (i + 1))
                        need(dve, pv_done, TB * (i + 1))
                        a, r = HD * ch, HD * (i % 2)
                        dst = OT[r:r + HD, i // H, (i % H) // 2, 4 * ch:4 * ch + 4, :].rearrange("p t c -> p (t c)")
                        dve.tensor_tensor(dst, banks(6 + i % 2)[a:a + HD, :], inv_wide[a:a + HD, :], ALU.mult)\
                            .then_inc(o_done, 1)

                    def head(i):
                        for k in range(TB):
                            if k == 0 and i > 0:
                                sum_step(i - 1, (i - 1) % 2, 1)
                            if i + 2 < HEADS:
                                max_step(i + 2, i % 2, k)
                            if k in (2, 3) and i > 0:
                                invert(i - 1, k - 2)
                            if k == 5:
                                sum_step(i, i % 2, 0)
                            if k == 6 and i > 0:
                                for ch in range(2):
                                    divide(i - 1, ch)

                    for i in range(2):
                        for k in range(TB):
                            max_step(i, i, k)
                    need_landed(dve, 1)
                    for i in range(HEADS):
                        head(i)
                    sum_step(HEADS - 1, (HEADS - 1) % 2, 1)
                    for half in range(2):
                        invert(HEADS - 1, half)
                    for t in range(EARLY):
                        residual(dve, t)
                    for ch in range(2):
                        divide(HEADS - 1, ch)

                @block.tensor
                def _(pe):
                    def max_step(i, k):
                        s, g = i % 4, (i // GROUP) % 2
                        if k == 0:
                            need(pe, ld_qa[s], 16 * (i // 4 + 1))
                            if i % GROUP == 0:
                                need(pe, ld_kv[g], 64 * (i // (2 * GROUP) + 1))
                            need(pe, mrow_done, 1 if i >= 2 else 0)
                        need(pe, max_done, TB * i + k - (2 if i < 2 else 0))
                        if k == 2:
                            need(pe, den_taken, i - 2)
                            need(pe, mrow_done, i if i >= 2 else 0)
                        for ch in range(2):
                            last = pe.matmul(banks(max_bank(i, k) + ch), QA[:, s, k * P:(k + 1) * P],
                                             KA[:, g, ch * 512:(ch + 1) * 512], start=True, stop=True)
                        last.then_inc(max_mm, 1)

                    def turn_m(i, s):
                        need(pe, max_done, TB * (i + 1))
                        pe.transpose(banks(m_bank(i))[0:TB, 0:P], M[:, s, :], ident[:, :]).then_inc(m_turned, 1)

                    def qk_step(i, k, chunks=(0, 1)):
                        g = (i // GROUP) % 2
                        if k == 0:
                            need(pe, ld_qb[i % 2], 16 * (i // 2 + 1))
                            need(pe, ld_m[i % 2], 16 * (i // 2 + 1))
                        need(pe, exp_done, TB * i + k - 1)
                        if i == 0 and k < 2:
                            pe.wait_ge(qb_filled, 4)
                            pe.wait_ge(max_done, 2 * TB - 2 + k)
                        for ch in chunks:
                            pe.matmul(scores(k % 2)[:, ch * 512:(ch + 1) * 512], KA[:, g, k * P:(k + 1) * P],
                                      QA[:, i % 4, ch * 512:(ch + 1) * 512], start=True, stop=False)
                        for ch in chunks:
                            last = pe.matmul(scores(k % 2)[:, ch * 512:(ch + 1) * 512], KB[:, g, k * P:(k + 1) * P],
                                             QB[:, i % 2, ch * 512:(ch + 1) * 512], start=False, stop=True)
                        if 1 in chunks:
                            last.then_inc(qk_done, 1)

                    def pv_step(i, k):
                        g = (i // GROUP) % 2
                        need(pe, exp_done, TB * i + k + 1)
                        if k == 0:
                            need(pe, o_done, 2 * (i - 1))
                        for ch in range(2):
                            last = pe.matmul(banks(6 + i % 2)[HD * ch:HD * ch + HD, :], V[:, g, k, :],
                                             E[:, k % 4, ch * 512:(ch + 1) * 512], start=(k == 0), stop=(k == TB - 1))
                        last.then_inc(pv_done, 1)

                    def denominators(i, s):
                        pe.wait_ge(filled, 3)
                        need(pe, sum_p_done, NP * (i + 1))
                        for c in range(4):
                            last = pe.matmul(banks(4)[32 * c:32 * c + 32, 0:DQ], ones[:, :],
                                             sum_p[:, s, c * DQ:(c + 1) * DQ], start=True, stop=True)
                        last.then_inc(den_mm, 1)

                    def small_products(i):
                        if i + 2 >= HEADS:
                            need(pe, mrow_done, i + 1)
                            need(pe, den_taken, i - 1)
                        need(pe, max_done, min(TB * (i + 2) + 2, TB * HEADS))
                        if i > 0:
                            denominators(i - 1, (i - 1) % 2)
                        if i + 1 < HEADS:
                            turn_m(i + 1, (i + 1) % 2)

                    def head(i):
                        for k in range(0, TB, 2):
                            qk_step(i, k)
                            if k == 2:
                                qk_step(i, k + 1, (0,))
                                small_products(i)
                                qk_step(i, k + 1, (1,))
                            else:
                                qk_step(i, k + 1)
                            if i + 2 < HEADS:
                                max_step(i + 2, k)
                            if k > 0:
                                pv_step(i, k - 1)
                            elif i > 0:
                                pv_step(i - 1, TB - 1)
                            pv_step(i, k)
                            if i + 2 < HEADS:
                                max_step(i + 2, k + 1)

                    for i in range(2):
                        for k in range(TB):
                            max_step(i, k)
                            if (i, k) == (1, 2):
                                turn_m(0, 0)
                    for i in range(HEADS):
                        head(i)
                    pv_step(HEADS - 1, TB - 1)

                    pe.wait_ge(loaded_late, 16 * len(late_loads))
                    pe.wait_ge(exp_done, TB * HEADS)
                    pe.wait_ge(o_done, 2 * H)
                    for t in range(2):
                        project_out(pe, t)
                    pe.wait_ge(den_taken, HEADS - 1)
                    denominators(HEADS - 1, (HEADS - 1) % 2)
                    for t in range(2, TB):
                        project_out(pe, t)

        early_sems.remove(loaded_late)
        nc.clear_and_free_semaphores(early_sems)

        with nc.Block() as block:
            @block.sync
            def _(sp):
                sp.dma_start(mask[:, :, :], mask_d[:, 0:2, :]).then_inc(ld_mask, 16)
                for l in range(DEPTH):
                    sp.dma_start(scale_row[:, l, 0, :], f_qs[l].partition_broadcast(P)).then_inc(ld_tab, 16)
                    sp.dma_start(scale_row[:, l, 1, :], f_ks[l].partition_broadcast(P)).then_inc(ld_tab, 16)
                    sp.dma_start(xpos[:, l].rearrange("p t s q d -> p t (s q d)"),
                                 xpos_d.rearrange("(t p) s x -> p t (s x)", p=P)).then_inc(ld_tab, 16)
                    if l == 0:
                        sp.wait_ge(ld_tab, LD_TAB)
                sp.wait_ge(ld_mask, 16)

            @block.gpsimd
            def _(pool):
                for t in range(EARLY, T):
                    second_rstd(pool, t)
                    if t >= T - TB:
                        scale_tables(pool, 0, t - TB, t - TB + 1)

            @block.tensor
            def _(pe):
                for t in range(TB, T):
                    project_out(pe, t)

            @block.vector
            def _(dve):
                for t in range(EARLY, T):
                    residual(dve, t)
        mid.close()
        ahead.close()

        XA = fsb("XA", [P, T, D])
        XS = fsb("XS", [P, T, D // 2])
        buffers = {}

        def sb(name, shape, dt=F32):
            if name not in buffers:
                buffers[name] = fsb(name, shape, dt)
            return buffers[name]

        def new_sem(name):
            return whole.enter_context(nc.semaphore(name))

        xn = fsb("xn_o", [P, 2, D])

        def modulation(dve):
            return [(lambda t, s: shifted_out(dve, t), 1), (lambda t, s: modulate_out(dve, t), 0)]

        parts = [({"vector": modulation}, 0)]
        before = {"xf_done": xf_done}
        for l in range(DEPTH):
            att_sems, attention = local_attention(l, psum, sb, new_sem, dict(before), XF, XA, XS, ident, minus_half,
                                                  fw_qkv, fw_o, xpos[:, l], mask)
            before.update(att_sems)
            mlp_sems, mlp = gated_mlp(l, psum, sb, new_sem, dict(before), X, XF, XA, XS, ident, minus_half, fw_1,
                                      fw_2, fb_1, f_ln, rows, out, scale_tables)
            before = {**att_sems, **{name: mlp_sems[name] for name in ("gelu_done", "u_done", "xf_done")}}
            parts += [(attention, LAYER_STEPS * l + AHEAD), (mlp, LAYER_STEPS * l + MLP_STEP + AHEAD)]

        def stages(engine, handle):
            return [(fn, lag + first) for part, first in parts if engine in part for fn, lag in part[engine](handle)]

        with nc.Block() as block:
            @block.sync
            def _(sp):
                over_tiles(stages("sync", sp))
                for s in range(2):
                    sp.wait_ge(mlp_sems[f"res_out{s}"], 16 * (T // 2))

            @block.gpsimd
            def _(pool):
                over_tiles(stages("gpsimd", pool))

            @block.scalar
            def _(act):
                over_tiles(stages("scalar", act))

            @block.vector
            def _(dve):
                over_tiles(stages("vector", dve))

            @block.tensor
            def _(pe):
                over_tiles(stages("tensor", pe))


def local_attention(l, psum, sb, new_sem, before, XF, XA, XS, ident, minus_half, fw_qkv, fw_o, xpos, mask):
    def banks(a, n=1):
        return psum[:, a:a + n, :].rearrange("p b c -> p (b c)")

    sems = {}

    def sem(name):
        sems[name] = new_sem(f"{name}_a{l}")
        return sems[name]

    NH = 2 * FH
    HR = 8
    hT = sb("hT_att", [P, HR, P + 1])
    raw = sb("raw_att", [P, 2, NH, HD])
    sq = sb("sq_att", [P, NH, HD])
    ss = sb("ss_att", [P, 2, NH])
    ss_up = sb("ss_up_att", [P, 2, NH])
    rinv = sb("rinv_att", [P, 2, NH])
    t1 = sb("t1_att", [P, NH, HD])
    t2 = sb("t2_att", [P, 2, NH, HD])
    qk = sb("qk_att", [P, 2, NH, HD])
    v = sb("v_att", [P, 2, INNER])
    vp = sb("vp_att", [P, 2, INNER])
    qT = sb("qT_att", [P, 2, FH // 2, P])
    kT = sb("kT_att", [P, 2, FH // 2, WIN + P])
    S = sb("S_att", [P, 2, FH, 2 * WIN])
    nmax = sb("nmax_att", [P, 2, FH])
    E = sb("E_att", [P, 2, FH, 2 * WIN])
    den = sb("den_att", [P, 2, FH])
    den_inv = sb("den_inv_att", [P, 2, FH])
    EN = sb("EN_att", [P, 2, FH, 2 * WIN])
    ET = sb("ET_att", [P, 2, FH, P])
    oT = sb("oT_att", [P, 2, FH // 2, P])

    cleared = sem("cleared")
    x_turned = sem("x_turned")
    hT_done = sem("hT_done")
    qk_proj = sem("qk_proj")
    raw_done = sem("raw_done")
    sq_done = sem("sq_done")
    ss_done = sem("ss_done")
    up_done = sem("up_done")
    rinv_done = sem("rinv_done")
    sin_done = sem("sin_done")
    cos_done = sem("cos_done")
    sum_done = sem("sum_done")
    qk_done = sem("qk_done")
    qk_turned = sem("qk_turned")
    qkT_done = sem("qkT_done")
    scores_done = sem("scores_done")
    max_done = sem("max_done")
    exp_done = sem("exp_done")
    inv_done = sem("inv_done")
    norm_done = sem("norm_done")
    e_turned = sem("e_turned")
    eT_done = sem("eT_done")
    v_proj = sem("v_proj")
    v_done = sem("v_done")
    vp_in = [sem("vp_in0"), sem("vp_in1")]
    pv_done = sem("pv_done")
    oT_done = sem("oT_done")
    out_proj = sem("out_proj")
    xa_done = sem("xa_done")
    xs_in = [sem(f"xs_in{b}") for b in range(B)]

    ps_qk = banks(0, 2).rearrange("p (h d) -> p h d", d=HD)
    ps_x = banks(7)[:, 0:P]

    PROJECT, NORMS, FINISH, SCORES, SOFTMAX, TURN_E, PV, OUT = 1, 2, 3, 4, 5, 6, 7, 8

    def sync(sp):
        if l == 0:
            sp.wait_ge(cleared, 1)

        def shift_v(t, s):
            need(sp, v_done, t + 1)
            need(sp, pv_done, t - 1)
            sp.dma_start(vp[0:WIN, s, :], v[WIN:P, 1 - s, :]).then_inc(vp_in[s], 16)
            sp.dma_start(vp[WIN:P, s, :], v[0:WIN, s, :]).then_inc(vp_in[s], 16)

        def shift_x(t, s):
            need(sp, xa_done, t + 1)
            sp.dma_start(XS[1:P, t, :], XA[0:P - 1, t, D // 2:D]).then_inc(xs_in[t // TB], 16)
            if t % TB > 0:
                sp.dma_start(XS[0:1, t, :], XA[P - 1:P, t - 1, D // 2:D]).then_inc(xs_in[t // TB], 16)

        return [(shift_v, TURN_E), (shift_x, OUT)]

    def gpsimd(pool):
        def square(t, s):
            need(pool, raw_done, t + 1)
            need(pool, ss_done, t)
            pool.tensor_tensor(sq[:, :, :], raw[:, s], raw[:, s], ALU.mult).then_inc(sq_done, 1)

        def sin_part(t, s):
            need(pool, sum_done, 2 * (t - 1))
            sin = xpos[:, t % TB, 1, :, :][:, :, None, :].to_broadcast([P, 2, FH, HD])
            pool.tensor_tensor(t2[:, s].rearrange("p (q h) d -> p q h d", q=2),
                               raw[:, s].rearrange("p (q h) d -> p q h d", q=2), sin, ALU.mult)\
                .then_inc(sin_done, 1)

        def inverse_norms(t, s):
            need(pool, ss_done, t + 1)
            pool.tensor_scalar(ss_up[:, s, :], ss[:, s, :], 1e-24, None, ALU.max).then_inc(up_done, 1)
            need(pool, up_done, t + 1)
            need(pool, qk_done, t - 1)
            pool.tensor_tensor(rinv[:, s, :], ss_up[:, s, :], minus_half[:, 0:NH], ALU.pow)\
                .then_inc(rinv_done, 1)

        return [(square, NORMS), (sin_part, NORMS), (inverse_norms, NORMS)]

    def scalar(act):
        if l == 0:
            act.wait_ge(cleared, 1)

        def take_oT(t, s):
            need(act, pv_done, t + 1)
            need(act, out_proj, t - 1)
            act.activation(oT[:, s], banks(7).rearrange("p (j c) -> p j c", c=P), ACT.Copy)\
                .then_inc(oT_done, 1)

        def take_v(t, s):
            need(act, v_proj, t + 1)
            need(act, pv_done, t - 1)
            if t > 0:
                act.wait_ge(vp_in[1 - s], 32 * ((t - 1) // 2 + 1))
            act.activation(v[:, s, :], banks(2), ACT.Copy).then_inc(v_done, 1)

        def take_qkT(t, s):
            need(act, qk_turned, 2 * t + 1)
            need(act, scores_done, t - 1)
            act.activation(qT[:, s, :, :], banks(3).rearrange("p (j c) -> p j c", c=P), ACT.Copy)\
                .then_inc(qkT_done, 1)
            need(act, qkT_done, 3 * t)
            if l > 0 and t == 0:
                act.wait_ge(before["qkT_done"], 3 * T)
            act.activation(kT[:, s, :, 0:WIN], kT[:, 1 - s, :, P:P + WIN], ACT.Copy).then_inc(qkT_done, 1)
            need(act, qk_turned, 2 * t + 2)
            act.activation(kT[:, s, :, WIN:WIN + P], banks(4).rearrange("p (j c) -> p j c", c=P), ACT.Copy)\
                .then_inc(qkT_done, 1)

        def take_hT(t, s):
            need(act, v_proj, t - HR + 1)
            need(act, x_turned, t + 1)
            need(act, hT_done, 3 * t)
            if l > 0 and t == 0:
                act.wait_ge(before["hT_done"], 3 * T)
            act.activation(hT[HD:P, t % HR, 0:1], hT[HD:P, (t - 1) % HR, P:P + 1], ACT.Copy,
                           scale=0.0 if t % TB == 0 else 1.0).then_inc(hT_done, 1)
            act.activation(hT[0:HD, t % HR, 0:P], ps_x[0:HD, :], ACT.Copy).then_inc(hT_done, 1)
            act.activation(hT[HD:P, t % HR, 1:P + 1], ps_x[HD:P, :], ACT.Copy).then_inc(hT_done, 1)

        def exponentials(t, s):
            need(act, norm_done, t - 1)
            for h in range(FH):
                need(act, max_done, FH * t + h + 1)
                act.activation(E[:, s, h, :], S[:, s, h, :], ACT.Exp, bias=nmax[:, s, h:h + 1],
                               scale=-1.0, accum_out=den[:, s, h:h + 1]).then_inc(exp_done, 1)

        def take_raw(t, s):
            need(act, qk_proj, t + 1)
            need(act, cos_done, t - 1)
            need(act, sin_done, t - 1)
            act.activation(raw[:, s], ps_qk, ACT.Copy).then_inc(raw_done, 1)

        def take_eT(t, s):
            need(act, pv_done, t - 1)
            for n in range(2):
                need(act, e_turned, 2 * t + n + 1)
                act.activation(ET[:, s, 4 * n:4 * n + 4, :], banks(3 + n).rearrange("p (h c) -> p h c", c=P),
                               ACT.Copy).then_inc(eT_done, 1)

        return ([(take_oT, OUT), (take_v, TURN_E), (take_qkT, SCORES), (take_hT, 0),
                    (exponentials, SOFTMAX), (take_raw, PROJECT), (take_eT, TURN_E)])

    def vector(dve):
        if l == 0:
            dve.memset(kT[:, 1, :, P:P + WIN], 0.0)
            dve.memset(v[WIN:P, 1, :], 0.0)
            for b in range(B):
                dve.memset(XS[0:1, b * TB, :], 0.0)
            dve.memset(hT[HD:P, HR - 1, P:P + 1], 0.0).then_inc(cleared, 1)

        def masked_max(t, s):
            need(dve, scores_done, t + 1)
            need(dve, exp_done, FH * (t - 1))
            for h in range(FH):
                dve.tensor_tensor_reduce(S[:, s, h, :], banks(5 + h % 2)[:, (h // 2) * P:(h // 2 + 1) * P],
                                         mask[:, min(t % TB, 1), :], -1.0, BIG, ALU.add, ALU.min,
                                         nmax[:, s, h:h + 1]).then_inc(max_done, 1)

        def residual(t, s):
            need(dve, out_proj, t + 1)
            dve.wait_ge(before["xf_done"], t + 1)
            dve.tensor_tensor(XA[:, t, :], banks(2)[:, 0:D], XF[:, t, :], ALU.add).then_inc(xa_done, 1)

        def finish(t, s):
            need(dve, cos_done, t + 1)
            need(dve, sin_done, t + 1)
            need(dve, qk_turned, 2 * (t - 1))
            m = HD // 2
            dve.tensor_tensor(qk[:, s, :, 0:m], t1[:, :, 0:m], t2[:, s, :, m:HD], ALU.add).then_inc(sum_done, 1)
            dve.tensor_tensor(qk[:, s, :, m:HD], t1[:, :, m:HD], t2[:, s, :, 0:m], ALU.add).then_inc(sum_done, 1)
            need(dve, sum_done, 2 * (t + 1))
            need(dve, rinv_done, t + 1)
            dve.tensor_tensor(qk[:, s], qk[:, s], rinv[:, s, :][:, :, None].to_broadcast([P, NH, HD]),
                              ALU.mult).then_inc(qk_done, 1)

        def square_sums(t, s):
            need(dve, sq_done, t + 1)
            need(dve, up_done, t - 1)
            dve.tensor_reduce(ss[:, s, :], sq[:, :, :], AX_X, ALU.add).then_inc(ss_done, 1)

        def cos_part(t, s):
            need(dve, raw_done, t + 1)
            need(dve, sum_done, 2 * t)
            cos = xpos[:, t % TB, 0, :, :][:, :, None, :].to_broadcast([P, 2, FH, HD])
            dve.tensor_tensor(t1[:, :, :].rearrange("p (q h) d -> p q h d", q=2),
                              raw[:, s].rearrange("p (q h) d -> p q h d", q=2), cos, ALU.mult)\
                .then_inc(cos_done, 1)

        def normalise(t, s):
            need(dve, exp_done, FH * (t + 1))
            need(dve, norm_done, t - 1)
            dve.reciprocal(den_inv[:, s, :], den[:, s, :]).then_inc(inv_done, 1)
            need(dve, inv_done, t + 1)
            need(dve, e_turned, 2 * (t - 1))
            dve.tensor_tensor(EN[:, s, :, :], E[:, s, :, :],
                              den_inv[:, s, :][:, :, None].to_broadcast([P, FH, 2 * WIN]), ALU.mult)\
                .then_inc(norm_done, 1)

        return ([(masked_max, SOFTMAX), (residual, OUT), (finish, FINISH), (square_sums, NORMS),
                    (cos_part, NORMS), (normalise, SOFTMAX)])

    def tensor(pe):
        def turn_qk(t, s):
            need(pe, qk_done, t + 1)
            if l > 0 and t == 0:
                pe.wait_ge(before["gelu_done"], HC * T)
                pe.wait_ge(before["u_done"], HC * T)
            need(pe, qkT_done, 3 * t)
            for n in range(2):
                need(pe, eT_done, 2 * (t + SCORES - 1 - TURN_E) + n + 1)
                for j in range(4):
                    src = qk[:, s, 8 * n + 2 * j:8 * n + 2 * j + 2, :].rearrange("p h d -> p (h d)")
                    last = pe.transpose(banks(3 + n)[:, j * P:(j + 1) * P], src, ident[:, :])
                last.then_inc(qk_turned, 1)

        def project_out(t, s):
            need(pe, oT_done, t + 1)
            need(pe, v_done, min(t + OUT - TURN_E + 1, T))
            need(pe, xa_done, t)
            for j in range(FH // 2):
                last = pe.matmul(banks(2)[:, 0:D], oT[:, s, j, :], fw_o[:, l, j, :], start=(j == 0),
                                 stop=(j == FH // 2 - 1))
            last.then_inc(out_proj, 1)

        def turn_x(t, s):
            pe.wait_ge(before["xf_done"], t + 1)
            need(pe, hT_done, 3 * t)
            need(pe, oT_done, t - OUT + 1)
            pe.transpose(ps_x, XF[:, t, :], ident[:, :]).then_inc(x_turned, 1)

        def project_qk(t, s):
            need(pe, hT_done, 3 * (t + 1))
            need(pe, raw_done, t)
            for n in range(2):
                last = pe.matmul(banks(n), hT[:, t % HR, 0:P], fw_qkv[:, l, n * INNER:(n + 1) * INNER],
                                 start=True, stop=True)
            last.then_inc(qk_proj, 1)

        def multiply_qk(t, s):
            need(pe, qkT_done, 3 * (t + 1))
            need(pe, max_done, FH * t)
            for h in range(FH):
                a = HD * (h % 2)
                for w in range(2):
                    last = pe.matmul(banks(5 + h % 2)[WIN * w:WIN * w + WIN, (h // 2) * P:(h // 2 + 1) * P],
                                     qT[a:a + HD, s, h // 2, WIN * w:WIN * w + WIN],
                                     kT[a:a + HD, s, h // 2, WIN * w:WIN * w + 2 * WIN],
                                     start=True, stop=True)
            last.then_inc(scores_done, 1)

        def turn_e(t, s):
            need(pe, norm_done, t + 1)
            need(pe, qkT_done, 3 * min(t + TURN_E - SCORES + 1, T))
            need(pe, eT_done, 2 * t)
            for n in range(2):
                for j in range(4):
                    last = pe.transpose(banks(3 + n)[:, j * P:(j + 1) * P], EN[:, s, 4 * n + j, :], ident[:, :])
                last.then_inc(e_turned, 1)

        def multiply_v(t, s):
            need(pe, vp_in[s], 32 * (t // 2 + 1))
            need(pe, hT_done, 3 * min(t + PV + 1, T))
            need(pe, oT_done, t)
            for h in range(FH):
                need(pe, eT_done, 2 * t + h // 4 + 1)
                a = HD * (h % 2)
                for w in range(2):
                    last = pe.matmul(banks(7)[a:a + HD, (h // 2) * P + WIN * w:(h // 2) * P + WIN * w + WIN],
                                     (v if w else vp)[:, s, h * HD:(h + 1) * HD],
                                     ET[:, s, h, WIN * w:WIN * w + WIN], start=True, stop=True)
            last.then_inc(pv_done, 1)

        def project_v(t, s):
            need(pe, v_done, t)
            need(pe, xa_done, t - (OUT - SOFTMAX) + 1)
            if l > 0 and t == 0:
                pe.wait_ge(before["xf_done"], T)
            pe.matmul(banks(2), hT[:, t % HR, 0:P], fw_qkv[:, l, 2 * INNER:3 * INNER], start=True, stop=True)\
                .then_inc(v_proj, 1)

        return ([(turn_qk, SCORES), (project_out, OUT), (turn_x, 0), (project_qk, PROJECT),
                    (multiply_qk, SCORES), (turn_e, TURN_E), (multiply_v, PV), (project_v, SOFTMAX)])

    return sems, {"sync": sync, "gpsimd": gpsimd, "scalar": scalar, "vector": vector, "tensor": tensor}


def gated_mlp(l, psum, sb, new_sem, before, X, XF, XA, XS, ident, minus_half, fw_1, fw_2, fb_1, f_ln, rows, out,
              scale_tables):
    def banks(a, n=1):
        return psum[:, a:a + n, :].rearrange("p b c -> p (b c)")

    sems = {}

    def sem(name):
        sems[name] = new_sem(f"{name}_m{l}")
        return sems[name]

    bn = sb("bn_mlp", [P, 2, 2, 6])
    mv = sb("mv_mlp", [P, 2, 2])
    rstd = sb("rstd_mlp", [P, 2, 1])
    var_eps = sb("var_eps_mlp", [P, 2, 1])
    xn = sb("xn_mlp", [P, 2, D])
    hT = sb("hT_mlp", [P, 2, P])
    gate = sb("gate_mlp", [P, 2, HC, P])
    act_in = sb("act_in_mlp", [P, 2, HC, P])
    y = sb("y_mlp", [P, 2, D])
    res = sb("res_mlp", [P, 2, D])

    ones_set = sem("ones_set")
    def ps_x(s):
        return banks(3 + 2 * s)[:, HC * P:(HC + 1) * P]

    ln_step = sem("ln_step")
    rstd_done = sem("rstd_done")
    eps_done = sem("eps_done")
    xn_done = sem("xn_done")
    x_turned = sem("x_turned")
    hT_done = sem("hT_done")
    w1_mm = sem("w1_mm")
    gelu_done = sem("gelu_done")
    u_done = sem("u_done")
    w2_mm = sem("w2_mm")
    xf_done = sem("xf_done")
    y_done = sem("y_done")
    res_done = sem("res_done")
    res_out = [sem("res_out0"), sem("res_out1")]
    last_layer = l == DEPTH - 1
    width = [P] * (HC - 1) + [HLAST]

    def sync(sp):
        def store(t, s):
            need(sp, res_done, t + 1)
            sp.dma_start(out[t // TB, bass.ts(t % TB, P), :], res[:, s, :]).then_inc(res_out[s], 16)

        return [(store, 6)] if last_layer else []

    def gpsimd(pool):
        def ln_rstd(t, s):
            need(pool, ln_step, 3 * t + 3)
            need(pool, xn_done, 2 * (t - 1))
            pool.tensor_scalar(var_eps[:, s, :], mv[:, s, 1:2], EPS, None, ALU.add).then_inc(eps_done, 1)
            need(pool, eps_done, t + 1)
            pool.tensor_tensor(rstd[:, s, :], var_eps[:, s, :], minus_half[:, 0:1], ALU.pow).then_inc(rstd_done, 1)

        def tables(t, s):
            if not last_layer and t < TB:
                scale_tables(pool, l + 1, t, t + 1)

        def result(t, s):
            need(pool, xf_done, t + 1)
            pool.tensor_tensor(y[:, s, :], XF[:, t, :], rows[:, t // TB, 3, :], ALU.mult).then_inc(y_done, 1)
            need(pool, y_done, t + 1)
            need(pool, res_out[s], 16 * (t // 2))
            pool.tensor_tensor(res[:, s, :], y[:, s, :], X[:, t, :], ALU.add).then_inc(res_done, 1)

        return [(ln_rstd, 0), (result, 6) if last_layer else (tables, 0)]

    def scalar(act):
        def take_hT(t, s):
            need(act, x_turned, t + 1)
            need(act, w1_mm, 2 * (t - 1))
            act.activation(hT[:, s, :], ps_x(s), ACT.Identity, bias=f_ln[:, l, 1:2],
                           scale=f_ln[:, l, 0:1]).then_inc(hT_done, 1)

        def gelu(t, s):
            need(act, w1_mm, 2 * t + 1)
            need(act, u_done, HC * (t - 1))
            for j, n in enumerate(width):
                act.activation(gate[0:n, s, j, :], banks(3 + 2 * s)[0:n, j * P:(j + 1) * P], ACT.Gelu,
                               bias=fb_1[0:n, l, 1, j:j + 1]).then_inc(gelu_done, 1)

        return [(gelu, 3), (take_hT, 2)]

    def vector(dve):
        if l == 0:
            for s in range(2):
                dve.memset(act_in[:, s, HC - 1, :], 1.0).then_inc(ones_set, 1)

        def ln_stats(t, s):
            need(dve, xn_done, 2 * (t - 1))
            dve.wait_ge(before["xa_done"], t + 1)
            dve.wait_ge(before[f"xs_in{t // TB}"], 16 * (2 * TB - 1))
            dve.bn_stats(bn[:, s, 0, :], XA[:, t, 0:D // 2]).then_inc(ln_step, 1)
            dve.bn_stats(bn[:, s, 1, :], XS[:, t, :]).then_inc(ln_step, 1)
            dve.wait_ge(ln_step, 3 * t + 2)
            dve.bn_aggr(mv[:, s, :], bn[:, s, :, :].rearrange("p a b -> p (a b)")).then_inc(ln_step, 1)

        def ln_apply(t, s):
            need(dve, rstd_done, t + 1)
            need(dve, x_turned, t - 1)
            for n, src in enumerate((XA[:, t, 0:D // 2], XS[:, t, :])):
                dve.tensor_scalar(xn[:, s, n * (D // 2):(n + 1) * (D // 2)], src, mv[:, s, 0:1], rstd[:, s, :],
                                  ALU.subtract, ALU.mult).then_inc(xn_done, 1)

        def gated(t, s):
            need(dve, w1_mm, 2 * t + 2)
            if l == 0 and t == 0:
                dve.wait_ge(ones_set, 2)
            need(dve, w2_mm, t - 1)
            for j, n in enumerate(width):
                need(dve, gelu_done, HC * t + j + 1)
                dve.scalar_tensor_tensor(act_in[0:n, s, j, :], banks(4 + 2 * s)[0:n, j * P:(j + 1) * P],
                                         fb_1[0:n, l, 0, j:j + 1], gate[0:n, s, j, :], ALU.add, ALU.mult)\
                    .then_inc(u_done, 1)

        def residual(t, s):
            need(dve, w2_mm, t + 1)
            dve.tensor_tensor(XF[:, t, :], banks(2)[:, 0:D], XA[:, t, :], ALU.add).then_inc(xf_done, 1)

        return [(gated, 4), (ln_apply, 2), (ln_stats, 0), (residual, 5)]

    def tensor(pe):
        def turn_x(t, s):
            need(pe, xn_done, 2 * (t + 1))
            need(pe, hT_done, t - 1)
            need(pe, gelu_done, HC * (t - 1))
            if t < 2:
                pe.wait_ge(before["eT_done"], 2 * T)
                pe.wait_ge(before["max_done"], FH * T)
            pe.transpose(ps_x(s), xn[:, s, :], ident[:, :]).then_inc(x_turned, 1)

        def hidden(t, s):
            need(pe, hT_done, t + 1)
            for m in range(2):
                need(pe, u_done if m else gelu_done, HC * (t - 1))
                off = 0 if m else HID
                for j, n in enumerate(width):
                    last = pe.matmul(banks(3 + 2 * s + m)[0:n, j * P:(j + 1) * P],
                                     fw_1[:, l, off + j * P:off + j * P + n], hT[:, s, :],
                                     start=True, stop=True)
                last.then_inc(w1_mm, 1)

        def project(t, s):
            need(pe, u_done, HC * (t + 1))
            need(pe, xf_done, t)
            if t == 0:
                pe.wait_ge(before["xa_done"], T)
            for j, n in enumerate(width):
                rows_in = n + (j == HC - 1)
                last = pe.matmul(banks(2)[:, 0:D], act_in[0:rows_in, s, j, :], fw_2[0:rows_in, l, j, :],
                                 start=(j == 0), stop=(j == HC - 1))
            last.then_inc(w2_mm, 1)

        return [(project, 5), (hidden, 3), (turn_x, 2)]

    return sems, {"sync": sync, "gpsimd": gpsimd, "scalar": scalar, "vector": vector, "tensor": tensor}


_INS = ['L0_attn_x', 'L0_attn_Wq', 'L0_attn_Wk', 'L0_attn_Wv', 'L0_attn_Wo', 'L0_ffn_wqkv', 'L0_ffn_q_scale',
        'L0_ffn_k_scale', 'L0_ffn_wo', 'L0_ffn_ln_g', 'L0_ffn_ln_b', 'L0_ffn_w1', 'L0_ffn_b1', 'L0_ffn_w2',
        'L0_ffn_b2', 'L0_c', 'L0_wmod']
_OUTS = [((B, N, D), 'float32')]


def kernel(**inputs):
    import concourse.bacc as bacc
    from concourse.bass_utils import run_bass_kernel_spmd

    nc = bacc.Bacc("TRN2", target_bir_lowering=False, num_devices=1)
    arrays, args = {}, []
    given = {name: np.ascontiguousarray(inputs[name]) for name in _INS} | shape_constants()
    for name, a in given.items():
        arrays[f"in_{name}_dram"] = a
        args.append(nc.dram_tensor(f"in_{name}_dram", a.shape, mybir.dt.from_np(a.dtype), kind="ExternalInput").ap())
    for i, (shape, dtype) in enumerate(_OUTS):
        args.append(nc.dram_tensor(f"out_{i}_dram", shape, mybir.dt.from_np(np.dtype(dtype)),
                                   kind="ExternalOutput").ap())
    adaln_block(nc, *args)
    r = run_bass_kernel_spmd(nc, [arrays], core_ids=[0])
    return r.results[0]["out_0_dram"]
```
